# Optimizing a Trainium2 kernel written in Bass

```python
import numpy as np
import jax
import jax.numpy as jnp

def _softmax(x, axis=-1):
    return jax.nn.softmax(x, axis=axis)

def _gelu(x):
    return jax.nn.gelu(x, approximate=True)

def _silu(x):
    return jax.nn.silu(x)

def _sigmoid(x):
    return jax.nn.sigmoid(x)

def _layernorm(x, axis=-1, eps=1e-05):
    m = jnp.mean(x, axis=axis, keepdims=True)
    v = jnp.var(x, axis=axis, keepdims=True)
    return (x - m) / jnp.sqrt(v + eps)

def _scatter_add(tgt, idx, src, axis=0):
    return tgt.at[idx].add(src)

def _segment_sum(src, seg, n):
    return jax.ops.segment_sum(src, seg, n)
kernel_name = 'mk_decoder_postln_d2_seqx_r4_d4afff'

def setup_inputs(seed: int=0):
    np.random.seed(seed)
    _w = jnp.asarray

    def _rec_inputs():
        import jax
        import jax.numpy as jnp
        _rk = jax.random.key(seed)
        x = 7.22e-05 + 1 * jax.random.normal(jax.random.fold_in(_rk, 1), (2, 1024, 256), jnp.float32)
        _lenS = 1024 - jax.random.randint(jax.random.fold_in(_rk, 7), (2,), 0, max(1, 1024 // 4) + 1, jnp.int32)
        _lenS2 = 154 - jax.random.randint(jax.random.fold_in(_rk, 8), (2,), 0, max(1, 154 // 4) + 1, jnp.int32)
        _ctx_768P = jax.random.normal(jax.random.fold_in(_rk, 11), (2, 16, 192), jnp.float32)
        _ctx_768c = jax.random.dirichlet(jax.random.fold_in(_rk, 511), 0.3 * jnp.ones((16,), jnp.float32), (2, 154))
        _ctx_768t = jnp.einsum('bsk,bkd->bsd', _ctx_768c, _ctx_768P)
        _ctx_768t = _ctx_768t * jax.lax.rsqrt(jnp.mean(jnp.square(_ctx_768t)) + 1e-12) * 0.953939
        ctx_768 = -0.000191848 + 0.999787 * (_ctx_768t + 0.3 * jax.random.normal(jax.random.fold_in(_rk, 611), (2, 154, 192), jnp.float32))
        return (x, ctx_768)
    x, ctx_768 = _rec_inputs()

    def _L0_attn_setup():
        import jax, jax.numpy as jnp
        import numpy as np
        NUM_HEADS = 16
        D_MODEL = 256
        HEAD_DIM = D_MODEL // NUM_HEADS
        NEG_INF = -1000000000.0

        def alibi_bidirectional_bias(num_heads, seq_len, dtype=jnp.float32):
            half = num_heads // 2
            base = 24.0 ** (1.0 / half)
            slopes = (1.0 / base ** jnp.arange(1, half + 1, dtype=dtype))[:, None, None]
            pos = jnp.arange(seq_len)
            rel = (pos[None, :] - pos[:, None]).astype(dtype)
            neg = jnp.full((seq_len, seq_len), NEG_INF, dtype=dtype)
            fwd = slopes * jnp.tril(rel) + jnp.triu(neg, 1)
            bwd = slopes * jnp.triu(-rel) + jnp.tril(neg, -1)
            return jnp.concatenate([fwd, bwd], axis=0)
        key = jax.random.key(seed)
        ks = jax.random.split(key, 9)
        B, S, D = (2, 512, D_MODEL)
        sc = 1.0 / np.sqrt(D)
        inp = {'x': jax.random.normal(ks[0], (B, S, D), dtype=jnp.float32)}
        inp['Wq'] = jax.random.normal(ks[1], (D, D), dtype=jnp.float32) * sc
        inp['bq'] = jnp.zeros((D,), dtype=jnp.float32)
        inp['Wk'] = jax.random.normal(ks[2], (D, D), dtype=jnp.float32) * sc
        inp['bk'] = jnp.zeros((D,), dtype=jnp.float32)
        inp['Wv'] = jax.random.normal(ks[3], (D, D), dtype=jnp.float32) * sc
        inp['bv'] = jnp.zeros((D,), dtype=jnp.float32)
        inp['Wf'] = jax.random.normal(ks[4], (D, D), dtype=jnp.float32) * sc
        inp['bf'] = jnp.zeros((D,), dtype=jnp.float32)
        return inp
    _L0_attn_all = _L0_attn_setup()
    _L0_attn_in = {k: v for k, v in _L0_attn_all.items() if k in ('Wq', 'bq', 'Wk', 'bk', 'Wv', 'bv', 'Wf', 'bf')}
    del _L0_attn_all

    def _L0_xattn_setup():
        import jax, jax.numpy as jnp
        import numpy as np
        NUM_HEADS = 16
        CLAMP = 10000.0
        key = jax.random.key(seed)
        ks = jax.random.split(key, 8)
        B, Nq, Nkv, Cq, Ckv = (4, 512, 512, 256, 192)
        s_q = 1.0 / np.sqrt(Cq)
        s_kv = 1.0 / np.sqrt(Ckv)
        return {'query': jax.random.normal(ks[0], (B, Nq, Cq), jnp.float32), 'key_value': jax.random.normal(ks[1], (B, Nkv, Ckv), jnp.float32), 'Wq': jax.random.normal(ks[2], (Cq, Cq), jnp.float32) * s_q, 'bq': jnp.zeros((Cq,), jnp.float32), 'Wk': jax.random.normal(ks[3], (Ckv, Cq), jnp.float32) * s_kv, 'bk': jnp.zeros((Cq,), jnp.float32), 'Wv': jax.random.normal(ks[4], (Ckv, Cq), jnp.float32) * s_kv, 'bv': jnp.zeros((Cq,), jnp.float32), 'Wo': jax.random.normal(ks[5], (Cq, Cq), jnp.float32) * s_q, 'bo': jnp.zeros((Cq,), jnp.float32)}
    _L0_xattn_all = _L0_xattn_setup()
    _L0_xattn_in = {k: v for k, v in _L0_xattn_all.items() if k in ('Wq', 'bq', 'Wk', 'bk', 'Wv', 'bv', 'Wo', 'bo')}
    del _L0_xattn_all

    def _L0_ffn_setup():
        import jax, jax.numpy as jnp
        import numpy as np
        D = 256
        F = 704
        E = 8
        TOP_K = 2
        key = jax.random.key(seed)
        ks = jax.random.split(key, 6)
        std = 0.02
        x = jax.random.normal(ks[0], (2, 512, D), dtype=jnp.float32)
        router_w = jax.random.normal(ks[1], (D, E), dtype=jnp.float32) * std
        w1 = jax.random.normal(ks[2], (E, D, F), dtype=jnp.float32) * std
        v1 = jax.random.normal(ks[3], (E, D, F), dtype=jnp.float32) * std
        w2 = jax.random.normal(ks[4], (E, F, D), dtype=jnp.float32) * std
        bias = jnp.zeros((D,), dtype=jnp.float32)
        return {'x': x, 'router_w': router_w, 'w1': w1, 'v1': v1, 'w2': w2, 'bias': bias}
    _L0_ffn_all = _L0_ffn_setup()
    _L0_ffn_in = {k: v for k, v in _L0_ffn_all.items() if k in ('router_w', 'w1', 'v1', 'w2', 'bias')}
    del _L0_ffn_all

    def _L1_attn_setup():
        import jax, jax.numpy as jnp
        import numpy as np
        NUM_HEADS = 16
        D_MODEL = 256
        HEAD_DIM = D_MODEL // NUM_HEADS
        EMB = 256
        B, L = (2, 512)
        key = jax.random.key(seed)
        k1, k2, k3 = jax.random.split(key, 3)
        scale_in = 1.0 / np.sqrt(EMB)
        scale_out = 1.0 / np.sqrt(D_MODEL)
        return {'x': jax.random.normal(k1, (B, L, EMB), dtype=jnp.float32), 'W_qkv': jax.random.normal(k2, (EMB, 3 * D_MODEL), dtype=jnp.float32) * scale_in, 'b_qkv': jnp.zeros((3 * D_MODEL,), dtype=jnp.float32), 'W_out': jax.random.normal(k3, (D_MODEL, EMB), dtype=jnp.float32) * scale_out, 'b_out': jnp.zeros((EMB,), dtype=jnp.float32)}
    _L1_attn_all = _L1_attn_setup()
    _L1_attn_in = {k: v for k, v in _L1_attn_all.items() if k in ('W_qkv', 'b_qkv', 'W_out', 'b_out')}
    del _L1_attn_all

    def _L1_xattn_setup():
        import jax, jax.numpy as jnp
        import numpy as np
        N_HEADS = 16
        D_EMBED = 256
        D_CROSS = 192
        D_HEAD = D_EMBED // N_HEADS
        key = jax.random.key(seed)
        ks = jax.random.split(key, 10)
        B, SQ, SKV = (8, 1024, 77)
        s_e = 1.0 / np.sqrt(D_EMBED)
        s_c = 1.0 / np.sqrt(D_CROSS)
        return {'x': jax.random.normal(ks[0], (B, SQ, D_EMBED), jnp.float32), 'y': jax.random.normal(ks[1], (B, SKV, D_CROSS), jnp.float32), 'wq': jax.random.normal(ks[2], (D_EMBED, D_EMBED), jnp.float32) * s_e, 'bq': jnp.zeros((D_EMBED,), jnp.float32), 'wk': jax.random.normal(ks[3], (D_CROSS, D_EMBED), jnp.float32) * s_c, 'bk': jnp.zeros((D_EMBED,), jnp.float32), 'wv': jax.random.normal(ks[4], (D_CROSS, D_EMBED), jnp.float32) * s_c, 'bv': jnp.zeros((D_EMBED,), jnp.float32), 'wo': jax.random.normal(ks[5], (D_EMBED, D_EMBED), jnp.float32) * s_e, 'bo': jnp.zeros((D_EMBED,), jnp.float32)}
    _L1_xattn_all = _L1_xattn_setup()
    _L1_xattn_in = {k: v for k, v in _L1_xattn_all.items() if k in ('wq', 'bq', 'wk', 'bk', 'wv', 'bv', 'wo', 'bo')}
    del _L1_xattn_all

    def _L1_ffn_setup():
        import jax, jax.numpy as jnp
        import numpy as np
        EMB = 256
        HEADS = 16
        SEQ = 512
        LATENT = 128
        N_EXP = 8
        TOP_K = 2
        EXP_DIM = 512
        BATCH = 2
        EPS = 1e-06

        def _rmsnorm(x, g):
            return x * jax.lax.rsqrt(jnp.mean(x * x, axis=-1, keepdims=True) + EPS) * g

        def _mla(h, Wq, Wdkv, Wuk, Wuv, Wo):
            B, S, D = h.shape
            hd = D // HEADS
            q = (h @ Wq).reshape(B, S, HEADS, hd)
            c = h @ Wdkv
            k = (c @ Wuk).reshape(B, S, HEADS, hd)
            v = (c @ Wuv).reshape(B, S, HEADS, hd)
            scores = jnp.einsum('bqhd,bkhd->bhqk', q, k) / jnp.sqrt(jnp.asarray(hd, h.dtype))
            causal = jnp.tril(jnp.ones((S, S), bool))
            scores = jnp.where(causal, scores, jnp.asarray(-1000000000.0, h.dtype))
            a = jax.nn.softmax(scores, axis=-1)
            out = jnp.einsum('bhqk,bkhd->bqhd', a, v).reshape(B, S, D)
            return out @ Wo

        def _moe(h, gate_w, w1, w2):
            B, S, D = h.shape
            t = h.reshape(B * S, D)
            logits = t @ gate_w
            top_v, top_i = jax.lax.top_k(logits, TOP_K)
            gates = jax.nn.softmax(top_v, axis=-1)
            T = t.shape[0]
            combine = jnp.zeros((T, N_EXP), t.dtype).at[jnp.arange(T)[:, None], top_i].add(gates)
            hid = jax.nn.silu(jnp.einsum('td,edh->teh', t, w1))
            ye = jnp.einsum('teh,ehd->ted', hid, w2)
            out = jnp.einsum('te,ted->td', combine, ye)
            return out.reshape(B, S, D)
        key = jax.random.key(seed)
        ks = jax.random.split(key, 12)
        s = 0.02
        return {'x': jax.random.normal(ks[0], (BATCH, SEQ, EMB), jnp.float32), 'g1': jnp.ones((EMB,), jnp.float32), 'Wq': jax.random.normal(ks[1], (EMB, EMB), jnp.float32) * s, 'Wdkv': jax.random.normal(ks[2], (EMB, LATENT), jnp.float32) * s, 'Wuk': jax.random.normal(ks[3], (LATENT, EMB), jnp.float32) * s, 'Wuv': jax.random.normal(ks[4], (LATENT, EMB), jnp.float32) * s, 'Wo': jax.random.normal(ks[5], (EMB, EMB), jnp.float32) * s, 'g2': jnp.ones((EMB,), jnp.float32), 'gate_w': jax.random.normal(ks[6], (EMB, N_EXP), jnp.float32) * s, 'w1': jax.random.normal(ks[7], (N_EXP, EMB, EXP_DIM), jnp.float32) * s, 'w2': jax.random.normal(ks[8], (N_EXP, EXP_DIM, EMB), jnp.float32) * s}
    _L1_ffn_all = _L1_ffn_setup()
    _L1_ffn_in = {k: v for k, v in _L1_ffn_all.items() if k in ('g1', 'Wq', 'Wdkv', 'Wuk', 'Wuv', 'Wo', 'g2', 'gate_w', 'w1', 'w2')}
    del _L1_ffn_all
    return {'x': x, 'ctx_768': ctx_768, 'L0_attn_Wq': _L0_attn_in['Wq'], 'L0_attn_bq': _L0_attn_in['bq'], 'L0_attn_Wk': _L0_attn_in['Wk'], 'L0_attn_bk': _L0_attn_in['bk'], 'L0_attn_Wv': _L0_attn_in['Wv'], 'L0_attn_bv': _L0_attn_in['bv'], 'L0_attn_Wf': _L0_attn_in['Wf'], 'L0_attn_bf': _L0_attn_in['bf'], 'L0_xattn_Wq': _L0_xattn_in['Wq'], 'L0_xattn_bq': _L0_xattn_in['bq'], 'L0_xattn_Wk': _L0_xattn_in['Wk'], 'L0_xattn_bk': _L0_xattn_in['bk'], 'L0_xattn_Wv': _L0_xattn_in['Wv'], 'L0_xattn_bv': _L0_xattn_in['bv'], 'L0_xattn_Wo': _L0_xattn_in['Wo'], 'L0_xattn_bo': _L0_xattn_in['bo'], 'L0_ffn_router_w': _L0_ffn_in['router_w'], 'L0_ffn_w1': _L0_ffn_in['w1'], 'L0_ffn_v1': _L0_ffn_in['v1'], 'L0_ffn_w2': _L0_ffn_in['w2'], 'L0_ffn_bias': _L0_ffn_in['bias'], 'L1_attn_W_qkv': _L1_attn_in['W_qkv'], 'L1_attn_b_qkv': _L1_attn_in['b_qkv'], 'L1_attn_W_out': _L1_attn_in['W_out'], 'L1_attn_b_out': _L1_attn_in['b_out'], 'L1_xattn_wq': _L1_xattn_in['wq'], 'L1_xattn_bq': _L1_xattn_in['bq'], 'L1_xattn_wk': _L1_xattn_in['wk'], 'L1_xattn_bk': _L1_xattn_in['bk'], 'L1_xattn_wv': _L1_xattn_in['wv'], 'L1_xattn_bv': _L1_xattn_in['bv'], 'L1_xattn_wo': _L1_xattn_in['wo'], 'L1_xattn_bo': _L1_xattn_in['bo'], 'L1_ffn_g1': _L1_ffn_in['g1'], 'L1_ffn_Wq': _L1_ffn_in['Wq'], 'L1_ffn_Wdkv': _L1_ffn_in['Wdkv'], 'L1_ffn_Wuk': _L1_ffn_in['Wuk'], 'L1_ffn_Wuv': _L1_ffn_in['Wuv'], 'L1_ffn_Wo': _L1_ffn_in['Wo'], 'L1_ffn_g2': _L1_ffn_in['g2'], 'L1_ffn_gate_w': _L1_ffn_in['gate_w'], 'L1_ffn_w1': _L1_ffn_in['w1'], 'L1_ffn_w2': _L1_ffn_in['w2']}

def reference(x, ctx_768, L0_attn_Wq, L0_attn_bq, L0_attn_Wk, L0_attn_bk, L0_attn_Wv, L0_attn_bv, L0_attn_Wf, L0_attn_bf, L0_xattn_Wq, L0_xattn_bq, L0_xattn_Wk, L0_xattn_bk, L0_xattn_Wv, L0_xattn_bv, L0_xattn_Wo, L0_xattn_bo, L0_ffn_router_w, L0_ffn_w1, L0_ffn_v1, L0_ffn_w2, L0_ffn_bias, L1_attn_W_qkv, L1_attn_b_qkv, L1_attn_W_out, L1_attn_b_out, L1_xattn_wq, L1_xattn_bq, L1_xattn_wk, L1_xattn_bk, L1_xattn_wv, L1_xattn_bv, L1_xattn_wo, L1_xattn_bo, L1_ffn_g1, L1_ffn_Wq, L1_ffn_Wdkv, L1_ffn_Wuk, L1_ffn_Wuv, L1_ffn_Wo, L1_ffn_g2, L1_ffn_gate_w, L1_ffn_w1, L1_ffn_w2):
    import jax
    import jax.numpy as jnp

    def _L0_attn_ref(x, Wq, bq, Wk, bk, Wv, bv, Wf, bf):
        import jax, jax.numpy as jnp
        import numpy as np
        NUM_HEADS = 16
        D_MODEL = 256
        HEAD_DIM = D_MODEL // NUM_HEADS
        NEG_INF = -1000000000.0

        def alibi_bidirectional_bias(num_heads, seq_len, dtype=jnp.float32):
            half = num_heads // 2
            base = 24.0 ** (1.0 / half)
            slopes = (1.0 / base ** jnp.arange(1, half + 1, dtype=dtype))[:, None, None]
            pos = jnp.arange(seq_len)
            rel = (pos[None, :] - pos[:, None]).astype(dtype)
            neg = jnp.full((seq_len, seq_len), NEG_INF, dtype=dtype)
            fwd = slopes * jnp.tril(rel) + jnp.triu(neg, 1)
            bwd = slopes * jnp.triu(-rel) + jnp.tril(neg, -1)
            return jnp.concatenate([fwd, bwd], axis=0)
        B, S, D = x.shape
        H, hd = (NUM_HEADS, HEAD_DIM)

        def heads(y):
            return y.reshape(B, S, H, hd).transpose(0, 2, 1, 3)
        q = heads(x @ Wq + bq)
        k = heads(x @ Wk + bk)
        v = heads(x @ Wv + bv)
        bias = alibi_bidirectional_bias(H, S, x.dtype)
        scores = jnp.einsum('bhqd,bhkd->bhqk', q, k) * (1.0 / np.sqrt(hd)) + bias[None]
        attn = jax.nn.softmax(scores, axis=-1)
        out = jnp.einsum('bhqk,bhkd->bhqd', attn, v)
        out = out.transpose(0, 2, 1, 3).reshape(B, S, D)
        return out @ Wf + bf

    def _L0_xattn_ref(query, key_value, Wq, bq, Wk, bk, Wv, bv, Wo, bo):
        import jax, jax.numpy as jnp
        import numpy as np
        NUM_HEADS = 16
        CLAMP = 10000.0
        B, Nq, Cq = query.shape
        Nkv = key_value.shape[1]
        H = NUM_HEADS
        D = Cq // H
        scale = D ** (-0.5)
        q = (query @ Wq + bq).reshape(B, Nq, H, D).transpose(0, 2, 1, 3)
        k = (key_value @ Wk + bk).reshape(B, Nkv, H, D).transpose(0, 2, 1, 3)
        v = (key_value @ Wv + bv).reshape(B, Nkv, H, D).transpose(0, 2, 1, 3)
        attn = jnp.einsum('bhqd,bhkd->bhqk', q, k) * scale
        attn = jnp.clip(attn, -CLAMP, CLAMP)
        attn = jax.nn.softmax(attn, axis=-1)
        attn = jnp.where(jnp.any(jnp.isnan(attn)), jnp.asarray(1.0 / Nkv, attn.dtype), attn)
        x = jnp.einsum('bhqk,bhkd->bqhd', attn, v).reshape(B, Nq, Cq)
        return x @ Wo + bo

    def _L0_ffn_ref(x, router_w, w1, v1, w2, bias):
        import jax, jax.numpy as jnp
        import numpy as np
        D = 256
        F = 704
        E = 8
        TOP_K = 2
        B, S, d = x.shape
        xt = x.reshape(B * S, d)
        scores = jax.nn.softmax(xt @ router_w, axis=-1)
        expert_weights, expert_idx = jax.lax.top_k(scores, TOP_K)
        h = jax.nn.gelu(jnp.einsum('td,edf->tef', xt, w1), approximate=False) * jnp.einsum('td,edf->tef', xt, v1)
        y = jnp.einsum('tef,efd->ted', h, w2)
        yk = jnp.take_along_axis(y, expert_idx[:, :, None], axis=1)
        out = jnp.sum(expert_weights[:, :, None] * yk, axis=1) + bias
        return out.reshape(B, S, d)

    def _L1_attn_ref(x, W_qkv, b_qkv, W_out, b_out):
        import jax, jax.numpy as jnp
        import numpy as np
        NUM_HEADS = 16
        D_MODEL = 256
        HEAD_DIM = D_MODEL // NUM_HEADS
        EMB = 256
        B, L = (2, 512)
        Bn, Ln, _ = x.shape
        qkv = x @ W_qkv + b_qkv
        q = qkv[:, :, :D_MODEL].reshape(Bn, Ln, NUM_HEADS, HEAD_DIM)
        k = qkv[:, :, D_MODEL:2 * D_MODEL].reshape(Bn, Ln, NUM_HEADS, HEAD_DIM)
        v = qkv[:, :, 2 * D_MODEL:].reshape(Bn, Ln, NUM_HEADS, HEAD_DIM)
        scores = jnp.einsum('bqhd,bkhd->bhqk', q, k)
        attn = jax.nn.softmax(scores / jnp.sqrt(jnp.float32(HEAD_DIM)), axis=-1)
        out = jnp.einsum('bhqk,bkhd->bqhd', attn, v).reshape(Bn, Ln, D_MODEL)
        return out @ W_out + b_out

    def _L1_xattn_ref(x, y, wq, bq, wk, bk, wv, bv, wo, bo):
        import jax, jax.numpy as jnp
        import numpy as np
        N_HEADS = 16
        D_EMBED = 256
        D_CROSS = 192
        D_HEAD = D_EMBED // N_HEADS
        B, SQ, _ = x.shape
        SKV = y.shape[1]
        q = (x @ wq + bq).reshape(B, SQ, N_HEADS, D_HEAD)
        k = (y @ wk + bk).reshape(B, SKV, N_HEADS, D_HEAD)
        v = (y @ wv + bv).reshape(B, SKV, N_HEADS, D_HEAD)
        scores = jnp.einsum('bqhd,bkhd->bhqk', q, k) / jnp.sqrt(jnp.asarray(D_HEAD, x.dtype))
        attn = jax.nn.softmax(scores, axis=-1)
        out = jnp.einsum('bhqk,bkhd->bqhd', attn, v).reshape(B, SQ, D_EMBED)
        return out @ wo + bo

    def _L1_ffn_ref(x, g1, Wq, Wdkv, Wuk, Wuv, Wo, g2, gate_w, w1, w2):
        import jax, jax.numpy as jnp
        import numpy as np
        EMB = 256
        HEADS = 16
        SEQ = 512
        LATENT = 128
        N_EXP = 8
        TOP_K = 2
        EXP_DIM = 512
        BATCH = 2
        EPS = 1e-06

        def _rmsnorm(x, g):
            return x * jax.lax.rsqrt(jnp.mean(x * x, axis=-1, keepdims=True) + EPS) * g

        def _mla(h, Wq, Wdkv, Wuk, Wuv, Wo):
            B, S, D = h.shape
            hd = D // HEADS
            q = (h @ Wq).reshape(B, S, HEADS, hd)
            c = h @ Wdkv
            k = (c @ Wuk).reshape(B, S, HEADS, hd)
            v = (c @ Wuv).reshape(B, S, HEADS, hd)
            scores = jnp.einsum('bqhd,bkhd->bhqk', q, k) / jnp.sqrt(jnp.asarray(hd, h.dtype))
            causal = jnp.tril(jnp.ones((S, S), bool))
            scores = jnp.where(causal, scores, jnp.asarray(-1000000000.0, h.dtype))
            a = jax.nn.softmax(scores, axis=-1)
            out = jnp.einsum('bhqk,bkhd->bqhd', a, v).reshape(B, S, D)
            return out @ Wo

        def _moe(h, gate_w, w1, w2):
            B, S, D = h.shape
            t = h.reshape(B * S, D)
            logits = t @ gate_w
            top_v, top_i = jax.lax.top_k(logits, TOP_K)
            gates = jax.nn.softmax(top_v, axis=-1)
            T = t.shape[0]
            combine = jnp.zeros((T, N_EXP), t.dtype).at[jnp.arange(T)[:, None], top_i].add(gates)
            hid = jax.nn.silu(jnp.einsum('td,edh->teh', t, w1))
            ye = jnp.einsum('teh,ehd->ted', hid, w2)
            out = jnp.einsum('te,ted->td', combine, ye)
            return out.reshape(B, S, D)
        x = x + _mla(_rmsnorm(x, g1), Wq, Wdkv, Wuk, Wuv, Wo)
        x = x + _moe(_rmsnorm(x, g2), gate_w, w1, w2)
        return x
    x = _layernorm(x + _L0_attn_ref(x, L0_attn_Wq, L0_attn_bq, L0_attn_Wk, L0_attn_bk, L0_attn_Wv, L0_attn_bv, L0_attn_Wf, L0_attn_bf), axis=-1)
    x = _layernorm(x + _L0_xattn_ref(x, ctx_768, L0_xattn_Wq, L0_xattn_bq, L0_xattn_Wk, L0_xattn_bk, L0_xattn_Wv, L0_xattn_bv, L0_xattn_Wo, L0_xattn_bo), axis=-1)
    x = _layernorm(x + _L0_ffn_ref(x, L0_ffn_router_w, L0_ffn_w1, L0_ffn_v1, L0_ffn_w2, L0_ffn_bias), axis=-1)
    x = _layernorm(x + _L1_attn_ref(x, L1_attn_W_qkv, L1_attn_b_qkv, L1_attn_W_out, L1_attn_b_out), axis=-1)
    x = _layernorm(x + _L1_xattn_ref(x, ctx_768, L1_xattn_wq, L1_xattn_bq, L1_xattn_wk, L1_xattn_bk, L1_xattn_wv, L1_xattn_bv, L1_xattn_wo, L1_xattn_bo), axis=-1)
    x = _layernorm(x + _L1_ffn_ref(x, L1_ffn_g1, L1_ffn_Wq, L1_ffn_Wdkv, L1_ffn_Wuk, L1_ffn_Wuv, L1_ffn_Wo, L1_ffn_g2, L1_ffn_gate_w, L1_ffn_w1, L1_ffn_w2), axis=-1)
    return x

_drawn_inputs = setup_inputs


def setup_inputs(seed=0):
    import zlib

    import numpy as np

    out = dict(_drawn_inputs(seed))
    spreads = {'L0_attn_bq': (0.0, 0.447),
     'L0_attn_bk': (0.0, 2.0),
     'L0_attn_bv': (0.0, 0.1),
     'L0_attn_bf': (0.0, 0.1),
     'L0_xattn_bq': (0.0, 0.409),
     'L0_xattn_bk': (0.0, 2.0),
     'L0_xattn_bv': (0.0, 0.1),
     'L0_xattn_bo': (0.0, 0.1),
     'L0_ffn_bias': (0.0, 0.276),
     'L1_attn_b_qkv': (0.0, 0.1),
     'L1_attn_b_out': (0.0, 0.1),
     'L1_xattn_bq': (0.0, 0.386),
     'L1_xattn_bk': (0.0, 2.0),
     'L1_xattn_bv': (0.0, 0.1),
     'L1_xattn_bo': (0.0, 0.1),
     'L1_ffn_g1': (1.0, 0.6),
     'L1_ffn_g2': (1.0, 0.6)}
    factors = {'L0_ffn_router_w': 8.0,
     'L0_ffn_w1': 8.0,
     'L0_ffn_v1': 8.0,
     'L0_ffn_w2': 8.0,
     'L1_ffn_Wq': 8.0,
     'L1_ffn_Wdkv': 5.935,
     'L1_ffn_Wuk': 8.0,
     'L1_ffn_Wuv': 5.555,
     'L1_ffn_Wo': 5.822,
     'L1_ffn_gate_w': 5.073,
     'L1_ffn_w1': 4.411,
     'L1_ffn_w2': 4.361}
    for name, (base, spread) in spreads.items():
        noise = np.random.default_rng([zlib.crc32(name.encode()), seed]).standard_normal(out[name].shape)
        drawn = base * np.exp(spread * noise) if base else spread * noise
        out[name] = jnp.asarray(drawn.astype(out[name].dtype))
    for name, factor in factors.items():
        out[name] = (out[name] * factor).astype(out[name].dtype)
    return out
```

```python
from contextlib import ExitStack

import numpy as np

import concourse.bass as bass
from concourse import mybir

F32 = mybir.dt.float32
BF16 = mybir.dt.bfloat16
I32 = mybir.dt.int32
U32 = mybir.dt.uint32
ACT = mybir.ActivationFunctionType
ALU = mybir.AluOpType
AX = mybir.AxisListType
ds = bass.ds

P = 128
NB, S, D = 2, 1024, 256
T = NB * S
NT = T // P
TPB = S // P
DC = D // P
H, HD = 16, 16
HG = 4
SC, CW = 154, 192
NX = 8
F0, F1 = 704, 512
NTILE = 2 * T // P + NX
NSLOT = NTILE * P
QSCALE = 1.0 / float(np.sqrt(HD))
NEG = -1e30
CLAMP = 10000.0
PART_Q = (0, 0, 1, 1, 0, 2)
PART_K = (0, 1, 0, 1, 2, 0)
STK = 16 * len(PART_Q)


def wait(eng, sem, value, start=0):
    if isinstance(value, int) and value <= 0:
        return
    eng.wait_ge(sem, start + value)


def hold(eng, sem, value, marker):
    eng.wait_ge(sem, value)
    eng.sem_inc(marker, 1)


def attention_units(mode, keys):
    units = []
    for qb in range(TPB):
        if keys < S:
            units.append((qb, (0, 1, 2, 3), 0, keys))
            continue
        lo = qb * P if mode == "bwd" else 0
        hi = (qb + 1) * P if mode in ("fwd", "causal") else keys
        if hi - lo <= 512:
            units += [(qb, (0, 1), lo, hi - lo), (qb, (2, 3), lo, hi - lo)]
        else:
            units += [(qb, (h,), lo, hi - lo) for h in range(HG)]
    return units


def attention_steps(mode, keys):
    steps = []
    for qh in range(2):
        blocks = range((keys + P - 1) // P)
        if mode == "bwd":
            blocks = [b for b in reversed(blocks) if b >= 4 * qh]
        elif mode in ("fwd", "causal"):
            blocks = [b for b in blocks if b < 4 * qh + 4]
        blocks = list(blocks)
        for kb in blocks:
            c0, c1, diag = 0, 512, None
            d = kb - 4 * qh
            if mode in ("fwd", "causal") and d >= 0:
                c0, diag = d * P, d * P
            if mode == "bwd" and d < 4:
                c1, diag = (d + 1) * P, d * P
            steps.append((qh, kb, min(P, keys - kb * P), c0, c1, diag, kb == blocks[0], kb == blocks[-1]))
    return steps


def block_events(n_steps, qh_ends, n_units):
    events, given, copied = [], 0, None
    first = n_steps // 5
    span = max(1, n_steps - 2 - first)
    for k in range(n_steps):
        due = min(n_units, -(-n_units * max(0, k + 1 - first) // span))
        units = list(range(given, due))
        given = due
        for hh in range(HG):
            events.append(("ST", k, hh))
            if hh >= 1 and units:
                n = -(-len(units) // (HG - hh))
                events += [("A", u) for u in units[:n]]
                units = units[n:]
        if n_units and k == n_steps - 2:
            events += [("MT",), ("MS",)]
        if copied is not None:
            events += [("OT", copied), ("ON", copied)]
            copied = None
        if k >= 1:
            events.append(("PV", k - 1))
            if k - 1 in qh_ends:
                events.append(("OC", qh_ends[k - 1]))
                copied = qh_ends[k - 1]
    assert given == n_units and copied is None
    return events + [("PV", n_steps - 1), ("OC", 1), ("OT", 1), ("ON", 1)]


class Attention:

    def __init__(self, name, modes, keys, alibi, clip, q_scr, k_scr, vx):
        self.name, self.modes, self.keys = name, modes, keys
        self.alibi, self.clip = alibi, clip
        self.q_scr, self.k_scr, self.vx = q_scr, k_scr, vx
        self.kblocks = (keys + P - 1) // P
        self.mrow = STK + (6 if alibi else 0)
        self.units = [attention_units(m, keys) for m in modes]
        self.steps = [attention_steps(m, keys) for m in modes]
        self.nu = [len(u) for u in self.units]
        self.ns = [len(s) for s in self.steps]
        self.events = []
        for slot in range(2):
            ends = {k: s[0] for k, s in enumerate(self.steps[slot]) if s[7] and k + 1 < self.ns[slot]}
            self.events.append([block_events(self.ns[slot], ends, n)
                                for n in (self.nu[1 - slot], 0)])
        self.loads = 12 + (2 if alibi else 0)

    def unit(self, slot, i, k):
        return i * (self.nu[0] + self.nu[1]) + (self.nu[0] if slot else 0) + k

    def step(self, slot, i, k):
        return i * (self.ns[0] + self.ns[1]) + (self.ns[0] if slot else 0) + k


def build_decoder(nc, a, out):
    stack = ExitStack()
    with stack:
        words = 52900
        arena = stack.enter_context(nc.sbuf_tensor("arena", [P, words], F32))
        psum = stack.enter_context(nc.psum_tensor("psum", [P, 8 * 512], F32))
        bank = [psum[:, 512 * n:512 * n + 512] for n in range(8)]
        sems = {}

        def sem(name):
            if name not in sems:
                sems[name] = stack.enter_context(nc.semaphore(name))
            return sems[name]

        top = [0]

        def take(n):
            top[0] += n
            assert top[0] <= words, top[0]
            return arena[:, top[0] - n:top[0]]

        x_tok = take(NT * D).rearrange("p (t d) -> p t d", t=NT)
        ident = take(P)
        identb = take(P // 2).bitcast(BF16)
        mask_right = take(P // 2).bitcast(BF16)
        mask_left = take(P // 2).bitcast(BF16)
        lower = take(P // 2).bitcast(BF16)
        onesb = take(P // 2).bitcast(BF16)
        halves = take(16)
        expert_rank = take(NT * NX).rearrange("p (t e) -> p t e", t=NT)
        slot_i = take(2 * NT).bitcast(I32).rearrange("p (k t) -> p k t", k=2)
        gate_w = take(2 * NT).rearrange("p (k t) -> p k t", k=2)
        tile_expert = take(NTILE).bitcast(I32)
        tile_no = take(NTILE)
        wslots = [take(2576) for _ in range(2)]
        tok_base = top[0]
        ats = take(TPB * D).rearrange("p (t d) -> p t d", t=TPB)
        att = take(TPB * D).rearrange("p (t c q) -> p t c q", t=TPB, c=DC)
        o_tok = take(NT * D)
        w2_low = arena[:, tok_base:top[0]]
        r_tok = take(TPB * D).rearrange("p (t d) -> p t d", t=TPB)
        xts_flat = take(DC * S)
        xts = xts_flat.rearrange("p (c t) -> p c t", c=DC)
        xb = take(2 * 512).rearrange("p (s t d) -> p s t d", s=2, t=2)
        exp_base = top[0] - TPB * D - DC * S - 2 * 512
        route_base = top[0]
        u_f = take(2 * 512).rearrange("p (s t) -> p s t", s=2)
        parts = take(2 * 768).bitcast(BF16).rearrange("p (s k t) -> p s k t", s=2, k=3)
        mv = take(TPB * 2 * 2).rearrange("p (n t k) -> p n t k", n=2, t=TPB)
        bst = take(TPB * 2 * 6).rearrange("p (n t k) -> p n t k", n=2, t=TPB)
        rstd = take(TPB * 2).rearrange("p (n t) -> p n t", n=2)
        ptmp = take(4)
        h_tok = ats
        lat = att.rearrange("p t c q -> p (t c q)")[:, 0:S]
        w2_high = take(2 * NX * D)
        att_base = top[0]
        stk = [[take(HG * S // 2).bitcast(BF16).rearrange("p (h t) -> p h t", h=HG) for _ in range(2)]
               for _ in range(2)]
        prob = take(2 * HG * 512).rearrange("p (s h q) -> p s h q", s=2, h=HG)
        v_st = [take(TPB * HG * 32).rearrange("p (k h w) -> p k h w", k=TPB, h=HG) for _ in range(2)]
        floor_t = take(HG * 512).rearrange("p (h q) -> p h q", h=HG)
        clipped = take(2 * 512).rearrange("p (s q) -> p s q", s=2)
        o_sb = take(512)
        mstat = take(2 * 32).rearrange("p (s m) -> p s m", s=2)
        m_f = take(P)
        m_parts = take(3 * P // 2).bitcast(BF16).rearrange("p (k q) -> p k q", k=3)
        orec = take(16)
        v_base = top[0]
        v_tok = take(NT * D)
        wu_all = arena[:, att_base:att_base + NX * DC * 2 * F0]
        assert att_base + NX * DC * 2 * F0 <= words
        gathered = arena[:, att_base:att_base + 2 * NT * D].rearrange("p (k t d) -> p k t d", k=2, t=NT)

        scr = {}

        def dram(name, shape, dt=F32):
            return nc.dram_tensor(name, shape, dt, kind="Internal").ap()

        q_scr = dram("q_parts", (3, 2, 2, NB, 64, S), BF16)
        k_scr = dram("k_parts", (3, 2, 2, NB, 64, S), BF16)
        kx_scr = [dram(f"kx_parts{n}", (3, 2, 2, NB, 64, SC), BF16) for n in range(2)]
        vx_scr = [dram(f"vx{n}", (P, 4 * 4 * 64)) for n in range(2)]
        xs_scr = dram("slot_rows", (NSLOT, D))
        ys_scr = dram("slot_out", (NSLOT, D))

        stage_done = sem("stage_done")
        stages = []

        def weight_slot(n):
            w = wslots[n % 2]
            return w

        wdefs = []

        def weights(*items):
            w, at, views, loads = wslots[len(wdefs) % 2], 0, [], []
            for kind, src in items:
                if kind == "mat":
                    rows, cols = src.shape
                    c = (rows + P - 1) // P
                    v = w[:, at:at + c * cols].rearrange("p (c n) -> p c n", c=c)
                    at += c * cols
                    if rows % P:
                        for k in range(c):
                            n = min(P, rows - k * P)
                            loads.append((v[0:n, k, :], src[k * P:k * P + n, :]))
                    else:
                        loads.append((v, src.rearrange("(c p) n -> p c n", p=P)))
                elif kind == "row":
                    v = w[:, at:at + D]
                    at += D
                    loads.append((v, src.partition_broadcast(P)))
                else:
                    v = w[:, at:at + DC]
                    at += DC
                    loads.append((v, src.rearrange("(c p) -> p c", p=P)))
                views.append(v)
            assert at <= 2576, at
            wdefs.append(loads)
            return views

        def load_weights(sp, n):
            if n < len(wdefs):
                for dst, src in wdefs[n]:
                    sp.dma_start(dst, src, allow_slow_non_contiguous=True).then_inc(sem(f"weights{n}"), 16)

        def weights_ready(eng, n):
            eng.wait_ge(sem(f"weights{n}"), 16 * len(wdefs[n]))

        def setup_pool(pool):
            c0 = sem("const_base")
            nc.gpsimd.memset(ident, 0.0)
            nc.gpsimd.memset(lower, 1.0)
            nc.gpsimd.memset(onesb, 1.0)
            nc.gpsimd.memset(halves, -0.5)
            nc.gpsimd.memset(mask_right, 0.0)
            nc.gpsimd.memset(mask_left, 0.0)
            nc.gpsimd.iota(tile_no.bitcast(I32), pattern=[[1, NTILE]], base=0, channel_multiplier=0)
            for e in range(NX):
                nc.gpsimd.memset(expert_rank[:, :, e:e + 1], float(NX - e))
            nc.gpsimd.memset(xts_flat, 0.0).then_inc(c0, 1)
            pool.wait_ge(c0, 1)
            nc.gpsimd.affine_select(out=ident, in_=ident, compare_op=ALU.not_equal, fill=1.0,
                                    base=0, pattern=[[-1, P]], channel_multiplier=1)
            nc.gpsimd.affine_select(out=lower, in_=lower, compare_op=ALU.is_gt, fill=0.0,
                                    base=0, pattern=[[1, P]], channel_multiplier=-1)
            nc.gpsimd.affine_select(out=mask_right, in_=mask_right, compare_op=ALU.is_ge, fill=NEG,
                                    base=0, pattern=[[-1, P]], channel_multiplier=1)
            nc.gpsimd.affine_select(out=mask_left, in_=mask_left, compare_op=ALU.is_ge, fill=NEG,
                                    base=0, pattern=[[1, P]], channel_multiplier=-1)\
                .then_inc(c0, 1)
            pool.wait_ge(c0, 2)
            nc.gpsimd.tensor_copy(identb, ident)
            nc.gpsimd.tensor_copy(tile_no, tile_no.bitcast(I32)).then_inc(c0, 1)

        def setup_sp(sp):
            load_weights(sp, 0)
            load_weights(sp, 1)
            sp.dma_start(x_tok, a["x"].rearrange("b (t p) d -> p (b t) d", p=P)).then_inc(sem("x_loaded"), 16)
            sp.wait_ge(sem("const_base"), 1)
            rows = NSLOT // TPB
            for n in range(TPB):
                sp.dma_start(xs_scr[n * rows:(n + 1) * rows, :].rearrange("(p r) d -> p (r d)", p=P),
                             xts_flat[:, 0:rows * D // P]).then_inc(sem("slots_zeroed"), 16)
            sp.wait_ge(sem("slots_zeroed"), 16 * TPB)
            sp.wait_ge(sem("x_loaded"), 16)

        stages.append(("setup", {"pool": setup_pool, "sp": setup_sp}))

        def token_stage(name, wn, source, norm, rms, outs, w, x_out=True, rows_out=False, final=False,
                        extra_sp=None):
            def t(n):
                return sem(f"tok_{n}")

            wo, brow = w.get("wo"), w.get("brow")
            work = []
            for o in outs:
                if o[0] == "latent":
                    work += [("latent", o, None, half) for half in range(2)]
                elif o[0] in ("qk", "klat"):
                    work += [(o[0], o, f, half) for f in range(2) for half in range(2)]
                elif o[0] in ("v", "vlat"):
                    work += [(o[0], o, None, p) for p in range(TPB // 2)]
                elif o[0] == "logits":
                    work += [("logits", o, None, p) for p in range(2)]
            nw = len(work)
            assert nw % 2 == 0
            nqk = sum(k in ("qk", "klat") for k, *_ in work)
            qk_no = {}
            for k, (kind, *_) in enumerate(work):
                if kind in ("qk", "klat"):
                    qk_no[k] = len(qk_no)
            scratch_use = [sum(1 for n in qk_no.values() if n % 2 == s) for s in range(2)]
            lats = [k for k, x in enumerate(work) if x[0] == "latent"]
            tr_src = h_tok if rms is not None else r_tok
            npool = 2 + (4 if rms is not None else 0)
            n_pairs = TPB // 2
            has_in = source != "x"
            norm_pairs = norm

            def sp_prog(sp):
                for n in ("scr0", "scr1", "out"):
                    sp.sem_inc(t(n), 1)
                if wn is not None:
                    load_weights(sp, wn + 1)
                if extra_sp:
                    extra_sp(sp)
                with sp.Fori(0, NB) as b:
                    if source == "x":
                        wait(sp, t("work_ps"), b * nw, 1)
                        sp.dma_start(xts, a["xT"][:, ds(b * S, S)].rearrange("(c p) t -> p c t", p=P))\
                            .then_inc(t("xt_in"), 16)
                    for k, n in qk_no.items():
                        kind, o, f, half = work[k]
                        sp.wait_ge(t("third"), 2 + b * nqk + n + 1)
                        dst = o[-1]
                        for j in range(2):
                            sp.dma_start(
                                dst[:, f, j, ds(b, 1), :, half * 512:half * 512 + 512]
                                .rearrange("k o r t -> r (k o) t"),
                                parts[j * 64:j * 64 + 64, n % 2, :, :]).then_inc(t(f"scr{n % 2}"), 16)
                    if final:
                        for p in range(n_pairs):
                            sp.wait_ge(t("xs"), b * TPB + 2 * p + 2)
                            sp.dma_start(out[ds(b, 1), p * 256:p * 256 + 256, :]
                                         .rearrange("o (t p) d -> p (o t) d", p=P),
                                         r_tok[:, 2 * p:2 * p + 2, :]).then_inc(t("out"), 16)
                for s in range(2):
                    wait(sp, t(f"scr{s}"), 32 * NB * scratch_use[s], 1)
                if final:
                    sp.wait_ge(t("out"), 1 + 16 * NB * n_pairs)

            def pool_prog(pool):
                if brow is not None:
                    weights_ready(pool, wn)
                with pool.Fori(0, NB) as b:
                    if source == "proj":
                        hold(pool, t("tra_ps"), 1 + b * n_pairs, t("held_pool"))
                        if rms is not None:
                            hold(pool, t("trx_ps"), 1 + b * n_pairs, t("held_pool"))
                            if rows_out:
                                hold(pool, t("pool_x"), 1 + b * 2 * n_pairs, t("held_pool"))
                        for u in range(TPB):
                            nc.gpsimd.tensor_copy(
                                ats[:, u, :].rearrange("p (g w) -> p g w", g=4),
                                o_tok.rearrange("p (g n) -> p g n", g=4)[:, :, ds(b * (TPB * 64) + u * 64, 64)])\
                                .then_inc(t("ats"), 1)
                    if has_in:
                        for p in range(n_pairs):
                            pool.wait_ge(t("r"), 2 + b * n_pairs + p - 1)
                            src = x_tok[:, ds(b * TPB + 2 * p, 2), :]
                            if brow is not None:
                                nc.gpsimd.tensor_tensor(xb[:, p % 2, :, :], src,
                                                        brow.unsqueeze(1).to_broadcast([P, 2, D]), ALU.add)\
                                    .then_inc(t("xb"), 1)
                            else:
                                nc.gpsimd.tensor_copy(xb[:, p % 2, :, :], src).then_inc(t("xb"), 1)
                            if p >= 1:
                                pool_norm(pool, b, p - 1)
                        pool_norm(pool, b, n_pairs - 1)
                        if rms is not None:
                            for p in range(n_pairs):
                                pool_rms(pool, b, p)
                        for p in range(n_pairs):
                            if x_out:
                                if norm:
                                    hold(pool, t("xs"), b * TPB + 2 * p + 2, t("held_pool"))
                                else:
                                    hold(pool, t("r"), 2 + b * n_pairs + p + 1, t("held_pool"))
                                xp = x_tok[:, ds(b * TPB + 2 * p, 2), :]
                                if x_out == "add":
                                    nc.gpsimd.tensor_tensor(xp, xp, r_tok[:, 2 * p:2 * p + 2, :], ALU.add)\
                                        .then_inc(t("pool_x"), 1)
                                else:
                                    nc.gpsimd.tensor_copy(xp, r_tok[:, 2 * p:2 * p + 2, :])\
                                        .then_inc(t("pool_x"), 1)
                            if rows_out:
                                hold(pool, t("h"), b * TPB + 2 * p + 2, t("held_pool"))
                                nc.gpsimd.tensor_copy(
                                    v_tok.rearrange("p (t d) -> p t d", t=NT)[:, ds(b * TPB + 2 * p, 2), :],
                                    h_tok[:, 2 * p:2 * p + 2, :]).then_inc(t("pool_x"), 1)
                    for k, n in qk_no.items():
                        s = n % 2
                        pool.wait_ge(t("second"), b * nqk + n + 1)
                        nc.gpsimd.tensor_tensor(parts[:, s, 2, :], u_f[:, s, :], parts[:, s, 1, :],
                                                ALU.subtract).then_inc(t("third"), 1)

            def pool_norm(pool, b, p):
                if not norm:
                    return
                hold(pool, t("mv"), b * TPB + 2 * p + 2, t("held_pool"))
                nc.gpsimd.tensor_scalar(rstd[:, 0, 2 * p:2 * p + 2], mv[:, 0, 2 * p:2 * p + 2, 1], 1e-5, None,
                                        ALU.add).then_inc(t("pool_n"), 1)
                pool.wait_ge(t("pool_n"), b * 2 * n_pairs + 2 * p + 1)
                nc.gpsimd.tensor_tensor(rstd[:, 0, 2 * p:2 * p + 2], rstd[:, 0, 2 * p:2 * p + 2],
                                        halves[:, 0:2], ALU.pow).then_inc(t("pool_n"), 1)

            def pool_rms(pool, b, p):
                sl = slice(2 * p, 2 * p + 2)
                base = b * 4 * n_pairs + 4 * p
                pool.wait_ge(t("mv2"), b * TPB + 2 * p + 2)
                nc.gpsimd.tensor_tensor(rstd[:, 1, sl], mv[:, 1, sl, 0], mv[:, 1, sl, 0], ALU.mult)\
                    .then_inc(t("pool_r"), 1)
                pool.wait_ge(t("pool_r"), base + 1)
                nc.gpsimd.tensor_tensor(rstd[:, 1, sl], rstd[:, 1, sl], mv[:, 1, sl, 1], ALU.add)\
                    .then_inc(t("pool_r"), 1)
                hold(pool, t("pool_r"), base + 2, t("held_pool"))
                nc.gpsimd.tensor_scalar(rstd[:, 1, sl], rstd[:, 1, sl], 1e-6, None, ALU.add)\
                    .then_inc(t("pool_r"), 1)
                pool.wait_ge(t("pool_r"), base + 3)
                nc.gpsimd.tensor_tensor(rstd[:, 1, sl], rstd[:, 1, sl], halves[:, 0:2], ALU.pow)\
                    .then_inc(t("pool_r"), 1)

            def act_prog(act):
                act.sem_inc(t("att"), 2)
                act.sem_inc(t("xts"), 2)
                with act.Fori(0, NB) as b:
                    if source == "proj":
                        wait(act, t("prj_ps"), b * n_pairs, 1)
                        if lats:
                            wait(act, t("work_ps"), b * nw, 1)
                        for p in range(n_pairs):
                            act.wait_ge(t("tra_ps"), 1 + b * n_pairs + p + 1)
                            nc.scalar.activation(att[:, 2 * p:2 * p + 2, :, :].rearrange("p t c q -> p (t c q)"),
                                                 bank[p % 2][:, :], ACT.Copy).then_inc(t("att"), 1)
                    if has_in and nw:
                        wait(act, t("work_ps"), b * nw, 1)
                        for p in range(n_pairs):
                            act.wait_ge(t("trx_ps"), 1 + b * n_pairs + p + 1)
                            nc.scalar.activation(
                                xts[:, :, 256 * p:256 * p + 256].rearrange("p c (t q) -> p t c q", t=2),
                                bank[4 + p % 2][:, :].rearrange("p (t c q) -> p t c q", t=2, c=DC),
                                ACT.Copy).then_inc(t("xts"), 1)
                    if lats:
                        for k in lats:
                            act.wait_ge(t("work_ps"), 1 + b * nw + k + 1)
                            if k == lats[0]:
                                act.wait_ge(t("prj_ps"), 1 + (b + 1) * n_pairs)
                            half = work[k][3]
                            nc.scalar.activation(lat[:, half * 512:half * 512 + 512], bank[6 + k % 2][:, :],
                                                 ACT.Copy).then_inc(t("lat"), 1)
                    for k, n in qk_no.items():
                        s = n % 2
                        uses = (n - s) // 2
                        act.wait_ge(t("first_u"), b * nqk + n + 1)
                        wait(act, t(f"scr{s}"), (b * scratch_use[s] + uses) * 32, 1)
                        nc.scalar.activation(parts[:, s, 0, :], u_f[:, s, :], ACT.Copy).then_inc(t("first"), 1)
                        act.wait_ge(t("rest_u"), b * nqk + n + 1)
                        nc.scalar.activation(parts[:, s, 1, :], u_f[:, s, :], ACT.Copy).then_inc(t("second"), 1)

            def pe_prog(pe):
                for n in ("tra_ps", "prj_ps", "trx_ps", "work_ps"):
                    pe.sem_inc(t(n), 1)
                weights_ready(pe, wn)
                with pe.Fori(0, NB) as b:
                    def tra(p):
                        for u in (2 * p, 2 * p + 1):
                            if u == 2 * p:
                                pe.wait_ge(t("ats"), b * TPB + 2 * p + 2)
                                pe.wait_ge(t("att"), 2 + b * n_pairs + p - 1)
                            for c in range(DC):
                                at = (u % 2) * D + c * P
                                last = nc.tensor.transpose(bank[p % 2][:, at:at + P], ats[:, u, c * P:c * P + P],
                                                           ident)
                        last.then_inc(t("tra_ps"), 1)

                    def prj(p):
                        pe.wait_ge(t("att"), 2 + b * n_pairs + p + 1)
                        pe.wait_ge(t("r"), 2 + b * n_pairs + p - 1)
                        for u in (2 * p, 2 * p + 1):
                            for c in range(DC):
                                last = nc.tensor.matmul(bank[2 + p % 2][:, (u % 2) * D:(u % 2) * D + D],
                                                        att[:, u, c, :], wo[:, c, :],
                                                        start=(c == 0), stop=(c == DC - 1))
                        last.then_inc(t("prj_ps"), 1)

                    if source == "proj":
                        tra(0)
                        tra(1)
                        for p in range(n_pairs):
                            prj(p)
                            if p + 2 < n_pairs:
                                tra(p + 2)
                    if has_in and nw:
                        for p in range(n_pairs):
                            if rms is not None:
                                pe.wait_ge(t("h"), b * TPB + 2 * p + 2)
                            else:
                                pe.wait_ge(t("xs"), b * TPB + 2 * p + 2)
                            pe.wait_ge(t("xts"), 2 + b * n_pairs + p - 1)
                            for u in (2 * p, 2 * p + 1):
                                for c in range(DC):
                                    at = (u % 2) * D + c * P
                                    last = nc.tensor.transpose(bank[4 + p % 2][:, at:at + P],
                                                               tr_src[:, u, c * P:c * P + P], ident)
                            last.then_inc(t("trx_ps"), 1)
                    if nw:
                        if has_in:
                            pe.wait_ge(t("xts"), 2 + (b + 1) * n_pairs)
                        else:
                            pe.wait_ge(t("xt_in"), 16 * (b + 1))
                        for k, (kind, o, f, half) in enumerate(work):
                            pe.wait_ge(t("work_free"), 2 + b * nw + k - 1)
                            ps = bank[6 + k % 2]
                            mat = o[1]
                            if kind == "qk":
                                for c in range(DC):
                                    last = nc.tensor.matmul(ps[:, :], mat[:, c, f * P:f * P + P],
                                                            xts[:, c, half * 512:half * 512 + 512],
                                                            start=(c == 0), stop=(c == DC - 1))
                            elif kind == "latent":
                                for c in range(DC):
                                    last = nc.tensor.matmul(ps[:, :], mat[:, c, :],
                                                            xts[:, c, half * 512:half * 512 + 512],
                                                            start=(c == 0), stop=(c == DC - 1))
                            elif kind == "klat":
                                pe.wait_ge(t("lat"), b * 2 + half + 1)
                                last = nc.tensor.matmul(ps[:, :], mat[:, 0, f * P:f * P + P],
                                                        lat[:, half * 512:half * 512 + 512], start=True, stop=True)
                            elif kind == "vlat":
                                for u in (2 * half, 2 * half + 1):
                                    last = nc.tensor.matmul(ps[:, (u % 2) * D:(u % 2) * D + D],
                                                            lat[:, u * P:u * P + P], mat[:, 0, :],
                                                            start=True, stop=True)
                            elif kind == "v":
                                for u in (2 * half, 2 * half + 1):
                                    for c in range(DC):
                                        last = nc.tensor.matmul(ps[:, (u % 2) * D:(u % 2) * D + D],
                                                                xts[:, c, u * P:u * P + P], mat[:, c, :],
                                                                start=(c == 0), stop=(c == DC - 1))
                            elif kind == "logits":
                                for u in range(4 * half, 4 * half + 4):
                                    for c in range(DC):
                                        last = nc.tensor.matmul(ps[:, (u % 4) * NX:(u % 4) * NX + NX],
                                                                xts[:, c, u * P:u * P + P], mat[:, c, :],
                                                                start=(c == 0), stop=(c == DC - 1))
                            last.then_inc(t("work_ps"), 1)

            def dve_prog(dve):
                if wn is not None:
                    weights_ready(dve, wn)
                if has_in:
                    dve.sem_inc(t("r"), 2)
                if nw:
                    dve.sem_inc(t("work_free"), 2)
                with dve.Fori(0, NB) as b:
                    def add(p):
                        rp = r_tok[:, 2 * p:2 * p + 2, :]
                        dve.wait_ge(t("xb"), b * n_pairs + p + 1)
                        if p == 0:
                            if nw and rms is None:
                                wait(dve, t("trx_ps"), b * n_pairs, 1)
                            if x_out:
                                wait(dve, t("pool_x"), b * n_pairs * (2 if rows_out else 1), 1)
                            if final:
                                wait(dve, t("out"), 16 * b * n_pairs, 1)
                        if source == "proj":
                            dve.wait_ge(t("prj_ps"), 1 + b * n_pairs + p + 1)
                            nc.vector.tensor_tensor(rp, bank[2 + p % 2][:, :].rearrange("p (t d) -> p t d", t=2),
                                                    xb[:, p % 2, :, :], ALU.add).then_inc(t("r"), 1)
                        else:
                            for n in range(2):
                                for u in range(2):
                                    last = nc.vector.scalar_tensor_tensor(
                                        out=r_tok[:, 2 * p + u, :],
                                        in0=gathered[:, n, ds(b * TPB + 2 * p + u, 1), :].rearrange("p o d -> p (o d)"),
                                        scalar=gate_w[:, n, ds(b * TPB + 2 * p + u, 1)],
                                        in1=(xb[:, p % 2, u, :] if n == 0 else r_tok[:, 2 * p + u, :]),
                                        op0=ALU.mult, op1=ALU.add)
                                    if n == 0:
                                        last.then_inc(t("first_row"), 1)
                                if n == 0:
                                    dve.wait_ge(t("first_row"), b * TPB + 2 * p + 2)
                            last.then_inc(t("r"), 1)

                    def moments(p, n, src, ready, value, done):
                        dve.wait_ge(ready, value)
                        for u in (2 * p, 2 * p + 1):
                            nc.vector.bn_stats(bst[:, n, u, :], src[:, u, :]).then_inc(t(f"st{n}"), 1)
                        for u in (2 * p, 2 * p + 1):
                            hold(dve, t(f"st{n}"), b * TPB + u + 1, t("held_dve"))
                            nc.vector.bn_aggr(mv[:, n, u, :], bst[:, n, u, :]).then_inc(t(done), 1)

                    def norm_rows(p):
                        dve.wait_ge(t("pool_n"), b * 2 * n_pairs + 2 * p + 2)
                        for u in (2 * p, 2 * p + 1):
                            nc.vector.tensor_scalar(r_tok[:, u, :], r_tok[:, u, :], mv[:, 0, u, 0:1],
                                                    rstd[:, 0, u:u + 1], ALU.subtract, ALU.mult)\
                                .then_inc(t("xs"), 1)

                    def rms_rows(p):
                        dve.wait_ge(t("pool_r"), b * 4 * n_pairs + 4 * p + 4)
                        if p == 0:
                            if source == "proj":
                                dve.wait_ge(t("tra_ps"), 1 + (b + 1) * n_pairs)
                        for u in (2 * p, 2 * p + 1):
                            nc.vector.scalar_tensor_tensor(out=h_tok[:, u, :], in0=r_tok[:, u, :],
                                                           scalar=rstd[:, 1, u:u + 1], in1=rms,
                                                           op0=ALU.mult, op1=ALU.mult).then_inc(t("h"), 1)

                    if has_in:
                        for p in range(n_pairs + 1):
                            if p < n_pairs:
                                add(p)
                                if norm:
                                    moments(p, 0, r_tok, t("r"), 2 + b * n_pairs + p + 1, "mv")
                                elif rms is not None:
                                    moments(p, 1, r_tok, t("r"), 2 + b * n_pairs + p + 1, "mv2")
                            if p >= 1 and norm:
                                norm_rows(p - 1)
                                if rms is not None:
                                    moments(p - 1, 1, r_tok, t("xs"), b * TPB + 2 * p, "mv2")
                        if rms is not None:
                            for p in range(n_pairs):
                                rms_rows(p)
                    for k, (kind, o, f, half) in enumerate(work):
                        dve_unit(dve, b, k, kind, o, f, half)

            def dve_unit(dve, b, k, kind, o, f, half):
                if kind == "latent":
                    dve.wait_ge(t("lat"), b * 2 + lats.index(k) + 1)
                    dve.sem_inc(t("work_free"), 1)
                    return
                ps = bank[6 + k % 2]
                if kind in ("qk", "klat"):
                    n = qk_no[k]
                    s = n % 2
                    dve.wait_ge(t("work_ps"), 1 + b * nw + k + 1)
                    dve.wait_ge(t("third"), 2 + b * nqk + n - 1)
                    bias, scale = (o[2], o[3]) if kind == "qk" else (None, 1.0)
                    if bias is None:
                        nc.vector.tensor_scalar(u_f[:, s, :], ps[:, :], scale, None, ALU.mult)\
                            .then_inc(t("first_u"), 1)
                    else:
                        nc.vector.tensor_scalar(u_f[:, s, :], ps[:, :], bias[:, f:f + 1], scale, ALU.add, ALU.mult)\
                            .then_inc(t("first_u"), 1)
                    dve.wait_ge(t("first_u"), b * nqk + n + 1)
                    dve.sem_inc(t("work_free"), 1)
                    dve.wait_ge(t("first"), b * nqk + n + 1)
                    nc.vector.tensor_tensor(u_f[:, s, :], u_f[:, s, :], parts[:, s, 0, :], ALU.subtract)\
                        .then_inc(t("rest_u"), 1)
                elif kind in ("v", "vlat"):
                    dve.wait_ge(t("work_ps"), 1 + b * nw + k + 1)
                    for u in range(2):
                        dst = v_tok.rearrange("p (g n) -> p g n", g=4)[:, :, ds(b * (TPB * 64) + (2 * half + u) * 64, 64)]
                        src = ps[:, u * D:u * D + D].rearrange("p (g w) -> p g w", g=4)
                        if kind == "v":
                            last = nc.vector.tensor_tensor(dst, src, o[2].rearrange("p (g w) -> p g w", g=4), ALU.add)
                        else:
                            last = nc.vector.tensor_copy(dst, src)
                    last.then_inc(t("work_free"), 1)
                elif kind == "logits":
                    dve.wait_ge(t("work_ps"), 1 + b * nw + k + 1)
                    nc.vector.tensor_copy(o[2][:, ds(b * TPB * NX + half * 4 * NX, 4 * NX)], ps[:, 0:4 * NX])\
                        .then_inc(t("work_free"), 1)

            def pool_wrapped(pool):
                pool.sem_inc(t("pool_x"), 1)
                if nqk:
                    pool.sem_inc(t("third"), 2)
                pool_prog(pool)

            progs = {"sp": sp_prog, "dve": dve_prog, "pool": pool_wrapped}
            if nw or source == "proj":
                progs["pe"] = pe_prog
                progs["act"] = act_prog
            stages.append((name, progs))

        def context_stage(name, wn, layers):
            ct = xts_flat[:, 0:2 * NB * SC].rearrange("p (c t) -> p c t", c=2)
            vx_t = o_tok[:, 0:2 * 1024].rearrange("p (l g n w) -> p l g n w", l=2, g=4, n=4)
            rows = (P, CW - P)
            n_tok = NB * SC

            def t(n):
                return sem(f"ctx_{n}")

            kunits = [(l, f) for l in range(2) for f in range(2)]
            vunits = [(l, b, kb) for l in range(2) for b in range(NB) for kb in range(2)]

            def sp_prog(sp):
                load_weights(sp, wn + 1)
                for c in range(2):
                    sp.dma_start(ct[0:rows[c], c, :], a["ctxT"][c * P:c * P + rows[c], :]).then_inc(t("in"), 16)
                for n, (l, f) in enumerate(kunits):
                    sp.wait_ge(t("third"), n + 1)
                    for j in range(2):
                        for b in range(NB):
                            sp.dma_start(kx_scr[l][:, f, j, b, :, :].rearrange("k r t -> r k t"),
                                         parts[j * 64:j * 64 + 64, n % 2, :, b * SC:b * SC + SC])\
                                .then_inc(t(f"scr{n % 2}"), 16)
                sp.wait_ge(t("v"), len(vunits))
                for l in range(2):
                    sp.dma_start(vx_scr[l], vx_t[:, l, :, :, :].rearrange("p g n w -> p (g n w)"))\
                        .then_inc(t("vstored"), 16)
                sp.wait_ge(t("vstored"), 32)
                for s in range(2):
                    sp.wait_ge(t(f"scr{s}"), 16 * 4 * 2)

            def pe_prog(pe):
                weights_ready(pe, wn)
                pe.wait_ge(t("in"), 32)
                for n, (l, f) in enumerate(kunits):
                    wait(pe, t("u"), n - 1)
                    for c in range(2):
                        last = nc.tensor.matmul(bank[n % 2][:, 0:n_tok], w_ctx[l]["wk"][0:rows[c], c, f * P:f * P + P],
                                                ct[0:rows[c], c, :], start=(c == 0), stop=(c == 1))
                    last.then_inc(t("k_ps"), 1)
                for n, (l, b, kb) in enumerate(vunits):
                    wait(pe, t("v"), n - 1)
                    k0, kn = b * SC + kb * P, min(P, SC - kb * P)
                    for c in range(2):
                        last = nc.tensor.matmul(bank[2 + n % 2][0:kn, 0:D], ct[0:rows[c], c, k0:k0 + kn],
                                                w_ctx[l]["wv"][0:rows[c], c, :], start=(c == 0), stop=(c == 1))
                    last.then_inc(t("v_ps"), 1)

            def act_prog(act):
                for n in range(len(kunits)):
                    s = n % 2
                    act.wait_ge(t("u"), n + 1)
                    wait(act, t(f"scr{s}"), (n // 2) * 64)
                    nc.scalar.activation(parts[:, s, 0, 0:n_tok], u_f[:, s, 0:n_tok], ACT.Copy).then_inc(t("first"), 1)
                    act.wait_ge(t("rest"), n + 1)
                    nc.scalar.activation(parts[:, s, 1, 0:n_tok], u_f[:, s, 0:n_tok], ACT.Copy).then_inc(t("second"), 1)

            def pool_prog(pool):
                for n in range(len(kunits)):
                    s = n % 2
                    pool.wait_ge(t("second"), n + 1)
                    nc.gpsimd.tensor_tensor(parts[:, s, 2, 0:n_tok], u_f[:, s, 0:n_tok], parts[:, s, 1, 0:n_tok],
                                            ALU.subtract).then_inc(t("third"), 1)

            def dve_prog(dve):
                weights_ready(dve, wn)
                nc.vector.memset(vx_t, 0.0).then_inc(t("zero"), 1)
                for n, (l, f) in enumerate(kunits):
                    s = n % 2
                    wait(dve, t("third"), n - 1)
                    dve.wait_ge(t("k_ps"), n + 1)
                    nc.vector.tensor_scalar(u_f[:, s, 0:n_tok], bank[s][:, 0:n_tok], w_ctx[l]["bk"][:, f:f + 1], None,
                                            ALU.add).then_inc(t("u"), 1)
                    dve.wait_ge(t("first"), n + 1)
                    nc.vector.tensor_tensor(u_f[:, s, 0:n_tok], u_f[:, s, 0:n_tok], parts[:, s, 0, 0:n_tok],
                                            ALU.subtract).then_inc(t("rest"), 1)
                dve.wait_ge(t("zero"), 1)
                for n, (l, b, kb) in enumerate(vunits):
                    kn = min(P, SC - kb * P)
                    dve.wait_ge(t("v_ps"), n + 1)
                    nc.vector.tensor_tensor(vx_t[0:kn, l, :, 2 * b + kb, :],
                                            bank[2 + n % 2][0:kn, 0:D].rearrange("p (g w) -> p g w", g=4),
                                            w_ctx[l]["bv"][0:kn, :].rearrange("p (g w) -> p g w", g=4), ALU.add)\
                        .then_inc(t("v"), 1)

            stages.append((name, {"sp": sp_prog, "pe": pe_prog, "act": act_prog, "pool": pool_prog, "dve": dve_prog}))

        def attention_stage(at, extra_sp=None):
            def t(n):
                return sem(f"att_{n}")

            keys, nkb = at.keys, at.kblocks
            vtiles = TPB if keys == S else 2
            a_bank = (0, 2)
            st_bank = (4, 5)

            def load_group(sp, s, i):
                q, k = stk[s]
                for n in range(6):
                    sp.dma_start(q[16 * n:16 * n + 16, :, :],
                                 at.q_scr[PART_Q[n], s].rearrange("j b (h d) t -> (j b) d h t", h=HG)[ds(i, 1)]
                                 .rearrange("o d h t -> d (o h) t")).then_inc(t(f"ld{s}"), 16)
                    sp.dma_start(k[16 * n:16 * n + 16, :, 0:keys],
                                 at.k_scr[PART_K[n], s].rearrange("j b (h d) t -> (j b) d h t", h=HG)[ds(i, 1)]
                                 .rearrange("o d h t -> d (o h) t")).then_inc(t(f"ld{s}"), 16)
                if at.alibi:
                    for side in range(2):
                        sp.dma_start(stk[s][side][STK:STK + 6, :, :],
                                     a["alibi"][side, s, ds(i, 1), :, :, :].rearrange("o r h t -> (o r) h t"))\
                            .then_inc(t(f"ld{s}"), 16)

            def load_max(sp, s, i):
                sp.wait_ge(t("m_parts"), 2 * i + s + 1)
                for n in range(3):
                    sp.dma_start(stk[s][0][at.mrow + n:at.mrow + n + 1, :, :]
                                 .rearrange("o h (b q) -> o (h b) q", q=P),
                                 m_parts[0:32, n, :]).then_inc(t(f"mld{s}"), 16)

            def sp_prog(sp):
                if keys < S:
                    sp.dma_start(v_tok[:, 0:1024], at.vx).then_inc(t("vx"), 16)
                for s in range(2):
                    sp.dma_start(stk[s][1][at.mrow:at.mrow + 3, :, 0:keys], a["ones"][0:3, :, 0:keys])\
                        .then_inc(t("ones"), 16)
                load_group(sp, 0, 0)
                load_group(sp, 1, 0)
                load_max(sp, 0, 0)
                if extra_sp:
                    extra_sp(sp)
                with sp.Fori(0, 3) as i:
                    load_max(sp, 1, i)
                    sp.wait_ge(t("pv"), 2 + at.step(0, i, at.ns[0]))
                    load_group(sp, 0, i + 1)
                    load_max(sp, 0, i + 1)
                    sp.wait_ge(t("pv"), 2 + at.step(1, i, at.ns[1]))
                    load_group(sp, 1, i + 1)
                load_max(sp, 1, 3)

            def stage_values(s, i):
                src = v_tok[:, ds(i * (vtiles * 64) + s * (2 * NB * vtiles * 64), vtiles * 64)]
                nc.gpsimd.tensor_copy(v_st[s][:, 0:vtiles, :, 0:HD],
                                      src.rearrange("p (k h w) -> p k h w", k=vtiles, h=HG)).then_inc(t("vs"), 1)

            def pool_prog(pool):
                for s in range(2):
                    nc.gpsimd.memset(v_st[s][:, :, :, HD:2 * HD], 1.0)
                if keys < S:
                    pool.wait_ge(t("vx"), 16)
                stage_values(0, 0)
                stage_values(1, 0)
                with pool.Fori(0, 3) as i:
                    for s in range(2):
                        pool.wait_ge(t("pv"), 2 + at.step(s, i, at.ns[s]))
                        stage_values(s, i + 1)

            def pe_max(pe, s, i, k):
                qb, heads, key0, width = at.units[s][k]
                u = at.unit(s, i, k)
                par = (k + (at.nu[0] if s else 0)) % 2
                if k == 0:
                    pe.wait_ge(t(f"ld{s}"), 16 * at.loads * (i + 1))
                pe.wait_ge(t("a_max"), 2 + u - 1)
                q, kst = stk[s]
                rows = STK + (6 if at.alibi else 0)
                mode = at.modes[s]
                for n, h in enumerate(heads):
                    if keys < S:
                        spans = [(bank[a_bank[par] + n // 2][:, (n % 2) * 256:(n % 2) * 256 + width], 0, width)]
                    elif len(heads) == 2:
                        spans = [(bank[a_bank[par] + n][:, 0:width], 0, width)]
                    else:
                        spans = [(bank[a_bank[par]][:, 0:512], 0, 512),
                                 (bank[a_bank[par] + 1][:, 0:width - 512], 512, width)]
                    dcol = {"fwd": width - P, "causal": width - P, "bwd": 0}.get(mode)
                    for dst, lo, hi in spans:
                        masked = dcol is not None and lo <= dcol < hi
                        last = nc.tensor.matmul(dst, q[0:rows, h, qb * P:qb * P + P],
                                                kst[0:rows, h, key0 + lo:key0 + hi], start=True, stop=not masked)
                        if masked:
                            m = mask_left if mode == "bwd" else mask_right
                            last = nc.tensor.matmul(dst[:, dcol - lo:dcol - lo + P], identb, m,
                                                    start=False, stop=True)
                last.then_inc(t("a_ps"), 1)

            def pe_scores(pe, s, i, k, hh):
                qh, kb, kn, c0, c1, diag, first, last_ = at.steps[s][k]
                u = at.step(s, i, k) * HG + hh
                par = hh % 2
                q, kst = stk[s]
                if k == 0 and hh == 0:
                    pe.wait_ge(t(f"mld{s}"), 48 * (i + 1))
                if at.clip and (kb == 0) and hh == 0:
                    for h in range(HG):
                        idx = ((2 * i + s) * 2 + qh) * HG + h
                        pe.wait_ge(t("st_read"), 2 + at.step(s, i, k) * HG)
                        pe.wait_ge(t("fl"), 2 + idx - 1)
                        nc.tensor.matmul(bank[st_bank[h % 2]][:, :], kst[at.mrow:at.mrow + 3, h, 0:P],
                                         q[at.mrow:at.mrow + 3, h, qh * 512:qh * 512 + 512],
                                         start=True, stop=True).then_inc(t("fl_ps"), 1)
                    pe.wait_ge(t("fl"), 2 + ((2 * i + s) * 2 + qh) * HG + HG)
                pe.wait_ge(t("st_read") if at.clip else t("p"), 2 + u - 1)
                dst = bank[st_bank[par]][0:kn, c0:c1]
                rows = at.mrow + 3
                last = nc.tensor.matmul(dst, kst[0:rows, hh, kb * P:kb * P + kn],
                                        q[0:rows, hh, qh * 512 + c0:qh * 512 + c1],
                                        start=True, stop=diag is None)
                if diag is not None:
                    m = mask_right if at.modes[s] == "bwd" else mask_left
                    last = nc.tensor.matmul(bank[st_bank[par]][:, diag:diag + P], identb, m, start=False, stop=True)
                last.then_inc(t("st_ps"), 1)

            def pe_values(pe, s, i, k):
                qh, kb, kn, c0, c1, diag, first, last_ = at.steps[s][k]
                n = at.step(s, i, k)
                par = (k + (at.ns[0] if s else 0)) % 2
                if k == 0:
                    pe.wait_ge(t("vs"), 2 * i + s + 1)
                if first:
                    wait(pe, t("o_sb"), (2 * i + s) * 2 + qh, 1)
                if kn <= 32:
                    hold(pe, t("p"), 2 + n * HG + HG, t("held_pe"))
                else:
                    pe.wait_ge(t("p"), 2 + n * HG + HG)
                for hh in range(HG):
                    last = nc.tensor.matmul(bank[6][32 * hh:32 * hh + 32, c0:c1], v_st[s][0:kn, kb, hh, :],
                                            prob[0:kn, par, hh, c0:c1], start=first, stop=last_)
                last.then_inc(t("pv"), 1)

            def pe_events(pe, ev, s, i, s2, i2, t0):
                use = 0
                for e in ev:
                    if e[0] == "A":
                        pe_max(pe, s2, i2, e[1])
                    elif e[0] == "ST":
                        pe_scores(pe, s, i, e[1], e[2])
                    elif e[0] == "PV":
                        pe_values(pe, s, i, e[1])
                    elif e[0] == "MT":
                        pe.wait_ge(t("a_max"), 2 + at.unit(s2, i2, at.nu[s2]))
                        wait(pe, t("t_read"), t0 + use)
                        nc.tensor.transpose(bank[7][0:32, 0:P], mstat[:, s2, :], ident).then_inc(t("t_ps"), 1)
                        use += 1
                    elif e[0] == "OT":
                        pe.wait_ge(t("o_sb"), 1 + (2 * i + s) * 2 + e[1] + 1)
                        wait(pe, t("t_read"), t0 + use)
                        for b in range(4):
                            last = nc.tensor.transpose(bank[7][:, b * P:b * P + P], o_sb[:, b * P:b * P + P], ident)
                        last.then_inc(t("t_ps"), 1)
                        use += 1

            def each_block(run):
                eng, block, prologue = run
                prologue(eng)
                with eng.Fori(0, 3) as i:
                    block(eng, at.events[0][0], 0, i, 1, i, 1 + 6 * i)
                    block(eng, at.events[1][0], 1, i, 0, i + 1, 4 + 6 * i)
                block(eng, at.events[0][0], 0, 3, 1, 3, 19)
                block(eng, at.events[1][1], 1, 3, None, None, 22)

            def pe_prog(pe):
                pe.wait_ge(t("ones"), 32)

                def prologue(pe):
                    for k in range(at.nu[0]):
                        pe_max(pe, 0, 0, k)
                    pe_events(pe, [("MT",)], None, None, 0, 0, 0)
                each_block((pe, pe_events, prologue))

            def act_events(act, ev, s, i, s2, i2, t0):
                for e in ev:
                    if e[0] != "ST":
                        continue
                    k, hh = e[1], e[2]
                    qh, kb, kn, c0, c1, diag, first, last_ = at.steps[s][k]
                    n = at.step(s, i, k)
                    par = (k + (at.ns[0] if s else 0)) % 2
                    if at.clip and kb == 0 and hh == 0:
                        for h in range(HG):
                            idx = ((2 * i + s) * 2 + qh) * HG + h
                            act.wait_ge(t("fl_ps"), idx + 1)
                            if h == 0:
                                wait(act, t("clip"), n * HG, 1)
                            nc.scalar.activation(floor_t[:, h, :], bank[st_bank[h % 2]][:, :], ACT.Copy,
                                                 bias=-CLAMP).then_inc(t("fl"), 1)
                    if hh == 0:
                        act.wait_ge(t("pv"), 2 + n - 1)
                    if at.clip:
                        act.wait_ge(t("clip"), 1 + n * HG + hh + 1)
                        src = clipped[0:kn, hh % 2, c0:c1]
                    else:
                        act.wait_ge(t("st_ps"), n * HG + hh + 1)
                        src = bank[st_bank[hh % 2]][0:kn, c0:c1]
                    nc.scalar.activation(prob[0:kn, par, hh, c0:c1], src, ACT.Exp).then_inc(t("p"), 1)

            def act_prog(act):
                act.sem_inc(t("p"), 2)
                if at.clip:
                    act.sem_inc(t("fl"), 2)
                each_block((act, act_events, lambda act: None))

            def dve_max(dve, s, i, k):
                qb, heads, key0, width = at.units[s][k]
                u = at.unit(s, i, k)
                par = (k + (at.nu[0] if s else 0)) % 2
                dve.wait_ge(t("a_ps"), u + 1)
                both = psum[:, 1024 * par:1024 * par + 1024]
                if keys < S:
                    src = both.rearrange("p (h k) -> p h k", h=HG)[:, :, 0:width]
                elif len(heads) == 2:
                    src = both.rearrange("p (h k) -> p h k", h=2)[:, :, 0:width]
                else:
                    src = both[:, 0:width].unsqueeze(1)
                dst = mstat[:, s, :].rearrange("p (h b) -> p h b", h=HG)[:, heads[0]:heads[-1] + 1, qb]
                nc.vector.tensor_reduce(dst, src, AX.X, ALU.max).then_inc(t("a_max"), 1)

            def dve_events(dve, ev, s, i, s2, i2, t0):
                use = 0
                for e in ev:
                    if e[0] == "A":
                        dve_max(dve, s2, i2, e[1])
                    elif e[0] == "ST" and at.clip:
                        k, hh = e[1], e[2]
                        qh, kb, kn, c0, c1, diag, first, last_ = at.steps[s][k]
                        n = at.step(s, i, k)
                        if kb == 0 and hh == 0:
                            dve.wait_ge(t("fl"), 2 + ((2 * i + s) * 2 + qh) * HG + HG)
                        dve.wait_ge(t("st_ps"), n * HG + hh + 1)
                        dve.wait_ge(t("p"), 2 + n * HG + hh - 1)
                        nc.vector.scalar_tensor_tensor(out=clipped[0:kn, hh % 2, :],
                                                       in0=bank[st_bank[hh % 2]][0:kn, :], scalar=0.0,
                                                       in1=floor_t[0:kn, hh, :], op0=ALU.min, op1=ALU.max)\
                            .then_inc(t("clip"), 1)
                        dve.wait_ge(t("clip"), 1 + n * HG + hh + 1)
                        dve.sem_inc(t("st_read"), 1)
                    elif e[0] == "OC":
                        ends = [k for k, x in enumerate(at.steps[s]) if x[7]]
                        n = at.step(s, i, ends[e[1]])
                        dve.wait_ge(t("pv"), 2 + n + 1)
                        nc.vector.tensor_copy(o_sb, bank[6][:, :]).then_inc(t("o_sb"), 1)
                    elif e[0] == "MS":
                        g = 2 * i2 + s2
                        dve.wait_ge(t("t_ps"), t0 + use + 1)
                        wait(dve, t(f"mld{1 - s2}"), mld_before(g, i2, s2))
                        if at.clip:
                            nc.vector.tensor_scalar(m_f[0:32, :], bank[7][0:32, 0:P], -CLAMP, CLAMP, ALU.max, ALU.min)\
                                .then_inc(t("m_step"), 1)
                            dve.wait_ge(t("m_step"), MS * g + 1)
                            nc.vector.tensor_scalar(m_f[0:32, :], m_f[0:32, :], -1.0, None, ALU.mult)\
                                .then_inc(t("m_step"), 1)
                            at0 = 2
                        else:
                            nc.vector.tensor_scalar(m_f[0:32, :], bank[7][0:32, 0:P], -1.0, None, ALU.mult)\
                                .then_inc(t("m_step"), 1)
                            at0 = 1
                        dve.wait_ge(t("m_step"), MS * g + at0)
                        dve.sem_inc(t("t_read"), 1)
                        nc.vector.tensor_copy(m_parts[0:32, 0, :], m_f[0:32, :]).then_inc(t("m_step"), 1)
                        dve.wait_ge(t("m_step"), MS * g + at0 + 1)
                        nc.vector.tensor_tensor(m_f[0:32, :], m_f[0:32, :], m_parts[0:32, 0, :], ALU.subtract)\
                            .then_inc(t("m_step"), 1)
                        dve.wait_ge(t("m_step"), MS * g + at0 + 2)
                        nc.vector.tensor_copy(m_parts[0:32, 1, :], m_f[0:32, :]).then_inc(t("m_step"), 1)
                        dve.wait_ge(t("m_step"), MS * g + at0 + 3)
                        nc.vector.tensor_tensor(m_parts[0:32, 2, :], m_f[0:32, :], m_parts[0:32, 1, :], ALU.subtract)\
                            .then_inc(t("m_parts"), 1)
                        use += 1
                    elif e[0] == "ON":
                        g2 = (2 * i + s) * 2 + e[1]
                        dve.wait_ge(t("t_ps"), t0 + use + 1)
                        sums = bank[7][:, :].rearrange("p (n w) -> p n w", w=32)
                        nc.vector.reciprocal(orec, sums[:, :, HD]).then_inc(t("rec"), 1)
                        dve.wait_ge(t("rec"), g2 + 1)
                        dst = o_tok[:, ds(i * (TPB * 64) + s * (2 * NB * TPB * 64) + e[1] * 256, 256)]
                        nc.vector.tensor_tensor(dst.rearrange("p (n w) -> p n w", w=HD), sums[:, :, 0:HD],
                                                orec.unsqueeze(2).to_broadcast([P, 16, HD]), ALU.mult)\
                            .then_inc(t("t_read"), 1)
                        use += 1

            MS = 5 if at.clip else 4

            def mld_before(g, i2, s2):
                return 48 * (i2 + 1) if s2 else 48 * i2

            def dve_prog(dve):
                dve.sem_inc(t("a_max"), 2)
                dve.sem_inc(t("o_sb"), 1)
                dve.sem_inc(t("clip"), 1)
                if at.clip:
                    dve.sem_inc(t("st_read"), 2)

                def prologue(dve):
                    for k in range(at.nu[0]):
                        dve_max(dve, 0, 0, k)
                    dve_events(dve, [("MS",)], None, None, 0, 0, 0)
                each_block((dve, dve_events, prologue))

            def pe_wrapped(pe):
                pe.sem_inc(t("pv"), 2)
                pe_prog(pe)

            stages.append((at.name, {"sp": sp_prog, "pool": pool_prog, "pe": pe_wrapped, "act": act_prog,
                                     "dve": dve_prog}))

        scratch = arena[:, route_base:route_base + 20 * NT * NX]

        def routing_stage(name, rows, soft_all, extra_sp=None):
            def t(n):
                return sem(f"route_{n}")

            def tile_of(n, k=NX):
                return scratch[:, n * NT * NX:n * NT * NX + NT * k].rearrange("p (t e) -> p t e", t=NT)

            lg, tmp, oh1, lg2, oh2, ex, pos, tot = (tile_of(n) for n in range(8))
            acc = scratch[:, 8 * 128:8 * 128 + (NT + 1) * NX].rearrange("p (t e) -> p t e", t=NT + 1)
            small = scratch[:, 10 * 128:11 * 128]
            m1, m2, mr, e2, den, rec, s1 = (small[:, n * NT:n * NT + NT] for n in range(7))
            few = scratch[:, 11 * 128:11 * 128 + 64]
            tiles_f, tiles_i, start, base = (few[:, n * 8:n * 8 + 8] for n in (0, 1, 2, 3))
            tiles_i = tiles_i.bitcast(I32)
            ohb = scratch[:, 12 * 128:12 * 128 + 64].bitcast(BF16)
            cmp = scratch[:, 13 * 128:13 * 128 + NTILE * (NX - 1)].rearrange("p (n e) -> p n e", n=NTILE)
            te_f = scratch[:, 16 * 128:16 * 128 + NTILE]

            def over_e(v):
                return v.unsqueeze(2).to_broadcast([P, NT, NX])

            def dve_prog(dve):
                done = [0]

                def then(ins):
                    done[0] += 1
                    ins.then_inc(t("step"), 1)
                    dve.wait_ge(t("step"), done[0])

                V = nc.vector
                for src, m, oh in ((lg, m1, oh1), (lg2, m2, oh2)):
                    then(V.tensor_reduce(m, src, AX.X, ALU.max))
                    then(V.tensor_tensor(tmp, src, over_e(m), ALU.is_equal))
                    then(V.tensor_tensor(tmp, tmp, expert_rank, ALU.mult))
                    then(V.tensor_reduce(mr, tmp, AX.X, ALU.max))
                    then(V.tensor_tensor(oh, expert_rank, over_e(mr), ALU.is_equal))
                    if oh is oh1:
                        then(V.scalar_tensor_tensor(out=lg2, in0=oh1, scalar=-3e38, in1=lg,
                                                    op0=ALU.mult, op1=ALU.add))
                V.tensor_tensor(ohb.rearrange("p (t e) -> p t e", t=NT), oh1, oh2, ALU.add).then_inc(t("oh"), 1)
                if soft_all:
                    V.tensor_tensor(ex, lg, over_e(m1), ALU.subtract).then_inc(t("ex_in"), 1)
                V.tensor_tensor(e2, m2, m1, ALU.subtract).then_inc(t("ex_in"), 1)
                dve.wait_ge(t("rank_ps"), 1)
                then(V.memset(acc[:, 0, :], 0.0))
                then(V.tensor_copy(tot.rearrange("p t e -> p (t e)"), bank[0][:, 0:P]))
                for n in range(NT):
                    then(V.tensor_tensor(acc[:, n + 1, :], acc[:, n, :], tot[:, n, :], ALU.add))
                then(V.tensor_scalar(tiles_i, acc[:, NT, :], float(P - 1), None, ALU.add))
                then(V.tensor_scalar(tiles_i, tiles_i, 7, None, ALU.arith_shift_right))
                then(V.tensor_copy(tiles_f, tiles_i))
                then(V.memset(start[:, 0:1], 0.0))
                for e in range(NX - 1):
                    then(V.tensor_tensor(start[:, e + 1:e + 2], start[:, e:e + 1], tiles_f[:, e:e + 1], ALU.add))
                then(V.tensor_scalar(base, start, float(P), None, ALU.mult))
                then(V.tensor_tensor(pos.rearrange("p t e -> p (t e)"), bank[0][:, P:2 * P],
                                     acc[:, 0:NT, :].rearrange("p t e -> p (t e)"), ALU.add))
                then(V.tensor_tensor(pos, pos, base.unsqueeze(1).to_broadcast([P, NT, NX]), ALU.add))
                for k, oh in enumerate((oh1, oh2)):
                    then(V.tensor_tensor(tmp, pos, oh, ALU.mult))
                    then(V.tensor_reduce(s1, tmp, AX.X, ALU.add))
                    then(V.tensor_copy(slot_i[:, k, :], s1))
                dve.sem_inc(t("slots"), 1)
                then(V.tensor_tensor(cmp, tile_no.unsqueeze(2).to_broadcast([P, NTILE, NX - 1]),
                                     start[:, 1:NX].unsqueeze(1).to_broadcast([P, NTILE, NX - 1]), ALU.is_ge))
                then(V.tensor_reduce(te_f, cmp, AX.X, ALU.add))
                then(V.tensor_copy(tile_expert, te_f))
                dve.wait_ge(t("ex_out"), 2 if soft_all else 1)
                if soft_all:
                    then(V.tensor_reduce(den, ex, AX.X, ALU.add))
                else:
                    then(V.tensor_scalar(den, e2, 1.0, None, ALU.add))
                then(V.reciprocal(gate_w[:, 0, :], den))
                then(V.tensor_tensor(gate_w[:, 1, :], gate_w[:, 0, :], e2, ALU.mult))

            def pe_prog(pe):
                pe.wait_ge(t("oh"), 1)
                nc.tensor.matmul(bank[0][:, 0:P], onesb, ohb, start=True, stop=True)
                nc.tensor.matmul(bank[0][:, P:2 * P], lower, ohb, start=True, stop=True).then_inc(t("rank_ps"), 1)

            def act_prog(act):
                for n, v in enumerate(([ex] if soft_all else []) + [e2]):
                    act.wait_ge(t("ex_in"), n + 1)
                    nc.scalar.activation(v, v, ACT.Exp).then_inc(t("ex_out"), 1)

            def pool_prog(pool):
                pool.wait_ge(t("slots"), 1)
                for k in range(2):
                    for n in range(NT):
                        nc.gpsimd.indirect_dma_start(
                            out=xs_scr, out_offset=bass.IndirectOffsetOnAxis(ap=slot_i[:, k, n:n + 1].bitcast(U32), axis=0),
                            in_=rows[:, n, :], in_offset=None).then_inc(sem(f"{name}_scattered"), 16)
                pool.wait_ge(sem(f"{name}_scattered"), 16 * 2 * NT)

            progs = {"dve": dve_prog, "pe": pe_prog, "act": act_prog, "pool": pool_prog}
            if extra_sp:
                progs["sp"] = extra_sp
            stages.append((name, progs))

        def expert_stage(name, gated, F, wu, w2, weights_wait):
            def t(n):
                return sem(f"experts_{n}")

            nf = (F + P - 1) // P
            fw = [min(P, F - n * P) for n in range(nf)]
            half = F // 2 if F > 512 else F
            nh = F // half
            at = [exp_base]

            def buf(n):
                at[0] += n
                return arena[:, at[0] - n:at[0]]

            xin = buf(2 * D).rearrange("p (s d) -> p s d", s=2)
            xT = buf(2 * D).rearrange("p (s c q) -> p s c q", s=2, c=DC)
            yo = buf(2 * D).rearrange("p (s d) -> p s d", s=2)
            gl, hs = buf(F), buf(F)
            hT = buf(2 * nf * P).rearrange("p (s n q) -> p s n q", s=2, n=nf)
            assert at[0] <= route_base
            h_ready = "h"

            def sp_load(sp, n, s):
                sp.dma_start(xin[:, s, :], xs_scr[ds(n * P, P), :]).then_inc(t(f"in{s}"), 16)

            def sp_store(sp, n, s):
                sp.wait_ge(t("y"), 1 + n + 1)
                sp.dma_start(ys_scr[ds(n * P, P), :], yo[:, s, :]).then_inc(t(f"st{s}"), 16)

            def sp_prog(sp):
                for s in range(2):
                    sp.sem_inc(t(f"st{s}"), 1)
                sp_load(sp, 0, 0)
                sp_load(sp, 1, 1)
                with sp.Fori(0, NTILE // 2 - 1) as i:
                    for s in range(2):
                        sp.wait_ge(t("xT_ps"), 2 * i + s + 1)
                        sp_load(sp, 2 * i + 2 + s, s)
                        sp_store(sp, 2 * i + s, s)
                sp_store(sp, NTILE - 2, 0)
                sp_store(sp, NTILE - 1, 1)
                for s in range(2):
                    sp.wait_ge(t(f"st{s}"), 1 + 16 * NTILE // 2)

            def pe_xt(pe, n, s, n2):
                pe.wait_ge(t(f"in{s}"), 16 * (n2 + 1))
                wait(pe, t("xT"), n)
                for c in range(DC):
                    last = nc.tensor.transpose(bank[6][:, c * P:c * P + P], xin[:, s, c * P:c * P + P], ident)
                last.then_inc(t("xT_ps"), 1)

            def pe_up(pe, n, s):
                e = pe.value_load(tile_expert[0:1, ds(n, 1)], min_val=0, max_val=NX - 1)
                pe.wait_ge(t("xT"), n + 1)
                wait(pe, t("g" if gated else h_ready), n)
                for w in range(2 if gated else 1):
                    if w == 1:
                        wait(pe, t(h_ready), n)
                    for hf in range(nh):
                        for c in range(DC):
                            last = nc.tensor.matmul(
                                bank[2 * w + hf][:, 0:half], xT[:, s, c, :],
                                wu[:, ds(e, 1), c, w, hf * half:hf * half + half].rearrange("p o f -> p (o f)"),
                                start=(c == 0), stop=(c == DC - 1))
                    last.then_inc(t("up"), 1)

            def pe_ht(pe, n):
                pe.wait_ge(t(h_ready), n + 1)
                wait(pe, t("hT"), n)
                for f in range(nf):
                    last = nc.tensor.transpose(bank[4 + f // 4][0:fw[f], (f % 4) * P:(f % 4) * P + P],
                                               hs[:, f * P:f * P + fw[f]], ident)
                last.then_inc(t("hT_ps"), 1)

            def pe_down(pe, n, s):
                e = pe.value_load(tile_expert[0:1, ds(n, 1)], min_val=0, max_val=NX - 1)
                pe.wait_ge(t("hT"), n + 1)
                wait(pe, t("y"), n, 1)
                for f in range(nf):
                    last = nc.tensor.matmul(bank[7][:, 0:D], hT[0:fw[f], s, f, :],
                                            w2[f][0:fw[f], ds(e, 1), :].rearrange("p o d -> p (o d)"),
                                            start=(f == 0), stop=(f == nf - 1))
                last.then_inc(t("y_ps"), 1)

            def pe_prog(pe):
                weights_wait(pe)
                pe.sem_inc(t("y_ps"), 1)
                pe_xt(pe, 0, 0, 0)
                pe_up(pe, 0, 0)
                pe_xt(pe, 1, 1, 0)
                pe_ht(pe, 0)
                with pe.Fori(0, NTILE // 2 - 1) as i:
                    pe_up(pe, 2 * i + 1, 1)
                    pe_xt(pe, 2 * i + 2, 0, i + 1)
                    pe_down(pe, 2 * i, 0)
                    pe_ht(pe, 2 * i + 1)
                    pe_up(pe, 2 * i + 2, 0)
                    pe_xt(pe, 2 * i + 3, 1, i + 1)
                    pe_down(pe, 2 * i + 1, 1)
                    pe_ht(pe, 2 * i + 2)
                pe_up(pe, NTILE - 1, 1)
                pe_down(pe, NTILE - 2, 0)
                pe_ht(pe, NTILE - 1)
                pe_down(pe, NTILE - 1, 1)

            up = 2 if gated else 1

            def act_xt(act, n, s):
                act.wait_ge(t("xT_ps"), n + 1)
                wait(act, t("up"), (n - 1) * up)
                nc.scalar.activation(xT[:, s, :, :].rearrange("p c q -> p (c q)"), bank[6][:, 0:D], ACT.Copy)\
                    .then_inc(t("xT"), 1)

            def act_hidden(act, n):
                act.wait_ge(t("up"), n * up + 1)
                if gated:
                    wait(act, t(h_ready), n)
                    nc.scalar.activation(gl.rearrange("p (h f) -> p h f", h=nh),
                                         psum[:, 0:1024].rearrange("p (h f) -> p h f", h=2)[:, :, 0:half],
                                         ACT.Gelu).then_inc(t("g"), 1)
                else:
                    wait(act, t("hT_ps"), n)
                    nc.scalar.activation(hs, bank[0][:, 0:F], ACT.Silu).then_inc(t(h_ready), 1)

            def act_out(act, n, s, n2):
                act.wait_ge(t("y_ps"), 1 + n + 1)
                wait(act, t(f"st{s}"), 16 * n2, 1)
                nc.scalar.activation(yo[:, s, :], bank[7][:, 0:D], ACT.Copy).then_inc(t("y"), 1)

            def act_prog(act):
                act.sem_inc(t("y"), 1)
                act_xt(act, 0, 0)
                act_hidden(act, 0)
                act_xt(act, 1, 1)
                with act.Fori(0, NTILE // 2 - 1) as i:
                    act_hidden(act, 2 * i + 1)
                    act_xt(act, 2 * i + 2, 0)
                    act_out(act, 2 * i, 0, i)
                    act_hidden(act, 2 * i + 2)
                    act_xt(act, 2 * i + 3, 1)
                    act_out(act, 2 * i + 1, 1, i)
                act_hidden(act, NTILE - 1)
                act_out(act, NTILE - 2, 0, NTILE // 2 - 1)
                act_out(act, NTILE - 1, 1, NTILE // 2 - 1)

            def dve_tile(dve, n, s):
                if gated:
                    dve.wait_ge(t("g"), n + 1)
                    dve.wait_ge(t("up"), n * up + 2)
                    wait(dve, t("hT_ps"), n)
                    nc.vector.tensor_tensor(hs.rearrange("p (h f) -> p h f", h=nh),
                                            gl.rearrange("p (h f) -> p h f", h=nh),
                                            psum[:, 1024:2048].rearrange("p (h f) -> p h f", h=2)[:, :, 0:half],
                                            ALU.mult).then_inc(t(h_ready), 1)
                dve.wait_ge(t("hT_ps"), n + 1)
                wait(dve, t("y_ps"), n - 1, 1)
                whole = F // P
                last = nc.vector.tensor_copy(hT[:, s, 0:whole, :].rearrange("p n q -> p (n q)"),
                                             psum[:, 2048:2048 + whole * P])
                if whole < nf:
                    last = nc.vector.tensor_copy(hT[0:fw[whole], s, whole, :],
                                                 psum[0:fw[whole], 2048 + whole * P:2048 + whole * P + P])
                last.then_inc(t("hT"), 1)

            def dve_prog(dve):
                dve_tile(dve, 0, 0)
                with dve.Fori(0, NTILE // 2 - 1) as i:
                    dve_tile(dve, 2 * i + 1, 1)
                    dve_tile(dve, 2 * i + 2, 0)
                dve_tile(dve, NTILE - 1, 1)

            stages.append((name, {"sp": sp_prog, "pe": pe_prog, "act": act_prog, "dve": dve_prog}))

        def gather_stage(name):
            def pool_prog(pool):
                for k in range(2):
                    for n in range(NT):
                        nc.gpsimd.indirect_dma_start(
                            out=gathered[:, k, n, :], out_offset=None, in_=ys_scr,
                            in_offset=bass.IndirectOffsetOnAxis(ap=slot_i[:, k, n:n + 1].bitcast(U32), axis=0))\
                            .then_inc(sem(f"{name}_gathered"), 16)
                pool.wait_ge(sem(f"{name}_gathered"), 16 * 2 * NT)
            stages.append((name, {"pool": pool_prog}))

        g = a.get
        W = {}
        v = weights(("mat", g("L0_attn_Wq")), ("mat", g("L0_attn_Wk")), ("mat", g("L0_attn_Wv")),
                    ("row", g("L0_attn_bv")), ("col", g("L0_attn_bq")), ("col", g("L0_attn_bk")))
        W["t0"] = dict(zip(("wq", "wk", "wv", "bv", "bq", "bk"), v))
        v = weights(("mat", g("L0_xattn_Wk")), ("mat", g("L0_xattn_Wv")), ("row", g("L0_xattn_bv")),
                    ("col", g("L0_xattn_bk")),
                    ("mat", g("L1_xattn_wk")), ("mat", g("L1_xattn_wv")), ("col", g("L1_xattn_bk")))
        w_ctx = [dict(zip(("wk", "wv", "bv", "bk"), v[0:4])), dict(zip(("wk", "wv", "bk"), v[4:7]))]
        bvx1 = floor_t.rearrange("p h q -> p (h q)")[:, 0:D]
        wdefs[-1].append((bvx1, g("L1_xattn_bv").partition_broadcast(P)))
        w_ctx[1]["bv"] = bvx1
        v = weights(("mat", g("L0_attn_Wf")), ("row", g("L0_attn_bf")), ("mat", g("L0_xattn_Wq")), ("col", g("L0_xattn_bq")))
        W["t1"] = dict(zip(("wo", "brow", "wq", "bq"), v))
        v = weights(("mat", g("L0_xattn_Wo")), ("row", g("L0_xattn_bo")), ("mat", g("L0_ffn_router_w")))
        W["t2"] = dict(zip(("wo", "brow", "router"), v))
        qkv = g("L1_attn_W_qkv")
        bqkv = g("L1_attn_b_qkv")
        v = weights(("mat", qkv[:, 0:D]), ("mat", qkv[:, D:2 * D]), ("mat", qkv[:, 2 * D:3 * D]),
                    ("row", bqkv[2 * D:3 * D]), ("col", bqkv[0:D]), ("col", bqkv[D:2 * D]), ("row", g("L0_ffn_bias")))
        W["t3"] = dict(zip(("wq", "wk", "wv", "bv", "bq", "bk", "brow"), v))
        v = weights(("mat", g("L1_attn_W_out")), ("row", g("L1_attn_b_out")), ("mat", g("L1_xattn_wq")), ("col", g("L1_xattn_bq")))
        W["t4"] = dict(zip(("wo", "brow", "wq", "bq"), v))
        v = weights(("mat", g("L1_xattn_wo")), ("row", g("L1_xattn_bo")), ("row", g("L1_ffn_g1")), ("mat", g("L1_ffn_Wq")),
                    ("mat", g("L1_ffn_Wdkv")), ("mat", g("L1_ffn_Wuk")), ("mat", g("L1_ffn_Wuv")))
        W["t5"] = dict(zip(("wo", "brow", "g1", "wq", "wdkv", "wuk", "wuv"), v))
        v = weights(("mat", g("L1_ffn_Wo")), ("row", g("L1_ffn_g2")), ("mat", g("L1_ffn_gate_w")))
        W["t6"] = dict(zip(("wo", "g2", "router"), v))

        logits = scratch[:, 0:NT * NX]
        wu0 = arena[:, att_base:att_base + NX * DC * 2 * F0].rearrange("p (e c w f) -> p e c w f", e=NX, c=DC, w=2)
        w2_0 = [w2_low[:, n * 2048:n * 2048 + 2048].rearrange("p (e d) -> p e d", e=NX) for n in range(4)] + \
               [w2_high[:, n * 2048:n * 2048 + 2048].rearrange("p (e d) -> p e d", e=NX) for n in range(2)]
        nw1 = NX * DC * F1
        wu1 = arena[:, att_base:att_base + nw1].rearrange("p (e c w f) -> p e c w f", e=NX, c=DC, w=1)
        w2_1 = [arena[:, att_base + nw1 + n * 2048:att_base + nw1 + n * 2048 + 2048]
                .rearrange("p (e d) -> p e d", e=NX) for n in range(4)]
        assert att_base + nw1 + 8192 <= v_base

        def up_weights0(sp):
            for e in range(NX):
                for w, src in enumerate((g("L0_ffn_w1"), g("L0_ffn_v1"))):
                    sp.dma_start(wu0[:, e, :, w, :], src[e].rearrange("(c p) f -> p c f", p=P)).then_inc(sem("up0"), 16)
            down_weights0(sp, (4, 5))

        def down_weights0(sp, chunks):
            for n in chunks:
                r = min(P, F0 - n * P)
                sp.dma_start(w2_0[n][0:r, :, :], g("L0_ffn_w2")[:, n * P:n * P + r, :].rearrange("e p d -> p e d"))\
                    .then_inc(sem("down0"), 16)

        def weights1(sp):
            for e in range(NX):
                sp.dma_start(wu1[:, e, :, 0, :], g("L1_ffn_w1")[e].rearrange("(c p) f -> p c f", p=P))\
                    .then_inc(sem("up1"), 16)
            for n in range(4):
                sp.dma_start(w2_1[n], g("L1_ffn_w2")[:, n * P:n * P + P, :].rearrange("e p d -> p e d"))\
                    .then_inc(sem("down1"), 16)

        def weights0_wait(pe):
            pe.wait_ge(sem("up0"), 16 * 2 * NX)
            pe.wait_ge(sem("down0"), 16 * 6)

        def weights1_wait(pe):
            pe.wait_ge(sem("up1"), 16 * NX)
            pe.wait_ge(sem("down1"), 16 * 4)

        w = W["t0"]
        token_stage("t0", 0, "x", False, None,
                    [("qk", w["wq"], w["bq"], QSCALE, q_scr), ("qk", w["wk"], w["bk"], 1.0, k_scr),
                     ("v", w["wv"], w["bv"])], w)
        context_stage("ctx", 1, 2)
        attention_stage(Attention("at0", ("fwd", "bwd"), S, True, False, q_scr, k_scr, None))
        w = W["t1"]
        token_stage("t1", 2, "proj", True, None, [("qk", w["wq"], w["bq"], QSCALE, q_scr)], w)
        attention_stage(Attention("xa0", ("full", "full"), SC, False, True, q_scr, kx_scr[0], vx_scr[0]))
        w = W["t2"]
        token_stage("t2", 3, "proj", True, None, [("logits", w["router"], logits)], w, extra_sp=up_weights0)
        routing_stage("rt0", x_tok, True, lambda sp: down_weights0(sp, (0, 1, 2, 3)))
        expert_stage("ex0", True, F0, wu0, w2_0, weights0_wait)
        gather_stage("ga0")
        w = W["t3"]
        token_stage("t3", 4, "comb", True, None,
                    [("qk", w["wq"], w["bq"], QSCALE, q_scr), ("qk", w["wk"], w["bk"], 1.0, k_scr),
                     ("v", w["wv"], w["bv"])], w)
        attention_stage(Attention("at1", ("full", "full"), S, False, False, q_scr, k_scr, None))
        w = W["t4"]
        token_stage("t4", 5, "proj", True, None, [("qk", w["wq"], w["bq"], QSCALE, q_scr)], w)
        attention_stage(Attention("xa1", ("full", "full"), SC, False, False, q_scr, kx_scr[1], vx_scr[1]))
        w = W["t5"]
        token_stage("t5", 6, "proj", True, w["g1"],
                    [("latent", w["wdkv"]), ("qk", w["wq"], None, QSCALE, q_scr), ("klat", w["wuk"], k_scr),
                     ("vlat", w["wuv"])], w)
        attention_stage(Attention("mla", ("causal", "causal"), S, False, False, q_scr, k_scr, None))
        w = W["t6"]
        token_stage("t6", 7, "proj", False, w["g2"], [("logits", w["router"], logits)], w, x_out="add", rows_out=True,
                    extra_sp=weights1)
        routing_stage("rt1", v_tok.rearrange("p (t d) -> p t d", t=NT), False)
        expert_stage("ex1", False, F1, wu1, w2_1, weights1_wait)
        gather_stage("ga1")
        token_stage("t7", None, "comb", True, None, [], {}, x_out=False, final=True)

        family = {"t": "tok_", "c": "ctx_", "a": "att_", "x": "att_", "m": "att_", "r": "route_", "e": "experts_"}

        def run(eng, key):
            for n, (name, progs) in enumerate(stages):
                if n:
                    eng.wait_ge(stage_done, 5 * n)
                    if key == "pool":
                        kind = family.get(stages[n - 1][0][0])
                        for other, handle in sems.items():
                            if kind and other.startswith(kind):
                                eng.sem_clear(handle)
                if key in progs:
                    progs[key](eng)
                if n + 1 < len(stages):
                    eng.drain().then_inc(stage_done, 1)

        block = stack.enter_context(nc.Block())

        @block.sync
        def _(sp):
            run(sp, "sp")

        @block.tensor
        def _(pe):
            run(pe, "pe")

        @block.scalar
        def _(act):
            run(act, "act")

        @block.vector
        def _(dve):
            run(dve, "dve")

        @block.gpsimd
        def _(pool):
            run(pool, "pool")


NAMES = ['L0_attn_Wq', 'L0_attn_bq', 'L0_attn_Wk', 'L0_attn_bk', 'L0_attn_Wv', 'L0_attn_bv', 'L0_attn_Wf', 'L0_attn_bf',
         'L0_xattn_Wq', 'L0_xattn_bq', 'L0_xattn_Wk', 'L0_xattn_bk', 'L0_xattn_Wv', 'L0_xattn_bv', 'L0_xattn_Wo',
         'L0_xattn_bo', 'L0_ffn_router_w', 'L0_ffn_w1', 'L0_ffn_v1', 'L0_ffn_w2', 'L0_ffn_bias', 'L1_attn_W_qkv',
         'L1_attn_b_qkv', 'L1_attn_W_out', 'L1_attn_b_out', 'L1_xattn_wq', 'L1_xattn_bq', 'L1_xattn_wk', 'L1_xattn_bk',
         'L1_xattn_wv', 'L1_xattn_bv', 'L1_xattn_wo', 'L1_xattn_bo', 'L1_ffn_g1', 'L1_ffn_Wq', 'L1_ffn_Wdkv',
         'L1_ffn_Wuk', 'L1_ffn_Wuv', 'L1_ffn_Wo', 'L1_ffn_g2', 'L1_ffn_gate_w', 'L1_ffn_w1', 'L1_ffn_w2']


def alibi_rows():
    bf = mybir.dt.np(BF16)
    half = H // 2
    slopes = 1.0 / (24.0 ** (1.0 / half)) ** np.arange(1, half + 1)
    rows = np.ones((2, 2, 2 * NB, 6, HG, S), bf)
    for slot in range(2):
        for i in range(2 * NB):
            for h in range(HG):
                value = slopes[HG * (i // NB) + h] * np.arange(S) * (-1.0 if slot else 1.0)
                for side, sign, at in ((0, -1.0, 0), (1, 1.0, 3)):
                    rest = sign * value
                    for n in range(3):
                        rows[side, slot, i, at + n, h] = rest.astype(bf)
                        rest = rest - rows[side, slot, i, at + n, h].astype(np.float64)
    return rows


def kernel(**inputs):
    import concourse.bacc as bacc
    from concourse.bass_utils import run_bass_kernel_spmd

    nc = bacc.Bacc("TRN2", target_bir_lowering=False, num_devices=1)
    x = np.asarray(inputs["x"])
    ctx = np.asarray(inputs["ctx_768"])
    arrays = {"x": x, "xT": np.ascontiguousarray(x.reshape(T, D).T),
              "ctxT": np.ascontiguousarray(ctx.reshape(NB * SC, CW).T),
              "alibi": alibi_rows(), "ones": np.ones((3, HG, S), mybir.dt.np(BF16))}
    for name in NAMES:
        arrays[name] = np.ascontiguousarray(inputs[name])
    aps = {name: nc.dram_tensor(f"in_{name}", v.shape, mybir.dt.from_np(v.dtype), kind="ExternalInput").ap()
           for name, v in arrays.items()}
    out = nc.dram_tensor("out", (NB, S, D), F32, kind="ExternalOutput").ap()
    build_decoder(nc, aps, out)
    r = run_bass_kernel_spmd(nc, [{f"in_{name}": v for name, v in arrays.items()}], core_ids=[0])
    return r.results[0]["out"]
```

```python
from contextlib import ExitStack

import numpy as np

import concourse.bass as bass
from concourse import mybir

F32 = mybir.dt.float32
BF16 = mybir.dt.bfloat16
I32 = mybir.dt.int32
U32 = mybir.dt.uint32
ACT = mybir.ActivationFunctionType
ALU = mybir.AluOpType
AX = mybir.AxisListType
ds = bass.ds

P = 128
NB, S, D = 2, 1024, 256
T = NB * S
NT = T // P
TPB = S // P
DC = D // P
H, HD = 16, 16
HG = 4
SC, CW = 154, 192
NX = 8
F0, F1 = 704, 512
NTILE = 2 * T // P + NX
NSLOT = NTILE * P
QSCALE = 1.0 / float(np.sqrt(HD))
NEG = -1e30
CLAMP = 10000.0
PART_Q = (0, 1, 2, 0, 1, 0)
PART_K = (0, 0, 0, 1, 1, 2)
STK = 16 * len(PART_Q)
FIRST_MAX = 2


def wait(eng, sem, value, start=0):
    if isinstance(value, int) and value <= 0:
        return
    eng.wait_ge(sem, start + value)


def hold(eng, sem, value, marker):
    eng.wait_ge(sem, value)
    eng.sem_inc(marker, 1)


def attention_units(mode, keys):
    units = []
    for qb in range(TPB):
        if keys < S:
            units.append((qb, (0, 1, 2, 3), 0, keys))
            continue
        lo = qb * P if mode == "bwd" else 0
        hi = (qb + 1) * P if mode in ("fwd", "causal") else keys
        if hi - lo <= 512:
            units += [(qb, (0, 1), lo, hi - lo), (qb, (2, 3), lo, hi - lo)]
        else:
            units += [(qb, (h,), lo, hi - lo) for h in range(HG)]
    return units


def attention_steps(mode, keys):
    steps = []
    for qh in range(2):
        n_blocks = -(-keys // P)
        size = -(-keys // n_blocks)
        blocks = range(n_blocks)
        if mode == "bwd":
            blocks = [b for b in reversed(blocks) if b >= 4 * qh]
        elif mode in ("fwd", "causal"):
            blocks = [b for b in blocks if b < 4 * qh + 4]
        blocks = list(blocks)
        for kb in blocks:
            c0, c1, diag = 0, 512, None
            d = kb - 4 * qh
            if mode in ("fwd", "causal") and d >= 0:
                c0, diag = d * P, d * P
            if mode == "bwd" and d < 4:
                c1, diag = (d + 1) * P, d * P
            steps.append((qh, kb, min(size, keys - kb * size), c0, c1, diag, kb == blocks[0], kb == blocks[-1]))
    return steps


def block_events(n_steps, half_end, n_units, first, lag, before):
    events, given, copied = [], 0, None
    span = max(1, n_steps - 2 - first)

    def values(k):
        nonlocal copied
        old, k = k < lag, (before if k < lag else 0) + k - lag
        if k < 0:
            return
        events.append(("PV", k, old))
        if old and k == before - 1:
            events.append(("OC", 1, old))
            copied = (1, old)
        elif not old and k == half_end:
            events.append(("OC", 0, old))
            copied = (0, old)

    for k in range(n_steps):
        due = min(n_units, -(-n_units * max(0, k + 1 - first) // span))
        units = [("A", u) for u in range(given, due)]
        given = due
        early = (len(units) + 1) // 2
        if k == 0:
            values(k)
        events += [("ST", k, 0)] + units[0:1] + [("ST", k, 1)] + units[1:early]
        if n_units and k == n_steps - 2:
            events += [("MT",), ("MS",)]
        if k > 0:
            values(k)
        units = units[early:]
        events += [("ST", k, 2)] + units[0:1] + [("ST", k, 3), ("CL", k)]
        if copied is not None:
            events += [("OT",) + copied] + units[1:] + [("ON",) + copied]
            copied = None
        else:
            events += units[1:]
    assert given == n_units
    return events


class Attention:

    def __init__(self, name, modes, keys, alibi, clip, q_scr, k_scr, vx):
        self.name, self.modes, self.keys = name, modes, keys
        self.alibi, self.clip = alibi, clip
        self.q_scr, self.k_scr, self.vx = q_scr, k_scr, vx
        self.kblocks = (keys + P - 1) // P
        self.kb_size = -(-keys // self.kblocks)
        self.mrow = STK + (6 if alibi else 0)
        self.units = [attention_units(m, keys) for m in modes]
        self.steps = [attention_steps(m, keys) for m in modes]
        self.nu = [len(u) for u in self.units]
        self.ns = [len(s) for s in self.steps]
        self.n_prob = 4
        self.lag = 2
        self.events = []
        for slot in range(2):
            ends = {k: s[0] for k, s in enumerate(self.steps[slot]) if s[7] and k + 1 < self.ns[slot]}
            (half_end,) = ends
            first = FIRST_MAX if keys == S else 0
            self.events.append([block_events(self.ns[slot], half_end, n, first, self.lag, before)
                                for n, before in ((self.nu[1 - slot], self.ns[1 - slot]), (0, self.ns[1 - slot]),
                                                  (self.nu[1 - slot], 0))])
        self.last = [("PV", self.ns[1] - n, True) for n in range(self.lag, 0, -1)] + \
                    [("OC", 1, True), ("OT", 1, True), ("ON", 1, True)]
        self.loads = 9 + (2 if alibi else 0)

    def part(self, slot, k):
        return (k + (self.ns[0] if slot else 0)) % self.n_prob

    def unit(self, slot, i, k):
        return i * (self.nu[0] + self.nu[1]) + (self.nu[0] if slot else 0) + k

    def step(self, slot, i, k):
        return i * (self.ns[0] + self.ns[1]) + (self.ns[0] if slot else 0) + k


def build_decoder(nc, a, out):
    stack = ExitStack()
    with stack:
        words = 52900
        arena = stack.enter_context(nc.sbuf_tensor("arena", [P, words], F32))
        psum = stack.enter_context(nc.psum_tensor("psum", [P, 8 * 512], F32))
        bank = [psum[:, 512 * n:512 * n + 512] for n in range(8)]
        sems = {}

        def sem(name):
            if name not in sems:
                sems[name] = stack.enter_context(nc.semaphore(name))
            return sems[name]

        top = [0]

        def take(n):
            top[0] += n
            assert top[0] <= words, top[0]
            return arena[:, top[0] - n:top[0]]

        x_tok = take(NT * D).rearrange("p (t d) -> p t d", t=NT)
        ident = take(P)
        identb = take(P // 2).bitcast(BF16)
        mask_right = take(P // 2).bitcast(BF16)
        mask_left = take(P // 2).bitcast(BF16)
        lower = take(P // 2).bitcast(BF16)
        onesb = take(P // 2).bitcast(BF16)
        pick_max = take(P // 2).bitcast(BF16)
        minus_clamp = take(1)
        halves = take(16)
        expert_rank = take(NT * NX).rearrange("p (t e) -> p t e", t=NT)
        slot_i = take(2 * NT).bitcast(I32).rearrange("p (k t) -> p k t", k=2)
        gate_w = take(2 * NT).rearrange("p (k t) -> p k t", k=2)
        tile_expert = take(NTILE).bitcast(I32)
        tile_no = take(NTILE)
        wslots = [take(2576) for _ in range(2)]
        tok_base = top[0]
        o_tok = take(NT * D)
        ats_base = top[0]
        ats = take(TPB * D).rearrange("p (t d) -> p t d", t=TPB)
        att = take(TPB * D).rearrange("p (t c q) -> p t c q", t=TPB, c=DC)
        w2_low = arena[:, tok_base:top[0]]
        r_tok = take(TPB * D).rearrange("p (t d) -> p t d", t=TPB)
        xts_flat = take(DC * S)
        xts = xts_flat.rearrange("p (c t) -> p c t", c=DC)
        xb_base = top[0]
        xb = take(2 * 512).rearrange("p (s t d) -> p s t d", s=2, t=2)
        exp_base = top[0] - TPB * D - DC * S - 2 * 512
        route_base = top[0]
        u_f = take(2 * 512).rearrange("p (s t) -> p s t", s=2)
        parts = take(2 * 768).bitcast(BF16).rearrange("p (s k t) -> p s k t", s=2, k=3)
        mv = take(TPB * 2 * 2).rearrange("p (n t k) -> p n t k", n=2, t=TPB)
        bst = take(TPB * 2 * 6).rearrange("p (n t k) -> p n t k", n=2, t=TPB)
        rstd = take(TPB * 2).rearrange("p (n t) -> p n t", n=2)
        ptmp = take(4)
        h_tok = ats
        lat = att.rearrange("p t c q -> p (t c q)")[:, 0:S]
        w2_high = take(2 * NX * D)
        att_base = top[0]
        stk = [[take(HG * S // 2).bitcast(BF16).rearrange("p (h t) -> p h t", h=HG) for _ in range(2)]
               for _ in range(2)]
        prob = take(2 * HG * 512).rearrange("p (s h q) -> p s h q", s=2, h=HG)
        v_st = [take(TPB * HG * 32).rearrange("p (k h w) -> p k h w", k=TPB, h=HG) for _ in range(2)]
        stack_words = HG * S // 2
        floor_t = take(HG * 512).rearrange("p (h q) -> p h q", h=HG)
        clipped = take(2 * 512).rearrange("p (s q) -> p s q", s=2)
        o_sb = take(512)
        mstat = take(2 * 32).rearrange("p (s m) -> p s m", s=2)
        m_f = take(P)
        m_parts = take(3 * P // 2).bitcast(BF16).rearrange("p (k q) -> p k q", k=3)
        orec = take(16)
        v_base = top[0]
        v_tok = take(NT * D)
        q_all = [arena[:, at0:at0 + 4 * stack_words].bitcast(BF16).rearrange("p (i h t) -> p i h t", i=2 * NB, h=HG)
                 for at0 in (att_base, ats_base)]
        assert ats_base + 4 * stack_words <= top[0] and 4 * stack_words == 4 * TPB * D
        kx_words = 2 * NB * HG * SC // 2
        k_all = [v_tok[:, 1024 + n * kx_words:1024 + (n + 1) * kx_words].bitcast(BF16)
                 .rearrange("p (i h t) -> p i h t", i=2 * NB, h=HG) for n in range(2)]
        wu_all = arena[:, att_base:att_base + NX * DC * 2 * F0]
        assert att_base + NX * DC * 2 * F0 <= words
        gathered = arena[:, att_base:att_base + 2 * NT * D].rearrange("p (k t d) -> p k t d", k=2, t=NT)

        scr = {}

        def dram(name, shape, dt=F32):
            return nc.dram_tensor(name, shape, dt, kind="Internal").ap()

        q_scr = dram("q_parts", (2, 2, NB, 3 * 64, S), BF16)
        k_scr = dram("k_parts", (2, 2, NB, 3 * 64, S), BF16)
        kx_scr = [dram(f"kx_parts{n}", (2, 2, NB, 3 * 64, SC), BF16) for n in range(2)]
        vx_scr = [dram(f"vx{n}", (P, 4 * 4 * 64)) for n in range(2)]
        xs_scr = dram("slot_rows", (NSLOT, D))
        ys_scr = dram("slot_out", (NSLOT, D))

        stage_done = sem("stage_done")
        stages = []

        def weight_slot(n):
            w = wslots[n % 2]
            return w

        wdefs = []

        def weights(*items):
            w, at, views, loads = wslots[len(wdefs) % 2], 0, [], []
            for kind, src in items:
                if kind == "mat":
                    rows, cols = src.shape
                    c = (rows + P - 1) // P
                    v = w[:, at:at + c * cols].rearrange("p (c n) -> p c n", c=c)
                    at += c * cols
                    if rows % P:
                        for k in range(c):
                            n = min(P, rows - k * P)
                            loads.append((v[0:n, k, :], src[k * P:k * P + n, :]))
                    else:
                        loads.append((v, src.rearrange("(c p) n -> p c n", p=P)))
                elif kind == "row":
                    v = w[:, at:at + D]
                    at += D
                    loads.append((v, src.partition_broadcast(P)))
                else:
                    v = w[:, at:at + DC]
                    at += DC
                    loads.append((v, src.rearrange("(c p) -> p c", p=P)))
                views.append(v)
            assert at <= 2576, at
            wdefs.append(loads)
            return views

        def load_weights(sp, n):
            if n < len(wdefs):
                for dst, src in wdefs[n]:
                    sp.dma_start(dst, src, allow_slow_non_contiguous=True).then_inc(sem(f"weights{n}"), 16)

        def weights_ready(eng, n):
            eng.wait_ge(sem(f"weights{n}"), 16 * len(wdefs[n]))

        def setup_pool(pool):
            c0 = sem("const_base")
            nc.gpsimd.memset(ident, 0.0)
            nc.gpsimd.memset(lower, 1.0)
            nc.gpsimd.memset(onesb, 1.0)
            nc.gpsimd.memset(halves, -0.5)
            nc.gpsimd.memset(pick_max, 0.0)
            nc.gpsimd.memset(minus_clamp, -CLAMP)
            nc.gpsimd.memset(mask_right, 0.0)
            nc.gpsimd.memset(mask_left, 0.0)
            nc.gpsimd.iota(tile_no.bitcast(I32), pattern=[[1, NTILE]], base=0, channel_multiplier=0)
            for e in range(NX):
                nc.gpsimd.memset(expert_rank[:, :, e:e + 1], float(NX - e))
            nc.gpsimd.memset(xts_flat, 0.0).then_inc(c0, 1)
            pool.wait_ge(c0, 1)
            nc.gpsimd.affine_select(out=ident, in_=ident, compare_op=ALU.not_equal, fill=1.0,
                                    base=0, pattern=[[-1, P]], channel_multiplier=1)
            nc.gpsimd.affine_select(out=lower, in_=lower, compare_op=ALU.is_gt, fill=0.0,
                                    base=0, pattern=[[1, P]], channel_multiplier=-1)
            nc.gpsimd.affine_select(out=mask_right, in_=mask_right, compare_op=ALU.is_ge, fill=NEG,
                                    base=0, pattern=[[-1, P]], channel_multiplier=1)
            nc.gpsimd.affine_select(out=mask_left, in_=mask_left, compare_op=ALU.is_ge, fill=NEG,
                                    base=0, pattern=[[1, P]], channel_multiplier=-1)\
                .then_inc(c0, 1)
            pool.wait_ge(c0, 2)
            nc.gpsimd.memset(pick_max[STK:STK + 3, :], 1.0).then_inc(c0, 1)
            pool.wait_ge(c0, 3)
            nc.gpsimd.tensor_copy(identb, ident)
            nc.gpsimd.tensor_copy(tile_no, tile_no.bitcast(I32)).then_inc(c0, 1)

        def setup_sp(sp):
            load_weights(sp, 0)
            load_weights(sp, 1)
            sp.dma_start(x_tok, a["x"].rearrange("b (t p) d -> p (b t) d", p=P)).then_inc(sem("x_loaded"), 16)
            sp.wait_ge(sem("const_base"), 1)
            rows = NSLOT // TPB
            for n in range(TPB):
                sp.dma_start(xs_scr[n * rows:(n + 1) * rows, :].rearrange("(p r) d -> p (r d)", p=P),
                             xts_flat[:, 0:rows * D // P]).then_inc(sem("slots_zeroed"), 16)
            sp.wait_ge(sem("slots_zeroed"), 16 * TPB)
            sp.wait_ge(sem("x_loaded"), 16)

        stages.append(("setup", {"pool": setup_pool, "sp": setup_sp}))

        def token_stage(name, wn, source, norm, rms, outs, w, x_out=True, rows_out=False, final=False,
                        extra_sp=None):
            def t(n):
                return sem(f"tok_{n}")

            wo, brow = w.get("wo"), w.get("brow")
            work = []
            for o in outs:
                if o[0] == "latent":
                    work += [("latent", o, None, half) for half in range(2)]
                elif o[0] in ("qk", "klat"):
                    work += [(o[0], o, f, half) for f in range(2) for half in range(2)]
                elif o[0] in ("v", "vlat"):
                    work += [(o[0], o, None, p) for p in range(TPB // 2)]
                elif o[0] == "logits":
                    work += [("logits", o, None, p) for p in range(2)]
            nw = len(work)
            assert nw % 2 == 0
            nqk = sum(k in ("qk", "klat") for k, *_ in work)
            qk_no = {}
            for k, (kind, *_) in enumerate(work):
                if kind in ("qk", "klat"):
                    qk_no[k] = len(qk_no)
            scratch_use = [sum(1 for n in qk_no.values() if n % 2 == s) for s in range(2)]
            lats = [k for k, x in enumerate(work) if x[0] == "latent"]
            tr_src = h_tok if rms is not None else r_tok
            npool = 2 + (4 if rms is not None else 0)
            n_pairs = TPB // 2
            has_in = source != "x"
            norm_pairs = norm

            def sp_prog(sp):
                for n in ("scr0", "scr1", "out"):
                    sp.sem_inc(t(n), 1)
                if wn is not None:
                    load_weights(sp, wn + 1)
                if extra_sp:
                    extra_sp(sp)
                with sp.Fori(0, NB) as b:
                    if source == "x":
                        wait(sp, t("work_ps"), b * nw, 1)
                        sp.dma_start(xts, a["xT"][:, ds(b * S, S)].rearrange("(c p) t -> p c t", p=P))\
                            .then_inc(t("xt_in"), 16)
                    for k, n in qk_no.items():
                        kind, o, f, half = work[k]
                        sp.wait_ge(t("third"), 2 + b * nqk + n + 1)
                        dst = o[-1]
                        for j in range(2):
                            sp.dma_start(
                                dst[f, j, ds(b, 1), :, half * 512:half * 512 + 512]
                                .rearrange("o (k r) t -> r (o k) t", k=3),
                                parts[j * 64:j * 64 + 64, n % 2, :, :]).then_inc(t(f"scr{n % 2}"), 16)
                    if final:
                        for p in range(n_pairs):
                            sp.wait_ge(t("xs"), b * TPB + 2 * p + 2)
                            sp.dma_start(out[ds(b, 1), p * 256:p * 256 + 256, :]
                                         .rearrange("o (t p) d -> p (o t) d", p=P),
                                         r_tok[:, 2 * p:2 * p + 2, :]).then_inc(t("out"), 16)
                for s in range(2):
                    wait(sp, t(f"scr{s}"), 32 * NB * scratch_use[s], 1)
                if final:
                    sp.wait_ge(t("out"), 1 + 16 * NB * n_pairs)

            def pool_prog(pool):
                if brow is not None:
                    weights_ready(pool, wn)
                with pool.Fori(0, NB) as b:
                    if source == "proj":
                        hold(pool, t("tra_ps"), 1 + b * n_pairs, t("held_pool"))
                        if rms is not None:
                            hold(pool, t("trx_ps"), 1 + b * n_pairs, t("held_pool"))
                            if rows_out:
                                hold(pool, t("pool_x"), 1 + b * 2 * n_pairs, t("held_pool"))
                        for u in range(TPB):
                            nc.gpsimd.tensor_copy(
                                ats[:, u, :].rearrange("p (g w) -> p g w", g=4),
                                o_tok.rearrange("p (g n) -> p g n", g=4)[:, :, ds(b * (TPB * 64) + u * 64, 64)])\
                                .then_inc(t("ats"), 1)
                    if has_in:
                        for p in range(n_pairs):
                            pool.wait_ge(t("r"), 2 + b * n_pairs + p - 1)
                            src = x_tok[:, ds(b * TPB + 2 * p, 2), :]
                            if brow is not None:
                                nc.gpsimd.tensor_tensor(xb[:, p % 2, :, :], src,
                                                        brow.unsqueeze(1).to_broadcast([P, 2, D]), ALU.add)\
                                    .then_inc(t("xb"), 1)
                            else:
                                nc.gpsimd.tensor_copy(xb[:, p % 2, :, :], src).then_inc(t("xb"), 1)
                            if p >= 1:
                                pool_norm(pool, b, p - 1)
                        pool_norm(pool, b, n_pairs - 1)
                        if rms is not None:
                            for p in range(n_pairs):
                                pool_rms(pool, b, p)
                        for p in range(n_pairs):
                            if x_out:
                                if norm:
                                    hold(pool, t("xs"), b * TPB + 2 * p + 2, t("held_pool"))
                                else:
                                    hold(pool, t("r"), 2 + b * n_pairs + p + 1, t("held_pool"))
                                xp = x_tok[:, ds(b * TPB + 2 * p, 2), :]
                                if x_out == "add":
                                    nc.gpsimd.tensor_tensor(xp, xp, r_tok[:, 2 * p:2 * p + 2, :], ALU.add)\
                                        .then_inc(t("pool_x"), 1)
                                else:
                                    nc.gpsimd.tensor_copy(xp, r_tok[:, 2 * p:2 * p + 2, :])\
                                        .then_inc(t("pool_x"), 1)
                            if rows_out:
                                hold(pool, t("h"), b * TPB + 2 * p + 2, t("held_pool"))
                                nc.gpsimd.tensor_copy(
                                    v_tok.rearrange("p (t d) -> p t d", t=NT)[:, ds(b * TPB + 2 * p, 2), :],
                                    h_tok[:, 2 * p:2 * p + 2, :]).then_inc(t("pool_x"), 1)
                    for k, n in qk_no.items():
                        s = n % 2
                        pool.wait_ge(t("second"), b * nqk + n + 1)
                        nc.gpsimd.tensor_tensor(parts[:, s, 2, :], u_f[:, s, :], parts[:, s, 1, :],
                                                ALU.subtract).then_inc(t("third"), 1)

            def pool_norm(pool, b, p):
                if not norm:
                    return
                hold(pool, t("mv"), b * TPB + 2 * p + 2, t("held_pool"))
                nc.gpsimd.tensor_scalar(rstd[:, 0, 2 * p:2 * p + 2], mv[:, 0, 2 * p:2 * p + 2, 1], 1e-5, None,
                                        ALU.add).then_inc(t("pool_n"), 1)
                pool.wait_ge(t("pool_n"), b * 2 * n_pairs + 2 * p + 1)
                nc.gpsimd.tensor_tensor(rstd[:, 0, 2 * p:2 * p + 2], rstd[:, 0, 2 * p:2 * p + 2],
                                        halves[:, 0:2], ALU.pow).then_inc(t("pool_n"), 1)

            def pool_rms(pool, b, p):
                sl = slice(2 * p, 2 * p + 2)
                base = b * 4 * n_pairs + 4 * p
                pool.wait_ge(t("mv2"), b * TPB + 2 * p + 2)
                nc.gpsimd.tensor_tensor(rstd[:, 1, sl], mv[:, 1, sl, 0], mv[:, 1, sl, 0], ALU.mult)\
                    .then_inc(t("pool_r"), 1)
                pool.wait_ge(t("pool_r"), base + 1)
                nc.gpsimd.tensor_tensor(rstd[:, 1, sl], rstd[:, 1, sl], mv[:, 1, sl, 1], ALU.add)\
                    .then_inc(t("pool_r"), 1)
                hold(pool, t("pool_r"), base + 2, t("held_pool"))
                nc.gpsimd.tensor_scalar(rstd[:, 1, sl], rstd[:, 1, sl], 1e-6, None, ALU.add)\
                    .then_inc(t("pool_r"), 1)
                pool.wait_ge(t("pool_r"), base + 3)
                nc.gpsimd.tensor_tensor(rstd[:, 1, sl], rstd[:, 1, sl], halves[:, 0:2], ALU.pow)\
                    .then_inc(t("pool_r"), 1)

            def act_prog(act):
                act.sem_inc(t("att"), 2)
                act.sem_inc(t("xts"), 2)
                with act.Fori(0, NB) as b:
                    if source == "proj":
                        wait(act, t("prj_ps"), b * n_pairs, 1)
                        if lats:
                            wait(act, t("work_ps"), b * nw, 1)
                        for p in range(n_pairs):
                            act.wait_ge(t("tra_ps"), 1 + b * n_pairs + p + 1)
                            nc.scalar.activation(att[:, 2 * p:2 * p + 2, :, :].rearrange("p t c q -> p (t c q)"),
                                                 bank[p % 2][:, :], ACT.Copy).then_inc(t("att"), 1)
                    if has_in and nw:
                        wait(act, t("work_ps"), b * nw, 1)
                        for p in range(n_pairs):
                            act.wait_ge(t("trx_ps"), 1 + b * n_pairs + p + 1)
                            nc.scalar.activation(
                                xts[:, :, 256 * p:256 * p + 256].rearrange("p c (t q) -> p t c q", t=2),
                                bank[4 + p % 2][:, :].rearrange("p (t c q) -> p t c q", t=2, c=DC),
                                ACT.Copy).then_inc(t("xts"), 1)
                    if lats:
                        for k in lats:
                            act.wait_ge(t("work_ps"), 1 + b * nw + k + 1)
                            if k == lats[0]:
                                act.wait_ge(t("prj_ps"), 1 + (b + 1) * n_pairs)
                            half = work[k][3]
                            nc.scalar.activation(lat[:, half * 512:half * 512 + 512], bank[6 + k % 2][:, :],
                                                 ACT.Copy).then_inc(t("lat"), 1)
                    for k, n in qk_no.items():
                        s = n % 2
                        uses = (n - s) // 2
                        act.wait_ge(t("first_u"), b * nqk + n + 1)
                        wait(act, t(f"scr{s}"), (b * scratch_use[s] + uses) * 32, 1)
                        nc.scalar.activation(parts[:, s, 0, :], u_f[:, s, :], ACT.Copy).then_inc(t("first"), 1)
                        act.wait_ge(t("rest_u"), b * nqk + n + 1)
                        nc.scalar.activation(parts[:, s, 1, :], u_f[:, s, :], ACT.Copy).then_inc(t("second"), 1)

            def pe_prog(pe):
                for n in ("tra_ps", "prj_ps", "trx_ps", "work_ps"):
                    pe.sem_inc(t(n), 1)
                weights_ready(pe, wn)
                with pe.Fori(0, NB) as b:
                    def tra(p):
                        for u in (2 * p, 2 * p + 1):
                            if u == 2 * p:
                                pe.wait_ge(t("ats"), b * TPB + 2 * p + 2)
                                pe.wait_ge(t("att"), 2 + b * n_pairs + p - 1)
                            for c in range(DC):
                                at = (u % 2) * D + c * P
                                last = nc.tensor.transpose(bank[p % 2][:, at:at + P], ats[:, u, c * P:c * P + P],
                                                           ident)
                        last.then_inc(t("tra_ps"), 1)

                    def prj(p):
                        pe.wait_ge(t("att"), 2 + b * n_pairs + p + 1)
                        pe.wait_ge(t("r"), 2 + b * n_pairs + p - 1)
                        for u in (2 * p, 2 * p + 1):
                            for c in range(DC):
                                last = nc.tensor.matmul(bank[2 + p % 2][:, (u % 2) * D:(u % 2) * D + D],
                                                        att[:, u, c, :], wo[:, c, :],
                                                        start=(c == 0), stop=(c == DC - 1))
                        last.then_inc(t("prj_ps"), 1)

                    if source == "proj":
                        tra(0)
                        tra(1)
                        for p in range(n_pairs):
                            prj(p)
                            if p + 2 < n_pairs:
                                tra(p + 2)
                    if has_in and nw:
                        for p in range(n_pairs):
                            if rms is not None:
                                pe.wait_ge(t("h"), b * TPB + 2 * p + 2)
                            else:
                                pe.wait_ge(t("xs"), b * TPB + 2 * p + 2)
                            pe.wait_ge(t("xts"), 2 + b * n_pairs + p - 1)
                            for u in (2 * p, 2 * p + 1):
                                for c in range(DC):
                                    at = (u % 2) * D + c * P
                                    last = nc.tensor.transpose(bank[4 + p % 2][:, at:at + P],
                                                               tr_src[:, u, c * P:c * P + P], ident)
                            last.then_inc(t("trx_ps"), 1)
                    if nw:
                        if has_in:
                            pe.wait_ge(t("xts"), 2 + (b + 1) * n_pairs)
                        else:
                            pe.wait_ge(t("xt_in"), 16 * (b + 1))
                        for k, (kind, o, f, half) in enumerate(work):
                            pe.wait_ge(t("work_free"), 2 + b * nw + k - 1)
                            ps = bank[6 + k % 2]
                            mat = o[1]
                            if kind == "qk":
                                for c in range(DC):
                                    last = nc.tensor.matmul(ps[:, :], mat[:, c, f * P:f * P + P],
                                                            xts[:, c, half * 512:half * 512 + 512],
                                                            start=(c == 0), stop=(c == DC - 1))
                            elif kind == "latent":
                                for c in range(DC):
                                    last = nc.tensor.matmul(ps[:, :], mat[:, c, :],
                                                            xts[:, c, half * 512:half * 512 + 512],
                                                            start=(c == 0), stop=(c == DC - 1))
                            elif kind == "klat":
                                pe.wait_ge(t("lat"), b * 2 + half + 1)
                                last = nc.tensor.matmul(ps[:, :], mat[:, 0, f * P:f * P + P],
                                                        lat[:, half * 512:half * 512 + 512], start=True, stop=True)
                            elif kind == "vlat":
                                for u in (2 * half, 2 * half + 1):
                                    last = nc.tensor.matmul(ps[:, (u % 2) * D:(u % 2) * D + D],
                                                            lat[:, u * P:u * P + P], mat[:, 0, :],
                                                            start=True, stop=True)
                            elif kind == "v":
                                for u in (2 * half, 2 * half + 1):
                                    for c in range(DC):
                                        last = nc.tensor.matmul(ps[:, (u % 2) * D:(u % 2) * D + D],
                                                                xts[:, c, u * P:u * P + P], mat[:, c, :],
                                                                start=(c == 0), stop=(c == DC - 1))
                            elif kind == "logits":
                                for u in range(4 * half, 4 * half + 4):
                                    for c in range(DC):
                                        last = nc.tensor.matmul(ps[:, (u % 4) * NX:(u % 4) * NX + NX],
                                                                xts[:, c, u * P:u * P + P], mat[:, c, :],
                                                                start=(c == 0), stop=(c == DC - 1))
                            last.then_inc(t("work_ps"), 1)

            def dve_prog(dve):
                if wn is not None:
                    weights_ready(dve, wn)
                if has_in:
                    dve.sem_inc(t("r"), 2)
                if nw:
                    dve.sem_inc(t("work_free"), 2)
                with dve.Fori(0, NB) as b:
                    def add(p):
                        rp = r_tok[:, 2 * p:2 * p + 2, :]
                        dve.wait_ge(t("xb"), b * n_pairs + p + 1)
                        if p == 0:
                            if nw and rms is None:
                                wait(dve, t("trx_ps"), b * n_pairs, 1)
                            if x_out:
                                wait(dve, t("pool_x"), b * n_pairs * (2 if rows_out else 1), 1)
                            if final:
                                wait(dve, t("out"), 16 * b * n_pairs, 1)
                        if source == "proj":
                            dve.wait_ge(t("prj_ps"), 1 + b * n_pairs + p + 1)
                            nc.vector.tensor_tensor(rp, bank[2 + p % 2][:, :].rearrange("p (t d) -> p t d", t=2),
                                                    xb[:, p % 2, :, :], ALU.add).then_inc(t("r"), 1)
                        else:
                            for n in range(2):
                                for u in range(2):
                                    last = nc.vector.scalar_tensor_tensor(
                                        out=r_tok[:, 2 * p + u, :],
                                        in0=gathered[:, n, ds(b * TPB + 2 * p + u, 1), :].rearrange("p o d -> p (o d)"),
                                        scalar=gate_w[:, n, ds(b * TPB + 2 * p + u, 1)],
                                        in1=(xb[:, p % 2, u, :] if n == 0 else r_tok[:, 2 * p + u, :]),
                                        op0=ALU.mult, op1=ALU.add)
                                    if n == 0:
                                        last.then_inc(t("first_row"), 1)
                                if n == 0:
                                    dve.wait_ge(t("first_row"), b * TPB + 2 * p + 2)
                            last.then_inc(t("r"), 1)

                    def moments(p, n, src, ready, value, done):
                        dve.wait_ge(ready, value)
                        for u in (2 * p, 2 * p + 1):
                            nc.vector.bn_stats(bst[:, n, u, :], src[:, u, :]).then_inc(t(f"st{n}"), 1)
                        for u in (2 * p, 2 * p + 1):
                            hold(dve, t(f"st{n}"), b * TPB + u + 1, t("held_dve"))
                            nc.vector.bn_aggr(mv[:, n, u, :], bst[:, n, u, :]).then_inc(t(done), 1)

                    def norm_rows(p):
                        dve.wait_ge(t("pool_n"), b * 2 * n_pairs + 2 * p + 2)
                        for u in (2 * p, 2 * p + 1):
                            nc.vector.tensor_scalar(r_tok[:, u, :], r_tok[:, u, :], mv[:, 0, u, 0:1],
                                                    rstd[:, 0, u:u + 1], ALU.subtract, ALU.mult)\
                                .then_inc(t("xs"), 1)

                    def rms_rows(p):
                        dve.wait_ge(t("pool_r"), b * 4 * n_pairs + 4 * p + 4)
                        if p == 0:
                            if source == "proj":
                                dve.wait_ge(t("tra_ps"), 1 + (b + 1) * n_pairs)
                        for u in (2 * p, 2 * p + 1):
                            nc.vector.scalar_tensor_tensor(out=h_tok[:, u, :], in0=r_tok[:, u, :],
                                                           scalar=rstd[:, 1, u:u + 1], in1=rms,
                                                           op0=ALU.mult, op1=ALU.mult).then_inc(t("h"), 1)

                    if has_in:
                        for p in range(n_pairs + 1):
                            if p < n_pairs:
                                add(p)
                                if norm:
                                    moments(p, 0, r_tok, t("r"), 2 + b * n_pairs + p + 1, "mv")
                                elif rms is not None:
                                    moments(p, 1, r_tok, t("r"), 2 + b * n_pairs + p + 1, "mv2")
                            if p >= 1 and norm:
                                norm_rows(p - 1)
                                if rms is not None:
                                    moments(p - 1, 1, r_tok, t("xs"), b * TPB + 2 * p, "mv2")
                        if rms is not None:
                            for p in range(n_pairs):
                                rms_rows(p)
                    for k, (kind, o, f, half) in enumerate(work):
                        dve_unit(dve, b, k, kind, o, f, half)

            def dve_unit(dve, b, k, kind, o, f, half):
                if kind == "latent":
                    dve.wait_ge(t("lat"), b * 2 + lats.index(k) + 1)
                    dve.sem_inc(t("work_free"), 1)
                    return
                ps = bank[6 + k % 2]
                if kind in ("qk", "klat"):
                    n = qk_no[k]
                    s = n % 2
                    dve.wait_ge(t("work_ps"), 1 + b * nw + k + 1)
                    dve.wait_ge(t("third"), 2 + b * nqk + n - 1)
                    bias, scale = (o[2], o[3]) if kind == "qk" else (None, 1.0)
                    if bias is None:
                        nc.vector.tensor_scalar(u_f[:, s, :], ps[:, :], scale, None, ALU.mult)\
                            .then_inc(t("first_u"), 1)
                    else:
                        nc.vector.tensor_scalar(u_f[:, s, :], ps[:, :], bias[:, f:f + 1], scale, ALU.add, ALU.mult)\
                            .then_inc(t("first_u"), 1)
                    dve.wait_ge(t("first_u"), b * nqk + n + 1)
                    dve.sem_inc(t("work_free"), 1)
                    dve.wait_ge(t("first"), b * nqk + n + 1)
                    nc.vector.tensor_tensor(u_f[:, s, :], u_f[:, s, :], parts[:, s, 0, :], ALU.subtract)\
                        .then_inc(t("rest_u"), 1)
                elif kind in ("v", "vlat"):
                    dve.wait_ge(t("work_ps"), 1 + b * nw + k + 1)
                    for u in range(2):
                        dst = v_tok.rearrange("p (g n) -> p g n", g=4)[:, :, ds(b * (TPB * 64) + (2 * half + u) * 64, 64)]
                        src = ps[:, u * D:u * D + D].rearrange("p (g w) -> p g w", g=4)
                        if kind == "v":
                            last = nc.vector.tensor_tensor(dst, src, o[2].rearrange("p (g w) -> p g w", g=4), ALU.add)
                        else:
                            last = nc.vector.tensor_copy(dst, src)
                    last.then_inc(t("work_free"), 1)
                elif kind == "logits":
                    dve.wait_ge(t("work_ps"), 1 + b * nw + k + 1)
                    nc.vector.tensor_copy(o[2][:, ds(b * TPB * NX + half * 4 * NX, 4 * NX)], ps[:, 0:4 * NX])\
                        .then_inc(t("work_free"), 1)

            def pool_wrapped(pool):
                pool.sem_inc(t("pool_x"), 1)
                if nqk:
                    pool.sem_inc(t("third"), 2)
                pool_prog(pool)

            progs = {"sp": sp_prog, "dve": dve_prog, "pool": pool_wrapped}
            if nw or source == "proj":
                progs["pe"] = pe_prog
                progs["act"] = act_prog
            stages.append((name, progs))

        def context_stage(name, wn, layers):
            ct = xts_flat[:, 0:2 * NB * SC].rearrange("p (c t) -> p c t", c=2)
            vx_t = o_tok[:, 0:2 * 1024].rearrange("p (l g n w) -> p l g n w", l=2, g=4, n=4)
            rows = (P, CW - P)
            n_tok = NB * SC

            def t(n):
                return sem(f"ctx_{n}")

            kunits = [(l, f) for l in range(2) for f in range(2)]
            vunits = [(l, b, kb) for l in range(2) for b in range(NB) for kb in range(2)]

            def sp_prog(sp):
                load_weights(sp, wn + 1)
                for c in range(2):
                    sp.dma_start(ct[0:rows[c], c, :], a["ctxT"][c * P:c * P + rows[c], :]).then_inc(t("in"), 16)
                for n, (l, f) in enumerate(kunits):
                    sp.wait_ge(t("third"), n + 1)
                    for j in range(2):
                        for b in range(NB):
                            sp.dma_start(kx_scr[l][f, j, b, :, :].rearrange("(k r) t -> r k t", k=3),
                                         parts[j * 64:j * 64 + 64, n % 2, :, b * SC:b * SC + SC])\
                                .then_inc(t(f"scr{n % 2}"), 16)
                sp.wait_ge(t("v"), len(vunits))
                for l in range(2):
                    sp.dma_start(vx_scr[l], vx_t[:, l, :, :, :].rearrange("p g n w -> p (g n w)"))\
                        .then_inc(t("vstored"), 16)
                sp.wait_ge(t("vstored"), 32)
                for s in range(2):
                    sp.wait_ge(t(f"scr{s}"), 16 * 4 * 2)

            def pe_prog(pe):
                weights_ready(pe, wn)
                pe.wait_ge(t("in"), 32)
                for n, (l, f) in enumerate(kunits):
                    wait(pe, t("u"), n - 1)
                    for c in range(2):
                        last = nc.tensor.matmul(bank[n % 2][:, 0:n_tok], w_ctx[l]["wk"][0:rows[c], c, f * P:f * P + P],
                                                ct[0:rows[c], c, :], start=(c == 0), stop=(c == 1))
                    last.then_inc(t("k_ps"), 1)
                for n, (l, b, kb) in enumerate(vunits):
                    wait(pe, t("v"), n - 1)
                    k0, kn = b * SC + kb * SC // 2, SC // 2
                    for c in range(2):
                        last = nc.tensor.matmul(bank[2 + n % 2][0:kn, 0:D], ct[0:rows[c], c, k0:k0 + kn],
                                                w_ctx[l]["wv"][0:rows[c], c, :], start=(c == 0), stop=(c == 1))
                    last.then_inc(t("v_ps"), 1)

            def act_prog(act):
                for n in range(len(kunits)):
                    s = n % 2
                    act.wait_ge(t("u"), n + 1)
                    wait(act, t(f"scr{s}"), (n // 2) * 64)
                    nc.scalar.activation(parts[:, s, 0, 0:n_tok], u_f[:, s, 0:n_tok], ACT.Copy).then_inc(t("first"), 1)
                    act.wait_ge(t("rest"), n + 1)
                    nc.scalar.activation(parts[:, s, 1, 0:n_tok], u_f[:, s, 0:n_tok], ACT.Copy).then_inc(t("second"), 1)

            def pool_prog(pool):
                for n in range(len(kunits)):
                    s = n % 2
                    pool.wait_ge(t("second"), n + 1)
                    nc.gpsimd.tensor_tensor(parts[:, s, 2, 0:n_tok], u_f[:, s, 0:n_tok], parts[:, s, 1, 0:n_tok],
                                            ALU.subtract).then_inc(t("third"), 1)

            def dve_prog(dve):
                weights_ready(dve, wn)
                nc.vector.memset(vx_t, 0.0).then_inc(t("zero"), 1)
                for n, (l, f) in enumerate(kunits):
                    s = n % 2
                    wait(dve, t("third"), n - 1)
                    dve.wait_ge(t("k_ps"), n + 1)
                    nc.vector.tensor_scalar(u_f[:, s, 0:n_tok], bank[s][:, 0:n_tok], w_ctx[l]["bk"][:, f:f + 1], None,
                                            ALU.add).then_inc(t("u"), 1)
                    dve.wait_ge(t("first"), n + 1)
                    nc.vector.tensor_tensor(u_f[:, s, 0:n_tok], u_f[:, s, 0:n_tok], parts[:, s, 0, 0:n_tok],
                                            ALU.subtract).then_inc(t("rest"), 1)
                dve.wait_ge(t("zero"), 1)
                for n, (l, b, kb) in enumerate(vunits):
                    kn = SC // 2
                    dve.wait_ge(t("v_ps"), n + 1)
                    nc.vector.tensor_tensor(vx_t[0:kn, l, :, 2 * b + kb, :],
                                            bank[2 + n % 2][0:kn, 0:D].rearrange("p (g w) -> p g w", g=4),
                                            w_ctx[l]["bv"][0:kn, :].rearrange("p (g w) -> p g w", g=4), ALU.add)\
                        .then_inc(t("v"), 1)

            stages.append((name, {"sp": sp_prog, "pe": pe_prog, "act": act_prog, "pool": pool_prog, "dve": dve_prog}))

        def load_context(sp, n):
            done = sem(f"context{n}")
            sp.dma_start(v_tok[:, 0:1024], vx_scr[n]).then_inc(done, 16)
            for s in range(2):
                row = 0
                for m in (3, 2, 1):
                    for r in range(m):
                        sp.dma_start(k_all[s][row:row + 16].rearrange("p i h t -> p i (h t)"),
                                     kx_scr[n][s].rearrange("j b (r h) t -> r (j b) (h t)", h=HG)
                                     [16 * (3 - m):16 * (4 - m)]).then_inc(done, 16)
                        row += 16
                sp.dma_start(k_all[s][STK:STK + 3].rearrange("p i h t -> p i (h t)"), a["ones_x"])\
                    .then_inc(done, 16)

        def context_loaded(eng, n):
            eng.wait_ge(sem(f"context{n}"), 16 * 15)

        def attention_stage(at, extra_sp=None):
            def t(n):
                return sem(f"att_{n}")

            keys, nkb = at.keys, at.kblocks
            vtiles = TPB if keys == S else 2
            probs = [prob[:, 0], prob[:, 1]] + [w2_high[:, n * HG * 512:(n + 1) * HG * 512]
                                                .rearrange("p (h q) -> p h q", h=HG) for n in range(2)]
            floors = [floor_t, arena[:, xb_base:xb_base + HG * 512].rearrange("p (h q) -> p h q", h=HG)]
            a_bank = (0, 2)
            st_bank = (4, 5)

            resident = keys < S

            def q_rows(s, i, row0, row1, h, lo, hi):
                if resident:
                    return q_all[s][row0:row1, ds(i, 1), h, lo:hi].rearrange("p o t -> p (o t)")
                return stk[s][0][row0:row1, h, lo:hi]

            def k_rows(s, i, row0, row1, h, lo, hi):
                if resident:
                    return k_all[s][row0:row1, ds(i, 1), h, lo:hi].rearrange("p o t -> p (o t)")
                return stk[s][1][row0:row1, h, lo:hi]

            def load_queries(sp, s, i):
                if not (isinstance(i, int) and i == 0):
                    sp.wait_ge(t(f"ld{s}"), 48 * i)
                row = 0
                for n in (3, 2, 1):
                    sp.dma_start(q_all[s][row:row + 16 * n, ds(i, 1)].rearrange("p o h t -> p (o h) t"),
                                 at.q_scr[s].rearrange("j b (k d h) t -> (j b) (k d) h t", k=3, h=HG)[ds(i, 1), 0:16 * n]
                                 .rearrange("o d h t -> (o d) h t")).then_inc(t(f"ld{s}"), 16)
                    row += 16 * n

            def load_group(sp, s, i):
                q, k = stk[s]
                row = 0
                for n in (3, 2, 1):
                    sp.dma_start(q[row:row + 16 * n, :, :],
                                 at.q_scr[s].rearrange("j b (k d h) t -> (j b) (k d) h t", k=3, h=HG)[ds(i, 1), 0:16 * n]
                                 .rearrange("o d h t -> (o d) h t")).then_inc(t(f"ld{s}"), 16)
                    for m in range(n):
                        sp.dma_start(k[row + 16 * m:row + 16 * m + 16, :, :],
                                     at.k_scr[s].rearrange("j b (k d h) t -> (j b) (k d) h t", k=3, h=HG)
                                     [ds(i, 1), 16 * (3 - n):16 * (4 - n)].rearrange("o d h t -> (o d) h t")).then_inc(t(f"ld{s}"), 16)
                    row += 16 * n
                if at.alibi:
                    for side in range(2):
                        sp.dma_start(stk[s][side][STK:STK + 6, :, :],
                                     a["alibi"][side, s, ds(i, 1), :, :, :].rearrange("o r h t -> (o r) h t"))\
                            .then_inc(t(f"ld{s}"), 16)

            def load_max(sp, s, i):
                sp.wait_ge(t("m_parts"), 2 * i + s + 1)
                for n in range(3):
                    q = q_all[s][:, ds(i, 1)].rearrange("p o h t -> p (o h) t") if resident else stk[s][0]
                    sp.dma_start(q[at.mrow + n:at.mrow + n + 1, :, :].rearrange("o h (b q) -> o (h b) q", q=P),
                                 m_parts[0:32, n, :]).then_inc(t(f"mld{s}"), 16)

            def sp_resident(sp):
                load_queries(sp, 0, 0)
                load_queries(sp, 1, 0)
                load_max(sp, 0, 0)
                load_queries(sp, 0, 1)
                with sp.Fori(0, 2) as i:
                    load_max(sp, 1, i)
                    load_queries(sp, 1, i + 1)
                    load_max(sp, 0, i + 1)
                    load_queries(sp, 0, i + 2)
                load_max(sp, 1, 2)
                load_queries(sp, 1, 3)
                load_max(sp, 0, 3)
                load_max(sp, 1, 3)

            def sp_prog(sp):
                if resident:
                    return sp_resident(sp)
                load_group(sp, 0, 0)
                for s in range(2):
                    sp.dma_start(stk[s][1][at.mrow:at.mrow + 3, :, :], a["ones"][0:3, :, :])\
                        .then_inc(t("ones"), 16)
                load_group(sp, 1, 0)
                load_max(sp, 0, 0)
                if extra_sp:
                    extra_sp(sp)
                with sp.Fori(0, 3) as i:
                    load_max(sp, 1, i)
                    sp.wait_ge(t("st_ps"), HG * at.step(0, i, at.ns[0]))
                    load_group(sp, 0, i + 1)
                    load_max(sp, 0, i + 1)
                    sp.wait_ge(t("st_ps"), HG * at.step(1, i, at.ns[1]))
                    load_group(sp, 1, i + 1)
                load_max(sp, 1, 3)

            def stage_values(s, i):
                src = v_tok[:, ds(i * (vtiles * 64) + s * (2 * NB * vtiles * 64), vtiles * 64)]
                nc.gpsimd.tensor_copy(v_st[s][:, 0:vtiles, :, 0:HD],
                                      src.rearrange("p (k h w) -> p k h w", k=vtiles, h=HG)).then_inc(t("vs"), 1)

            def pool_prog(pool):
                for s in range(2):
                    nc.gpsimd.memset(v_st[s][:, :, :, HD:2 * HD], 1.0)
                if keys < S:
                    context_loaded(pool, at.vx)
                stage_values(0, 0)
                stage_values(1, 0)
                with pool.Fori(0, 3) as i:
                    for s in range(2):
                        pool.wait_ge(t("pv"), at.n_prob + at.step(s, i, at.ns[s]))
                        stage_values(s, i + 1)

            def pe_max(pe, s, i, k):
                qb, heads, key0, width = at.units[s][k]
                u = at.unit(s, i, k)
                par = (k + (at.nu[0] if s else 0)) % 2
                if k == 0:
                    pe.wait_ge(t(f"ld{s}"), (48 if resident else 16 * at.loads) * (i + 1))
                pe.wait_ge(t("a_max"), 2 + u - 1)
                rows = STK + (6 if at.alibi else 0)
                mode = at.modes[s]
                for n, h in enumerate(heads):
                    if keys < S:
                        spans = [(bank[a_bank[par] + n // 2][:, (n % 2) * 256:(n % 2) * 256 + width], 0, width)]
                    elif len(heads) == 2:
                        spans = [(bank[a_bank[par] + n][:, 0:width], 0, width)]
                    else:
                        spans = [(bank[a_bank[par]][:, 0:512], 0, 512),
                                 (bank[a_bank[par] + 1][:, 0:width - 512], 512, width)]
                    dcol = {"fwd": width - P, "causal": width - P, "bwd": 0}.get(mode)
                    for dst, lo, hi in spans:
                        masked = dcol is not None and lo <= dcol < hi
                        last = nc.tensor.matmul(dst, q_rows(s, i, 0, rows, h, qb * P, qb * P + P),
                                                k_rows(s, i, 0, rows, h, key0 + lo, key0 + hi), start=True, stop=not masked)
                        if masked:
                            m = mask_left if mode == "bwd" else mask_right
                            last = nc.tensor.matmul(dst[:, dcol - lo:dcol - lo + P], identb, m,
                                                    start=False, stop=True)
                last.then_inc(t("a_ps"), 1)

            def pe_scores(pe, s, i, k, hh):
                qh, kb, kn, c0, c1, diag, first, last_ = at.steps[s][k]
                u = at.step(s, i, k) * HG + hh
                par = hh % 2
                if k == 0 and hh == 0:
                    pe.wait_ge(t(f"mld{s}"), 48 * (i + 1))
                if at.clip and (kb == 0) and hh == 0:
                    for h in range(HG):
                        idx = ((2 * i + s) * 2 + qh) * HG + h
                        if h < 2:
                            pe.wait_ge(t("p"), 2 + at.step(s, i, k) * HG + h - 1)
                        pe.wait_ge(t("fl"), 2 + idx - 1)
                        nc.tensor.matmul(bank[st_bank[h % 2]][:, :], pick_max[0:at.mrow + 3, :],
                                         q_rows(s, i, 0, at.mrow + 3, h, qh * 512, qh * 512 + 512),
                                         start=True, stop=True).then_inc(t("fl_ps"), 1)
                if at.clip and kb == 0 and hh < 2:
                    pe.wait_ge(t("fl"), 2 + ((2 * i + s) * 2 + qh) * HG + HG + hh - 1)
                else:
                    pe.wait_ge(t("p"), 2 + u - 1)
                dst = bank[st_bank[par]][0:kn, c0:c1]
                rows = at.mrow + 3
                last = nc.tensor.matmul(dst, k_rows(s, i, 0, rows, hh, kb * at.kb_size, kb * at.kb_size + kn),
                                        q_rows(s, i, 0, rows, hh, qh * 512 + c0, qh * 512 + c1),
                                        start=True, stop=diag is None)
                if diag is not None:
                    m = mask_right if at.modes[s] == "bwd" else mask_left
                    last = nc.tensor.matmul(bank[st_bank[par]][:, diag:diag + P], identb, m, start=False, stop=True)
                last.then_inc(t("st_ps"), 1)

            def pe_values(pe, s, i, k):
                qh, kb, kn, c0, c1, diag, first, last_ = at.steps[s][k]
                n = at.step(s, i, k)
                place = at.part(s, k)
                if k == 0:
                    pe.wait_ge(t("vs"), 2 * i + s + 1)
                if first:
                    wait(pe, t("o_sb"), (2 * i + s) * 2 + qh, 1)
                if at.clip:
                    pe.wait_ge(t("clip"), nkb + 1 + n + 1)
                else:
                    pe.wait_ge(t("p"), 2 + n * HG + HG)
                for hh in range(HG):
                    last = nc.tensor.matmul(bank[6][32 * hh:32 * hh + 32, c0:c1], v_st[s][0:kn, kb, hh, :],
                                            probs[place][0:kn, hh, c0:c1], start=first, stop=last_)
                last.then_inc(t("pv"), 1)

            def group_of(s, i, old):
                return (s, i) if not old else ((0, i) if s else (1, i - 1))

            def pe_events(pe, ev, s, i, s2, i2, t0):
                use = 0
                for e in ev:
                    if e[0] == "A":
                        pe_max(pe, s2, i2, e[1])
                    elif e[0] == "ST":
                        pe_scores(pe, s, i, e[1], e[2])
                    elif e[0] == "PV":
                        pe_values(pe, *group_of(s, i, e[2]), e[1])
                    elif e[0] == "MT":
                        pe.wait_ge(t("a_max"), 2 + at.unit(s2, i2, at.nu[s2]))
                        wait(pe, t("t_read"), t0 + use)
                        nc.tensor.transpose(bank[7][0:32, 0:P], mstat[:, s2, :], ident).then_inc(t("t_ps"), 1)
                        use += 1
                    elif e[0] == "OT":
                        so, io = group_of(s, i, e[2])
                        pe.wait_ge(t("o_sb"), 1 + (2 * io + so) * 2 + e[1] + 1)
                        wait(pe, t("t_read"), t0 + use)
                        for b in range(4):
                            last = nc.tensor.transpose(bank[7][:, b * P:b * P + P], o_sb[:, b * P:b * P + P], ident)
                        last.then_inc(t("t_ps"), 1)
                        use += 1

            def each_block(run):
                eng, block, prologue = run
                prologue(eng)
                block(eng, at.events[0][2], 0, 0, 1, 0, 1)
                with eng.Fori(0, 3) as i:
                    block(eng, at.events[1][0], 1, i, 0, i + 1, 3 + 6 * i)
                    block(eng, at.events[0][0], 0, i + 1, 1, i + 1, 6 + 6 * i)
                block(eng, at.events[1][1], 1, 3, None, None, 21)
                block(eng, at.last, 0, 4, None, None, 23)

            def pe_prog(pe):
                def prologue(pe):
                    if resident:
                        context_loaded(pe, at.vx)
                    for k in range(at.nu[0]):
                        pe_max(pe, 0, 0, k)
                    if not resident:
                        pe.wait_ge(t("ones"), 32)
                    pe_events(pe, [("MT",)], None, None, 0, 0, 0)
                each_block((pe, pe_events, prologue))

            def act_events(act, ev, s, i, s2, i2, t0):
                for e in ev:
                    if e[0] != "ST":
                        continue
                    k, hh = e[1], e[2]
                    qh, kb, kn, c0, c1, diag, first, last_ = at.steps[s][k]
                    n = at.step(s, i, k)
                    if at.clip and kb == 0 and hh == 0:
                        for h in range(HG):
                            idx = ((2 * i + s) * 2 + qh) * HG + h
                            act.wait_ge(t("fl_ps"), idx + 1)
                            if h == 0:
                                act.wait_ge(t("clip"), n + 1)
                            nc.scalar.activation(floors[qh][:, h, :], bank[st_bank[h % 2]][:, :], ACT.Exp,
                                                 bias=minus_clamp[:, 0:1]).then_inc(t("fl"), 1)
                    if hh == 0:
                        act.wait_ge(t("pv"), n + 1)
                    act.wait_ge(t("st_ps"), n * HG + hh + 1)
                    src = bank[st_bank[hh % 2]][0:kn, c0:c1]
                    nc.scalar.activation(probs[at.part(s, k)][0:kn, hh, c0:c1], src, ACT.Exp).then_inc(t("p"), 1)

            def act_prog(act):
                act.sem_inc(t("p"), 2)
                if at.clip:
                    act.sem_inc(t("fl"), 2)
                each_block((act, act_events, lambda act: None))

            def dve_max(dve, s, i, k):
                qb, heads, key0, width = at.units[s][k]
                u = at.unit(s, i, k)
                par = (k + (at.nu[0] if s else 0)) % 2
                dve.wait_ge(t("a_ps"), u + 1)
                both = psum[:, 1024 * par:1024 * par + 1024]
                if keys < S:
                    src = both.rearrange("p (h k) -> p h k", h=HG)[:, :, 0:width]
                elif len(heads) == 2:
                    src = both.rearrange("p (h k) -> p h k", h=2)[:, :, 0:width]
                else:
                    src = both[:, 0:width].unsqueeze(1)
                dst = mstat[:, s, :].rearrange("p (h b) -> p h b", h=HG)[:, heads[0]:heads[-1] + 1, qb]
                nc.vector.tensor_reduce(dst, src, AX.X, ALU.max).then_inc(t("a_max"), 1)

            def dve_events(dve, ev, s, i, s2, i2, t0):
                use = 0
                for e in ev:
                    if e[0] == "A":
                        dve_max(dve, s2, i2, e[1])
                    elif e[0] == "CL" and at.clip:
                        k = e[1]
                        qh, kb, kn, c0, c1, diag, first, last_ = at.steps[s][k]
                        n = at.step(s, i, k)
                        place = probs[at.part(s, k)][0:kn]
                        if kb == 0:
                            dve.wait_ge(t("fl"), 2 + ((2 * i + s) * 2 + qh) * HG + HG)
                        dve.wait_ge(t("p"), 2 + n * HG + HG)
                        nc.vector.scalar_tensor_tensor(out=place, in0=place,
                                                       scalar=1.0, in1=floors[qh][0:kn, :, :],
                                                       op0=ALU.min, op1=ALU.max).then_inc(t("clip"), 1)
                    elif e[0] == "OC":
                        so, io = group_of(s, i, e[2])
                        ends = [k for k, x in enumerate(at.steps[so]) if x[7]]
                        n = at.step(so, io, ends[e[1]])
                        dve.wait_ge(t("pv"), at.n_prob + n + 1)
                        nc.vector.tensor_copy(o_sb, bank[6][:, :]).then_inc(t("o_sb"), 1)
                    elif e[0] == "MS":
                        g = 2 * i2 + s2
                        dve.wait_ge(t("t_ps"), t0 + use + 1)
                        wait(dve, t(f"mld{1 - s2}"), mld_before(g, i2, s2))
                        if at.clip:
                            nc.vector.tensor_scalar(m_f[0:32, :], bank[7][0:32, 0:P], -CLAMP, CLAMP, ALU.max, ALU.min)\
                                .then_inc(t("m_step"), 1)
                            dve.wait_ge(t("m_step"), MS * g + 1)
                            nc.vector.tensor_scalar(m_f[0:32, :], m_f[0:32, :], -1.0, None, ALU.mult)\
                                .then_inc(t("m_step"), 1)
                            at0 = 2
                        else:
                            nc.vector.tensor_scalar(m_f[0:32, :], bank[7][0:32, 0:P], -1.0, None, ALU.mult)\
                                .then_inc(t("m_step"), 1)
                            at0 = 1
                        dve.wait_ge(t("m_step"), MS * g + at0)
                        dve.sem_inc(t("t_read"), 1)
                        nc.vector.tensor_copy(m_parts[0:32, 0, :], m_f[0:32, :]).then_inc(t("m_step"), 1)
                        dve.wait_ge(t("m_step"), MS * g + at0 + 1)
                        nc.vector.tensor_tensor(m_f[0:32, :], m_f[0:32, :], m_parts[0:32, 0, :], ALU.subtract)\
                            .then_inc(t("m_step"), 1)
                        dve.wait_ge(t("m_step"), MS * g + at0 + 2)
                        nc.vector.tensor_copy(m_parts[0:32, 1, :], m_f[0:32, :]).then_inc(t("m_step"), 1)
                        dve.wait_ge(t("m_step"), MS * g + at0 + 3)
                        nc.vector.tensor_tensor(m_parts[0:32, 2, :], m_f[0:32, :], m_parts[0:32, 1, :], ALU.subtract)\
                            .then_inc(t("m_parts"), 1)
                        use += 1
                    elif e[0] == "ON":
                        so, io = group_of(s, i, e[2])
                        g2 = (2 * io + so) * 2 + e[1]
                        dve.wait_ge(t("t_ps"), t0 + use + 1)
                        sums = bank[7][:, :].rearrange("p (n w) -> p n w", w=32)
                        nc.vector.reciprocal(orec, sums[:, :, HD]).then_inc(t("rec"), 1)
                        dve.wait_ge(t("rec"), g2 + 1)
                        dst = o_tok[:, ds(io * (TPB * 64) + so * (2 * NB * TPB * 64) + e[1] * 256, 256)]
                        nc.vector.tensor_tensor(dst.rearrange("p (n w) -> p n w", w=HD), sums[:, :, 0:HD],
                                                orec.unsqueeze(2).to_broadcast([P, 16, HD]), ALU.mult)\
                            .then_inc(t("t_read"), 1)
                        use += 1

            MS = 5 if at.clip else 4

            def mld_before(g, i2, s2):
                return 48 * (i2 + 1) if s2 else 48 * i2

            def dve_prog(dve):
                dve.sem_inc(t("a_max"), 2)
                dve.sem_inc(t("o_sb"), 1)
                dve.sem_inc(t("clip"), nkb + 1)

                def prologue(dve):
                    for k in range(at.nu[0]):
                        dve_max(dve, 0, 0, k)
                    dve_events(dve, [("MS",)], None, None, 0, 0, 0)
                each_block((dve, dve_events, prologue))

            def pe_wrapped(pe):
                pe.sem_inc(t("pv"), at.n_prob)
                pe_prog(pe)

            stages.append((at.name, {"sp": sp_prog, "pool": pool_prog, "pe": pe_wrapped, "act": act_prog,
                                     "dve": dve_prog}))

        scratch = arena[:, route_base:route_base + 20 * NT * NX]

        def routing_stage(name, rows, soft_all, extra_sp=None):
            def t(n):
                return sem(f"route_{n}")

            def tile_of(n, k=NX):
                return scratch[:, n * NT * NX:n * NT * NX + NT * k].rearrange("p (t e) -> p t e", t=NT)

            lg, tmp, oh1, lg2, oh2, ex, pos, tot = (tile_of(n) for n in range(8))
            acc = scratch[:, 8 * 128:8 * 128 + (NT + 1) * NX].rearrange("p (t e) -> p t e", t=NT + 1)
            small = scratch[:, 10 * 128:11 * 128]
            m1, m2, mr, e2, den, rec, s1 = (small[:, n * NT:n * NT + NT] for n in range(7))
            few = scratch[:, 11 * 128:11 * 128 + 64]
            tiles_f, tiles_i, start, base = (few[:, n * 8:n * 8 + 8] for n in (0, 1, 2, 3))
            tiles_i = tiles_i.bitcast(I32)
            ohb = scratch[:, 12 * 128:12 * 128 + 64].bitcast(BF16)
            cmp = scratch[:, 13 * 128:13 * 128 + NTILE * (NX - 1)].rearrange("p (n e) -> p n e", n=NTILE)
            te_f = scratch[:, 16 * 128:16 * 128 + NTILE]

            def over_e(v):
                return v.unsqueeze(2).to_broadcast([P, NT, NX])

            def dve_prog(dve):
                done = [0]

                def then(ins):
                    done[0] += 1
                    ins.then_inc(t("step"), 1)
                    dve.wait_ge(t("step"), done[0])

                V = nc.vector
                for src, m, oh in ((lg, m1, oh1), (lg2, m2, oh2)):
                    then(V.tensor_reduce(m, src, AX.X, ALU.max))
                    then(V.tensor_tensor(tmp, src, over_e(m), ALU.is_equal))
                    then(V.tensor_tensor(tmp, tmp, expert_rank, ALU.mult))
                    then(V.tensor_reduce(mr, tmp, AX.X, ALU.max))
                    then(V.tensor_tensor(oh, expert_rank, over_e(mr), ALU.is_equal))
                    if oh is oh1:
                        then(V.scalar_tensor_tensor(out=lg2, in0=oh1, scalar=-3e38, in1=lg,
                                                    op0=ALU.mult, op1=ALU.add))
                V.tensor_tensor(ohb.rearrange("p (t e) -> p t e", t=NT), oh1, oh2, ALU.add).then_inc(t("oh"), 1)
                if soft_all:
                    V.tensor_tensor(ex, lg, over_e(m1), ALU.subtract).then_inc(t("ex_in"), 1)
                V.tensor_tensor(e2, m2, m1, ALU.subtract).then_inc(t("ex_in"), 1)
                dve.wait_ge(t("rank_ps"), 1)
                then(V.memset(acc[:, 0, :], 0.0))
                then(V.tensor_copy(tot.rearrange("p t e -> p (t e)"), bank[0][:, 0:P]))
                for n in range(NT):
                    then(V.tensor_tensor(acc[:, n + 1, :], acc[:, n, :], tot[:, n, :], ALU.add))
                then(V.tensor_scalar(tiles_i, acc[:, NT, :], float(P - 1), None, ALU.add))
                then(V.tensor_scalar(tiles_i, tiles_i, 7, None, ALU.arith_shift_right))
                then(V.tensor_copy(tiles_f, tiles_i))
                then(V.memset(start[:, 0:1], 0.0))
                for e in range(NX - 1):
                    then(V.tensor_tensor(start[:, e + 1:e + 2], start[:, e:e + 1], tiles_f[:, e:e + 1], ALU.add))
                then(V.tensor_scalar(base, start, float(P), None, ALU.mult))
                then(V.tensor_tensor(pos.rearrange("p t e -> p (t e)"), bank[0][:, P:2 * P],
                                     acc[:, 0:NT, :].rearrange("p t e -> p (t e)"), ALU.add))
                then(V.tensor_tensor(pos, pos, base.unsqueeze(1).to_broadcast([P, NT, NX]), ALU.add))
                for k, oh in enumerate((oh1, oh2)):
                    then(V.tensor_tensor(tmp, pos, oh, ALU.mult))
                    then(V.tensor_reduce(s1, tmp, AX.X, ALU.add))
                    then(V.tensor_copy(slot_i[:, k, :], s1))
                dve.sem_inc(t("slots"), 1)
                then(V.tensor_tensor(cmp, tile_no.unsqueeze(2).to_broadcast([P, NTILE, NX - 1]),
                                     start[:, 1:NX].unsqueeze(1).to_broadcast([P, NTILE, NX - 1]), ALU.is_ge))
                then(V.tensor_reduce(te_f, cmp, AX.X, ALU.add))
                then(V.tensor_copy(tile_expert, te_f))
                dve.wait_ge(t("ex_out"), 2 if soft_all else 1)
                if soft_all:
                    then(V.tensor_reduce(den, ex, AX.X, ALU.add))
                else:
                    then(V.tensor_scalar(den, e2, 1.0, None, ALU.add))
                then(V.reciprocal(gate_w[:, 0, :], den))
                then(V.tensor_tensor(gate_w[:, 1, :], gate_w[:, 0, :], e2, ALU.mult))

            def pe_prog(pe):
                pe.wait_ge(t("oh"), 1)
                nc.tensor.matmul(bank[0][:, 0:P], onesb, ohb, start=True, stop=True)
                nc.tensor.matmul(bank[0][:, P:2 * P], lower, ohb, start=True, stop=True).then_inc(t("rank_ps"), 1)

            def act_prog(act):
                for n, v in enumerate(([ex] if soft_all else []) + [e2]):
                    act.wait_ge(t("ex_in"), n + 1)
                    nc.scalar.activation(v, v, ACT.Exp).then_inc(t("ex_out"), 1)

            def pool_prog(pool):
                pool.wait_ge(t("slots"), 1)
                for k in range(2):
                    for n in range(NT):
                        nc.gpsimd.indirect_dma_start(
                            out=xs_scr, out_offset=bass.IndirectOffsetOnAxis(ap=slot_i[:, k, n:n + 1].bitcast(U32), axis=0),
                            in_=rows[:, n, :], in_offset=None).then_inc(sem(f"{name}_scattered"), 16)
                pool.wait_ge(sem(f"{name}_scattered"), 16 * 2 * NT)

            progs = {"dve": dve_prog, "pe": pe_prog, "act": act_prog, "pool": pool_prog}
            if extra_sp:
                progs["sp"] = extra_sp
            stages.append((name, progs))

        def expert_stage(name, gated, F, wu, w2, weights_wait):
            def t(n):
                return sem(f"experts_{n}")

            nf = (F + P - 1) // P
            fw = [min(P, F - n * P) for n in range(nf)]
            half = F // 2 if F > 512 else F
            nh = F // half
            at = [exp_base]

            def buf(n):
                at[0] += n
                return arena[:, at[0] - n:at[0]]

            xin = buf(2 * D).rearrange("p (s d) -> p s d", s=2)
            xT = buf(2 * D).rearrange("p (s c q) -> p s c q", s=2, c=DC)
            yo = buf(2 * D).rearrange("p (s d) -> p s d", s=2)
            gl, hs = buf(F), buf(F)
            hT = buf(2 * nf * P).rearrange("p (s n q) -> p s n q", s=2, n=nf)
            assert at[0] <= route_base
            h_ready = "h"

            def sp_load(sp, n, s):
                sp.dma_start(xin[:, s, :], xs_scr[ds(n * P, P), :]).then_inc(t(f"in{s}"), 16)

            def sp_store(sp, n, s):
                sp.wait_ge(t("y"), 1 + n + 1)
                sp.dma_start(ys_scr[ds(n * P, P), :], yo[:, s, :]).then_inc(t(f"st{s}"), 16)

            def sp_prog(sp):
                for s in range(2):
                    sp.sem_inc(t(f"st{s}"), 1)
                def next_load(n, s):
                    sp.wait_ge(t("xT_ps"), n + 1)
                    sp_load(sp, n + 2, s)

                sp_load(sp, 0, 0)
                sp_load(sp, 1, 1)
                next_load(0, 0)
                with sp.Fori(0, NTILE // 2 - 2) as i:
                    for s in range(2):
                        next_load(2 * i + 1 + s, 1 - s)
                        sp_store(sp, 2 * i + s, s)
                next_load(NTILE - 3, 1)
                sp_store(sp, NTILE - 4, 0)
                sp_store(sp, NTILE - 3, 1)
                sp_store(sp, NTILE - 2, 0)
                sp_store(sp, NTILE - 1, 1)
                for s in range(2):
                    sp.wait_ge(t(f"st{s}"), 1 + 16 * NTILE // 2)

            def pe_xt(pe, n, s, n2):
                pe.wait_ge(t(f"in{s}"), 16 * (n2 + 1))
                wait(pe, t("xT"), n)
                for c in range(DC):
                    last = nc.tensor.transpose(bank[6][:, c * P:c * P + P], xin[:, s, c * P:c * P + P], ident)
                last.then_inc(t("xT_ps"), 1)

            def pe_up(pe, n, s):
                e = pe.value_load(tile_expert[0:1, ds(n, 1)], min_val=0, max_val=NX - 1)
                pe.wait_ge(t("xT"), n + 1)
                wait(pe, t("g" if gated else h_ready), n)
                for w in range(2 if gated else 1):
                    if w == 1:
                        wait(pe, t(h_ready), n)
                    for hf in range(nh):
                        for c in range(DC):
                            last = nc.tensor.matmul(
                                bank[2 * w + hf][:, 0:half], xT[:, s, c, :],
                                wu[:, ds(e, 1), c, w, hf * half:hf * half + half].rearrange("p o f -> p (o f)"),
                                start=(c == 0), stop=(c == DC - 1))
                    last.then_inc(t("up"), 1)

            def pe_ht(pe, n):
                pe.wait_ge(t(h_ready), n + 1)
                wait(pe, t("hT"), n)
                for f in range(nf):
                    last = nc.tensor.transpose(bank[4 + f // 4][0:fw[f], (f % 4) * P:(f % 4) * P + P],
                                               hs[:, f * P:f * P + fw[f]], ident)
                last.then_inc(t("hT_ps"), 1)

            def pe_down(pe, n, s):
                e = pe.value_load(tile_expert[0:1, ds(n, 1)], min_val=0, max_val=NX - 1)
                pe.wait_ge(t("hT"), n + 1)
                wait(pe, t("y"), n, 1)
                for f in range(nf):
                    last = nc.tensor.matmul(bank[7][:, 0:D], hT[0:fw[f], s, f, :],
                                            w2[f][0:fw[f], ds(e, 1), :].rearrange("p o d -> p (o d)"),
                                            start=(f == 0), stop=(f == nf - 1))
                last.then_inc(t("y_ps"), 1)

            def pe_prog(pe):
                weights_wait(pe)
                pe.sem_inc(t("y_ps"), 1)
                pe_xt(pe, 0, 0, 0)
                pe_up(pe, 0, 0)
                pe_xt(pe, 1, 1, 0)
                pe_ht(pe, 0)
                with pe.Fori(0, NTILE // 2 - 1) as i:
                    pe_up(pe, 2 * i + 1, 1)
                    pe_xt(pe, 2 * i + 2, 0, i + 1)
                    pe_down(pe, 2 * i, 0)
                    pe_ht(pe, 2 * i + 1)
                    pe_up(pe, 2 * i + 2, 0)
                    pe_xt(pe, 2 * i + 3, 1, i + 1)
                    pe_down(pe, 2 * i + 1, 1)
                    pe_ht(pe, 2 * i + 2)
                pe_up(pe, NTILE - 1, 1)
                pe_down(pe, NTILE - 2, 0)
                pe_ht(pe, NTILE - 1)
                pe_down(pe, NTILE - 1, 1)

            up = 2 if gated else 1

            def act_xt(act, n, s):
                act.wait_ge(t("xT_ps"), n + 1)
                wait(act, t("up"), (n - 1) * up)
                nc.scalar.activation(xT[:, s, :, :].rearrange("p c q -> p (c q)"), bank[6][:, 0:D], ACT.Copy)\
                    .then_inc(t("xT"), 1)

            def act_hidden(act, n):
                act.wait_ge(t("up"), n * up + 1)
                if gated:
                    wait(act, t(h_ready), n)
                    nc.scalar.activation(gl.rearrange("p (h f) -> p h f", h=nh),
                                         psum[:, 0:1024].rearrange("p (h f) -> p h f", h=2)[:, :, 0:half],
                                         ACT.Gelu).then_inc(t("g"), 1)
                else:
                    wait(act, t("hT_ps"), n)
                    nc.scalar.activation(hs, bank[0][:, 0:F], ACT.Silu).then_inc(t(h_ready), 1)

            def act_out(act, n, s, n2):
                act.wait_ge(t("y_ps"), 1 + n + 1)
                wait(act, t(f"st{s}"), 16 * n2, 1)
                nc.scalar.activation(yo[:, s, :], bank[7][:, 0:D], ACT.Copy).then_inc(t("y"), 1)

            def act_prog(act):
                act.sem_inc(t("y"), 1)
                act_xt(act, 0, 0)
                act_hidden(act, 0)
                act_xt(act, 1, 1)
                with act.Fori(0, NTILE // 2 - 1) as i:
                    act_hidden(act, 2 * i + 1)
                    act_xt(act, 2 * i + 2, 0)
                    act_out(act, 2 * i, 0, i)
                    act_hidden(act, 2 * i + 2)
                    act_xt(act, 2 * i + 3, 1)
                    act_out(act, 2 * i + 1, 1, i)
                act_hidden(act, NTILE - 1)
                act_out(act, NTILE - 2, 0, NTILE // 2 - 1)
                act_out(act, NTILE - 1, 1, NTILE // 2 - 1)

            def dve_tile(dve, n, s):
                if gated:
                    dve.wait_ge(t("g"), n + 1)
                    dve.wait_ge(t("up"), n * up + 2)
                    wait(dve, t("hT_ps"), n)
                    nc.vector.tensor_tensor(hs.rearrange("p (h f) -> p h f", h=nh),
                                            gl.rearrange("p (h f) -> p h f", h=nh),
                                            psum[:, 1024:2048].rearrange("p (h f) -> p h f", h=2)[:, :, 0:half],
                                            ALU.mult).then_inc(t(h_ready), 1)
                dve.wait_ge(t("hT_ps"), n + 1)
                wait(dve, t("y_ps"), n - 1, 1)
                whole = F // P
                last = nc.vector.tensor_copy(hT[:, s, 0:whole, :].rearrange("p n q -> p (n q)"),
                                             psum[:, 2048:2048 + whole * P])
                if whole < nf:
                    last = nc.vector.tensor_copy(hT[0:fw[whole], s, whole, :],
                                                 psum[0:fw[whole], 2048 + whole * P:2048 + whole * P + P])
                last.then_inc(t("hT"), 1)

            def dve_prog(dve):
                dve_tile(dve, 0, 0)
                with dve.Fori(0, NTILE // 2 - 1) as i:
                    dve_tile(dve, 2 * i + 1, 1)
                    dve_tile(dve, 2 * i + 2, 0)
                dve_tile(dve, NTILE - 1, 1)

            stages.append((name, {"sp": sp_prog, "pe": pe_prog, "act": act_prog, "dve": dve_prog}))

        def gather_stage(name):
            def pool_prog(pool):
                for k in range(2):
                    for n in range(NT):
                        nc.gpsimd.indirect_dma_start(
                            out=gathered[:, k, n, :], out_offset=None, in_=ys_scr,
                            in_offset=bass.IndirectOffsetOnAxis(ap=slot_i[:, k, n:n + 1].bitcast(U32), axis=0))\
                            .then_inc(sem(f"{name}_gathered"), 16)
                pool.wait_ge(sem(f"{name}_gathered"), 16 * 2 * NT)
            stages.append((name, {"pool": pool_prog}))

        g = a.get
        W = {}
        v = weights(("mat", g("L0_attn_Wq")), ("mat", g("L0_attn_Wk")), ("mat", g("L0_attn_Wv")),
                    ("row", g("L0_attn_bv")), ("col", g("L0_attn_bq")), ("col", g("L0_attn_bk")))
        W["t0"] = dict(zip(("wq", "wk", "wv", "bv", "bq", "bk"), v))
        v = weights(("mat", g("L0_xattn_Wk")), ("mat", g("L0_xattn_Wv")), ("row", g("L0_xattn_bv")),
                    ("col", g("L0_xattn_bk")),
                    ("mat", g("L1_xattn_wk")), ("mat", g("L1_xattn_wv")), ("col", g("L1_xattn_bk")))
        w_ctx = [dict(zip(("wk", "wv", "bv", "bk"), v[0:4])), dict(zip(("wk", "wv", "bk"), v[4:7]))]
        bvx1 = floor_t.rearrange("p h q -> p (h q)")[:, 0:D]
        wdefs[-1].append((bvx1, g("L1_xattn_bv").partition_broadcast(P)))
        w_ctx[1]["bv"] = bvx1
        v = weights(("mat", g("L0_attn_Wf")), ("row", g("L0_attn_bf")), ("mat", g("L0_xattn_Wq")), ("col", g("L0_xattn_bq")))
        W["t1"] = dict(zip(("wo", "brow", "wq", "bq"), v))
        v = weights(("mat", g("L0_xattn_Wo")), ("row", g("L0_xattn_bo")), ("mat", g("L0_ffn_router_w")))
        W["t2"] = dict(zip(("wo", "brow", "router"), v))
        qkv = g("L1_attn_W_qkv")
        bqkv = g("L1_attn_b_qkv")
        v = weights(("mat", qkv[:, 0:D]), ("mat", qkv[:, D:2 * D]), ("mat", qkv[:, 2 * D:3 * D]),
                    ("row", bqkv[2 * D:3 * D]), ("col", bqkv[0:D]), ("col", bqkv[D:2 * D]), ("row", g("L0_ffn_bias")))
        W["t3"] = dict(zip(("wq", "wk", "wv", "bv", "bq", "bk", "brow"), v))
        v = weights(("mat", g("L1_attn_W_out")), ("row", g("L1_attn_b_out")), ("mat", g("L1_xattn_wq")), ("col", g("L1_xattn_bq")))
        W["t4"] = dict(zip(("wo", "brow", "wq", "bq"), v))
        v = weights(("mat", g("L1_xattn_wo")), ("row", g("L1_xattn_bo")), ("row", g("L1_ffn_g1")), ("mat", g("L1_ffn_Wq")),
                    ("mat", g("L1_ffn_Wdkv")), ("mat", g("L1_ffn_Wuk")), ("mat", g("L1_ffn_Wuv")))
        W["t5"] = dict(zip(("wo", "brow", "g1", "wq", "wdkv", "wuk", "wuv"), v))
        v = weights(("mat", g("L1_ffn_Wo")), ("row", g("L1_ffn_g2")), ("mat", g("L1_ffn_gate_w")))
        W["t6"] = dict(zip(("wo", "g2", "router"), v))

        logits = scratch[:, 0:NT * NX]
        wu0 = arena[:, att_base:att_base + NX * DC * 2 * F0].rearrange("p (e c w f) -> p e c w f", e=NX, c=DC, w=2)
        w2_0 = [w2_low[:, n * 2048:n * 2048 + 2048].rearrange("p (e d) -> p e d", e=NX) for n in range(4)] + \
               [w2_high[:, n * 2048:n * 2048 + 2048].rearrange("p (e d) -> p e d", e=NX) for n in range(2)]
        nw1 = NX * DC * F1
        wu1 = arena[:, att_base:att_base + nw1].rearrange("p (e c w f) -> p e c w f", e=NX, c=DC, w=1)
        w2_1 = [arena[:, att_base + nw1 + n * 2048:att_base + nw1 + n * 2048 + 2048]
                .rearrange("p (e d) -> p e d", e=NX) for n in range(4)]
        assert att_base + nw1 + 8192 <= v_base

        def up_weights0(sp):
            for e in range(NX):
                for w, src in enumerate((g("L0_ffn_w1"), g("L0_ffn_v1"))):
                    sp.dma_start(wu0[:, e, :, w, :], src[e].rearrange("(c p) f -> p c f", p=P)).then_inc(sem("up0"), 16)
            down_weights0(sp, (4, 5))

        def down_weights0(sp, chunks):
            for n in chunks:
                r = min(P, F0 - n * P)
                sp.dma_start(w2_0[n][0:r, :, :], g("L0_ffn_w2")[:, n * P:n * P + r, :].rearrange("e p d -> p e d"))\
                    .then_inc(sem("down0"), 16)

        def weights1(sp):
            for e in range(NX):
                sp.dma_start(wu1[:, e, :, 0, :], g("L1_ffn_w1")[e].rearrange("(c p) f -> p c f", p=P))\
                    .then_inc(sem("up1"), 16)
            for n in range(4):
                sp.dma_start(w2_1[n], g("L1_ffn_w2")[:, n * P:n * P + P, :].rearrange("e p d -> p e d"))\
                    .then_inc(sem("down1"), 16)

        def weights0_wait(pe):
            pe.wait_ge(sem("up0"), 16 * 2 * NX)
            pe.wait_ge(sem("down0"), 16 * 6)

        def weights1_wait(pe):
            pe.wait_ge(sem("up1"), 16 * NX)
            pe.wait_ge(sem("down1"), 16 * 4)

        w = W["t0"]
        token_stage("t0", 0, "x", False, None,
                    [("qk", w["wq"], w["bq"], QSCALE, q_scr), ("qk", w["wk"], w["bk"], 1.0, k_scr),
                     ("v", w["wv"], w["bv"])], w)
        context_stage("ctx", 1, 2)
        attention_stage(Attention("at0", ("fwd", "bwd"), S, True, False, q_scr, k_scr, None))
        w = W["t1"]
        token_stage("t1", 2, "proj", True, None, [("qk", w["wq"], w["bq"], QSCALE, q_scr)], w,
                    extra_sp=lambda sp: load_context(sp, 0))
        attention_stage(Attention("xa0", ("full", "full"), SC, False, True, q_scr, kx_scr[0], 0))
        w = W["t2"]
        token_stage("t2", 3, "proj", True, None, [("logits", w["router"], logits)], w, extra_sp=up_weights0)
        routing_stage("rt0", x_tok, True, lambda sp: down_weights0(sp, (0, 1, 2, 3)))
        expert_stage("ex0", True, F0, wu0, w2_0, weights0_wait)
        gather_stage("ga0")
        w = W["t3"]
        token_stage("t3", 4, "comb", True, None,
                    [("qk", w["wq"], w["bq"], QSCALE, q_scr), ("qk", w["wk"], w["bk"], 1.0, k_scr),
                     ("v", w["wv"], w["bv"])], w)
        attention_stage(Attention("at1", ("full", "full"), S, False, False, q_scr, k_scr, None))
        w = W["t4"]
        token_stage("t4", 5, "proj", True, None, [("qk", w["wq"], w["bq"], QSCALE, q_scr)], w,
                    extra_sp=lambda sp: load_context(sp, 1))
        attention_stage(Attention("xa1", ("full", "full"), SC, False, False, q_scr, kx_scr[1], 1))
        w = W["t5"]
        token_stage("t5", 6, "proj", True, w["g1"],
                    [("latent", w["wdkv"]), ("qk", w["wq"], None, QSCALE, q_scr), ("klat", w["wuk"], k_scr),
                     ("vlat", w["wuv"])], w)
        attention_stage(Attention("mla", ("causal", "causal"), S, False, False, q_scr, k_scr, None))
        w = W["t6"]
        token_stage("t6", 7, "proj", False, w["g2"], [("logits", w["router"], logits)], w, x_out="add", rows_out=True,
                    extra_sp=weights1)
        routing_stage("rt1", v_tok.rearrange("p (t d) -> p t d", t=NT), False)
        expert_stage("ex1", False, F1, wu1, w2_1, weights1_wait)
        gather_stage("ga1")
        token_stage("t7", None, "comb", True, None, [], {}, x_out=False, final=True)

        family = {"t": "tok_", "c": "ctx_", "a": "att_", "x": "att_", "m": "att_", "r": "route_", "e": "experts_"}

        def run(eng, key):
            for n, (name, progs) in enumerate(stages):
                if n:
                    eng.wait_ge(stage_done, 5 * n)
                    if key == "pool":
                        kind = family.get(stages[n - 1][0][0])
                        for other, handle in sems.items():
                            if kind and other.startswith(kind):
                                eng.sem_clear(handle)
                if key in progs:
                    progs[key](eng)
                if n + 1 < len(stages):
                    eng.drain().then_inc(stage_done, 1)

        block = stack.enter_context(nc.Block())

        @block.sync
        def _(sp):
            run(sp, "sp")

        @block.tensor
        def _(pe):
            run(pe, "pe")

        @block.scalar
        def _(act):
            run(act, "act")

        @block.vector
        def _(dve):
            run(dve, "dve")

        @block.gpsimd
        def _(pool):
            run(pool, "pool")


NAMES = ['L0_attn_Wq', 'L0_attn_bq', 'L0_attn_Wk', 'L0_attn_bk', 'L0_attn_Wv', 'L0_attn_bv', 'L0_attn_Wf', 'L0_attn_bf',
         'L0_xattn_Wq', 'L0_xattn_bq', 'L0_xattn_Wk', 'L0_xattn_bk', 'L0_xattn_Wv', 'L0_xattn_bv', 'L0_xattn_Wo',
         'L0_xattn_bo', 'L0_ffn_router_w', 'L0_ffn_w1', 'L0_ffn_v1', 'L0_ffn_w2', 'L0_ffn_bias', 'L1_attn_W_qkv',
         'L1_attn_b_qkv', 'L1_attn_W_out', 'L1_attn_b_out', 'L1_xattn_wq', 'L1_xattn_bq', 'L1_xattn_wk', 'L1_xattn_bk',
         'L1_xattn_wv', 'L1_xattn_bv', 'L1_xattn_wo', 'L1_xattn_bo', 'L1_ffn_g1', 'L1_ffn_Wq', 'L1_ffn_Wdkv',
         'L1_ffn_Wuk', 'L1_ffn_Wuv', 'L1_ffn_Wo', 'L1_ffn_g2', 'L1_ffn_gate_w', 'L1_ffn_w1', 'L1_ffn_w2']


QK_NAMES = ('L0_attn_Wq', 'L0_attn_bq', 'L0_attn_Wk', 'L0_attn_bk', 'L0_xattn_Wq', 'L0_xattn_bq', 'L0_xattn_Wk',
            'L0_xattn_bk', 'L1_xattn_wq', 'L1_xattn_bq', 'L1_xattn_wk', 'L1_xattn_bk', 'L1_ffn_Wq', 'L1_ffn_Wuk')


def heads_inside(w):
    return np.ascontiguousarray(w.reshape(w.shape[:-1] + (-1, HG, HD)).swapaxes(-1, -2).reshape(w.shape))


def alibi_rows():
    bf = mybir.dt.np(BF16)
    half = H // 2
    slopes = 1.0 / (24.0 ** (1.0 / half)) ** np.arange(1, half + 1)
    rows = np.ones((2, 2, 2 * NB, 6, HG, S), bf)
    for slot in range(2):
        for i in range(2 * NB):
            for h in range(HG):
                value = slopes[HG * (i // NB) + h] * np.arange(S) * (-1.0 if slot else 1.0)
                for side, sign, at in ((0, -1.0, 0), (1, 1.0, 3)):
                    rest = sign * value
                    for n in range(3):
                        rows[side, slot, i, at + n, h] = rest.astype(bf)
                        rest = rest - rows[side, slot, i, at + n, h].astype(np.float64)
    return rows


def kernel(**inputs):
    import concourse.bacc as bacc
    from concourse.bass_utils import run_bass_kernel_spmd

    nc = bacc.Bacc("TRN2", target_bir_lowering=False, num_devices=1)
    x = np.asarray(inputs["x"])
    ctx = np.asarray(inputs["ctx_768"])
    arrays = {"x": x, "xT": np.ascontiguousarray(x.reshape(T, D).T),
              "ctxT": np.ascontiguousarray(ctx.reshape(NB * SC, CW).T),
              "alibi": alibi_rows(), "ones": np.ones((3, HG, S), mybir.dt.np(BF16)),
              "ones_x": np.ones((3, 2 * NB, HG * SC), mybir.dt.np(BF16))}
    for name in NAMES:
        arrays[name] = np.ascontiguousarray(inputs[name])
        if name in QK_NAMES:
            arrays[name] = heads_inside(arrays[name])
        elif name in ("L1_attn_W_qkv", "L1_attn_b_qkv"):
            arrays[name] = np.concatenate([heads_inside(arrays[name][..., 0:2 * D]), arrays[name][..., 2 * D:]], -1)
    aps = {name: nc.dram_tensor(f"in_{name}", v.shape, mybir.dt.from_np(v.dtype), kind="ExternalInput").ap()
           for name, v in arrays.items()}
    out = nc.dram_tensor("out", (NB, S, D), F32, kind="ExternalOutput").ap()
    build_decoder(nc, aps, out)
    r = run_bass_kernel_spmd(nc, [{f"in_{name}": v for name, v in arrays.items()}], core_ids=[0])
    return r.results[0]["out"]
```

```python
from contextlib import ExitStack

import numpy as np

import concourse.bass as bass
from concourse import mybir

F32 = mybir.dt.float32
BF16 = mybir.dt.bfloat16
I32 = mybir.dt.int32
U32 = mybir.dt.uint32
ACT = mybir.ActivationFunctionType
ALU = mybir.AluOpType
AX = mybir.AxisListType
ds = bass.ds

P = 128
NB, S, D = 2, 1024, 256
T = NB * S
NT = T // P
TPB = S // P
DC = D // P
H, HD = 16, 16
HG = 4
SC, CW = 154, 192
NX = 8
F0, F1 = 704, 512
NTILE = (2 * T + NX * (P - 1)) // P
NZERO = 3
assert NTILE % 2 == 1 and NTILE % NZERO == 0
NSLOT = NTILE * P
QSCALE = 1.0 / float(np.sqrt(HD))
NEG = -1e30
CLAMP = 10000.0
PARTS = ((3, 0), (2, 1), (1, 2))
STK = HD * sum(n for n, m in PARTS)
FIRST_MAX = 2
NPLACE = 4
EARLY = 3


def wait(eng, sem, value, start=0):
    if isinstance(value, int) and value <= 0:
        return
    eng.wait_ge(sem, start + value)


def hold(eng, sem, value, marker):
    eng.wait_ge(sem, value)
    eng.sem_inc(marker, 1)


def attention_units(mode, keys):
    units = []
    for qb in range(TPB):
        if keys < S:
            units.append((qb, (0, 1, 2, 3), 0, keys))
            continue
        lo = qb * P if mode == "bwd" else 0
        hi = (qb + 1) * P if mode in ("fwd", "causal") else keys
        if hi - lo <= 512:
            units += [(qb, (0, 1), lo, hi - lo), (qb, (2, 3), lo, hi - lo)]
        else:
            units += [(qb, (h,), lo, hi - lo) for h in range(HG)]
    return units


def attention_steps(mode, keys):
    steps = []
    for qh in range(2):
        blocks = range(-(-keys // P))
        if mode == "bwd":
            blocks = [b for b in reversed(blocks) if b >= 4 * qh]
        elif mode in ("fwd", "causal"):
            blocks = [b for b in blocks if b < 4 * qh + 4]
        blocks = list(blocks)
        for kb in blocks:
            c0, c1, diag = 0, 512, None
            d = kb - 4 * qh
            if mode in ("fwd", "causal") and d >= 0:
                c0, diag = d * P, d * P
            if mode == "bwd" and d < 4:
                c1, diag = (d + 1) * P, d * P
            steps.append((qh, kb, min(kb * P, keys - P), c0, c1, diag, kb == blocks[0], kb == blocks[-1]))
    return steps


def block_events(n_steps, half_end, n_units, first, lag, before, own=None):
    events, given, copied = [], 0, None
    if own:
        first = own[2]
    span = max(1, n_steps - 2 - first)

    def values(k):
        nonlocal copied
        old, k = k < lag, (before if k < lag else 0) + k - lag
        if k < 0:
            return
        events.append(("PV", k, old))
        if old and k == before - 1:
            events.append(("OC", 1, old))
            copied = (1, old)
        elif not old and k == half_end:
            events.append(("OC", 0, old))
            copied = (0, old)

    for k in range(n_steps):
        due = min(n_units, -(-n_units * max(0, k + 1 - first) // span))
        units = [("A", u) for u in range(given, due)]
        given = due
        if own and k < own[2]:
            lo, hi = (own[0] + (own[1] - own[0]) * n // own[2] for n in (k, k + 1))
            units = [("B", u) for u in range(lo, hi)]
        early = (len(units) + 1) // 2
        if k == 0:
            values(k)
            if own:
                events += units
                units = []
        events += [("ST", k, 0)] + units[0:1] + [("ST", k, 1)] + units[1:early]
        if own and k == own[2]:
            events += [("MT2",), ("MS2",)]
        if n_units and k == n_steps - 2:
            events += [("MT",), ("MS",)]
        if k > 0:
            values(k)
        units = units[early:]
        events += [("ST", k, 2)] + units[0:1] + [("ST", k, 3), ("CL", k)]
        if copied is not None:
            events += [("OT",) + copied] + units[1:] + [("ON",) + copied]
            copied = None
        else:
            events += units[1:]
    assert given == n_units
    return events


class Attention:

    def __init__(self, name, modes, keys, alibi, clip, q_scr, k_scr, vx):
        self.name, self.modes, self.keys = name, modes, keys
        self.alibi, self.clip = alibi, clip
        self.q_scr, self.k_scr, self.vx = q_scr, k_scr, vx
        self.kblocks = (keys + P - 1) // P
        self.mrow = STK + (6 if alibi else 0)
        self.units = [attention_units(m, keys) for m in modes]
        self.steps = [attention_steps(m, keys) for m in modes]
        self.nu = [len(u) for u in self.units]
        self.ns = [len(s) for s in self.steps]
        self.halved = int(keys == S)
        self.n_first = sum(u[0] < TPB // 2 for u in self.units[0]) if self.halved else self.nu[0]
        self.n_prob = 4
        self.lag = 2
        self.events = []
        for slot in range(2):
            ends = {k: s[0] for k, s in enumerate(self.steps[slot]) if s[7] and k + 1 < self.ns[slot]}
            (half_end,) = ends
            first = FIRST_MAX if keys == S else 0
            own = None
            if self.halved and slot == 0:
                own = (self.n_first, self.nu[0], min(half_end, 4))
            self.events.append([block_events(self.ns[slot], half_end, n, first, self.lag, before)
                                for n, before in ((self.nu[1 - slot], self.ns[1 - slot]), (0, self.ns[1 - slot]))] +
                               [block_events(self.ns[slot], half_end, self.nu[1 - slot], first, self.lag, 0, own)])
        self.last = [("PV", self.ns[1] - n, True) for n in range(self.lag, 0, -1)] + \
                    [("OC", 1, True), ("OT", 1, True), ("ON", 1, True)]
        self.loads = 9 + (2 if alibi else 0)

    def part(self, slot, k):
        return (k + (self.ns[0] if slot else 0)) % self.n_prob

    def unit(self, slot, i, k):
        return i * (self.nu[0] + self.nu[1]) + (self.nu[0] if slot else 0) + k

    def step(self, slot, i, k):
        return i * (self.ns[0] + self.ns[1]) + (self.ns[0] if slot else 0) + k


def build_decoder(nc, a, out):
    stack = ExitStack()
    with stack:
        words = 52900
        arena = stack.enter_context(nc.sbuf_tensor("arena", [P, words], F32))
        psum = stack.enter_context(nc.psum_tensor("psum", [P, 8 * 512], F32))
        bank = [psum[:, 512 * n:512 * n + 512] for n in range(8)]
        sems = {}

        def sem(name):
            if name not in sems:
                sems[name] = stack.enter_context(nc.semaphore(name))
            return sems[name]

        top = [0]

        def take(n):
            top[0] += n
            assert top[0] <= words, top[0]
            return arena[:, top[0] - n:top[0]]

        x_tok = take(NT * D).rearrange("p (t d) -> p t d", t=NT)
        ident = take(P)
        identb = take(P // 2).bitcast(BF16)
        mask_right = take(P // 2).bitcast(BF16)
        mask_left = take(P // 2).bitcast(BF16)
        lower = take(P // 2).bitcast(BF16)
        onesb = take(P // 2).bitcast(BF16)
        pick_max = take(P // 2).bitcast(BF16)
        minus_clamp = take(1)
        eps_col = take(1)
        halves = take(16)
        expert_rank = take(NT * NX).rearrange("p (t e) -> p t e", t=NT)
        slot_i = take(2 * NT).bitcast(I32).rearrange("p (k t) -> p k t", k=2)
        gate_w = take(2 * NT).rearrange("p (k t) -> p k t", k=2)
        tile_expert = take(NTILE).bitcast(I32)
        tile_no = take(NTILE)
        wslots = [take(2576) for _ in range(2)]
        tok_base = top[0]
        o_tok = take(NT * D)
        ats_base = top[0]
        ats = take(TPB * D).rearrange("p (t d) -> p t d", t=TPB)
        att = take(TPB * D).rearrange("p (t c q) -> p t c q", t=TPB, c=DC)
        w2_low = arena[:, tok_base:top[0]]
        r_tok = take(TPB * D).rearrange("p (t d) -> p t d", t=TPB)
        xts_flat = take(DC * S)
        xts = xts_flat.rearrange("p (c t) -> p c t", c=DC)
        floor_base = top[0]
        take(2 * 512)
        exp_base = top[0] - TPB * D - DC * S - 2 * 512
        route_base = top[0]
        u_f = take(2 * 512).rearrange("p (s t) -> p s t", s=2)
        parts = take(2 * 768).bitcast(BF16).rearrange("p (s k t) -> p s k t", s=2, k=3)
        mv = take(TPB * 2 * 2).rearrange("p (n t k) -> p n t k", n=2, t=TPB)
        bst = take(TPB * 2 * 6).rearrange("p (n t k) -> p n t k", n=2, t=TPB)
        rstd = take(TPB * 2).rearrange("p (n t) -> p n t", n=2)
        h_tok = ats
        lat = att.rearrange("p t c q -> p (t c q)")[:, 0:S]
        w2_high = take(2 * NX * D)
        att_base = top[0]
        stk = [[take(HG * S // 2).bitcast(BF16).rearrange("p (h t) -> p h t", h=HG) for _ in range(2)]
               for _ in range(2)]
        rest_base = top[0]
        prob = take(2 * HG * 512).rearrange("p (s h q) -> p s h q", s=2, h=HG)
        v_st = [take(TPB * HG * 32).rearrange("p (k h w) -> p k h w", k=TPB, h=HG) for _ in range(2)]
        stack_words = HG * S // 2
        floor_t = take(HG * 512).rearrange("p (h q) -> p h q", h=HG)
        o_sb = take(512)
        mstat = take(2 * 32).rearrange("p (s m) -> p s m", s=2)
        m_f = take(P)
        m_parts = take(3 * P // 2).bitcast(BF16).rearrange("p (k q) -> p k q", k=3)
        orec = take(16)
        v_base = top[0]
        v_tok = take(NT * D)
        q_all = [arena[:, at0:at0 + 4 * stack_words].bitcast(BF16).rearrange("p (i h t) -> p i h t", i=2 * NB, h=HG)
                 for at0 in (att_base, ats_base)]
        assert ats_base + 4 * stack_words <= top[0] and 4 * stack_words == 4 * TPB * D
        kx_words = 2 * NB * HG * SC // 2
        k_all = [v_tok[:, 1024 + n * kx_words:1024 + (n + 1) * kx_words].bitcast(BF16)
                 .rearrange("p (i h t) -> p i h t", i=2 * NB, h=HG) for n in range(2)]
        places = w2_high[:, 0:NPLACE * 768].bitcast(BF16).rearrange("p (s k t) -> p s k t", s=NPLACE, k=3)
        rest = arena[:, rest_base:rest_base + NPLACE * 512].rearrange("p (s t) -> p s t", s=NPLACE)
        zeros = arena[:, ats_base:ats_base + NSLOT // NZERO * D // P]
        assert NSLOT // NZERO * D // P <= 2 * TPB * D
        assert att_base + NX * DC * 2 * F0 <= words
        gathered = arena[:, att_base:att_base + 2 * NT * D].rearrange("p (k t d) -> p k t d", k=2, t=NT)

        def dram(name, shape, dt=F32):
            return nc.dram_tensor(name, shape, dt, kind="Internal").ap()

        q_scr = dram("q_parts", (2, 2, NB, 3 * 64, S), BF16)
        k_scr = dram("k_parts", (2, 2, NB, 3 * 64, S), BF16)
        kx_scr = [dram(f"kx_parts{n}", (2, 2, NB, 3 * 64, SC), BF16) for n in range(2)]
        vx_scr = [dram(f"vx{n}", (P, 4, 4, 64)) for n in range(2)]
        xs_scr = dram("slot_rows", (NSLOT, D))
        ys_scr = dram("slot_out", (NSLOT, D))

        stage_done = sem("stage_done")
        stages = []

        wdefs = []

        def weights(*items):
            w, at, views, loads = wslots[len(wdefs) % 2], 0, [], []
            for kind, src in items:
                if kind == "mat":
                    rows, cols = src.shape
                    c = (rows + P - 1) // P
                    v = w[:, at:at + c * cols].rearrange("p (c n) -> p c n", c=c)
                    at += c * cols
                    if rows % P:
                        for k in range(c):
                            n = min(P, rows - k * P)
                            loads.append((v[0:n, k, :], src[k * P:k * P + n, :]))
                    else:
                        loads.append((v, src.rearrange("(c p) n -> p c n", p=P)))
                elif kind == "row":
                    v = w[:, at:at + D]
                    at += D
                    loads.append((v, src.partition_broadcast(P)))
                else:
                    v = w[:, at:at + DC]
                    at += DC
                    loads.append((v, src.rearrange("(c p) -> p c", p=P)))
                views.append(v)
            assert at <= 2576, at
            wdefs.append(loads)
            return views

        def load_weights(sp, n):
            if n < len(wdefs):
                for dst, src in wdefs[n]:
                    sp.dma_start(dst, src, allow_slow_non_contiguous=True).then_inc(sem(f"weights{n}"), 16)

        def weights_ready(eng, n):
            eng.wait_ge(sem(f"weights{n}"), 16 * len(wdefs[n]))

        def setup_pool(pool):
            c0 = sem("const_base")
            nc.gpsimd.memset(ident, 0.0)
            nc.gpsimd.memset(lower, 1.0)
            nc.gpsimd.memset(onesb, 1.0)
            nc.gpsimd.memset(halves, -0.5)
            nc.gpsimd.memset(pick_max, 0.0)
            nc.gpsimd.memset(minus_clamp, -CLAMP)
            nc.gpsimd.memset(eps_col, 1e-5)
            nc.gpsimd.memset(mask_right, 0.0)
            nc.gpsimd.memset(mask_left, 0.0)
            nc.gpsimd.iota(tile_no.bitcast(I32), pattern=[[1, NTILE]], base=0, channel_multiplier=0)
            for e in range(NX):
                nc.gpsimd.memset(expert_rank[:, :, e:e + 1], float(NX - e))
            nc.gpsimd.memset(zeros, 0.0).then_inc(c0, 1)
            pool.wait_ge(c0, 1)
            nc.gpsimd.affine_select(out=ident, in_=ident, compare_op=ALU.not_equal, fill=1.0,
                                    base=0, pattern=[[-1, P]], channel_multiplier=1)
            nc.gpsimd.affine_select(out=lower, in_=lower, compare_op=ALU.is_gt, fill=0.0,
                                    base=0, pattern=[[1, P]], channel_multiplier=-1)
            nc.gpsimd.affine_select(out=mask_right, in_=mask_right, compare_op=ALU.is_ge, fill=NEG,
                                    base=0, pattern=[[-1, P]], channel_multiplier=1)
            nc.gpsimd.affine_select(out=mask_left, in_=mask_left, compare_op=ALU.is_ge, fill=NEG,
                                    base=0, pattern=[[1, P]], channel_multiplier=-1)\
                .then_inc(c0, 1)
            pool.wait_ge(c0, 2)
            nc.gpsimd.memset(pick_max[STK:STK + 3, :], 1.0).then_inc(c0, 1)
            pool.wait_ge(c0, 3)
            nc.gpsimd.tensor_copy(identb, ident)
            nc.gpsimd.tensor_copy(tile_no, tile_no.bitcast(I32)).then_inc(c0, 1)

        def setup_sp(sp):
            load_weights(sp, 0)

        def load_inputs(sp):
            load_context_rows(sp)
            sp.dma_start(x_tok, a["x"].rearrange("b (t p) d -> p (b t) d", p=P)).then_inc(sem("x_loaded"), 16)

        def zero_slots(sp):
            sp.wait_ge(sem("const_base"), 1)
            rows = NSLOT // NZERO
            for n in range(NZERO):
                sp.dma_start(xs_scr[n * rows:(n + 1) * rows, :].rearrange("(p r) d -> p (r d)", p=P),
                             zeros).then_inc(sem("slots_zeroed"), 16)

        stages.append(("setup", {"pool": setup_pool, "sp": setup_sp}))

        def load_queries(sp, at, s, i):
            if not (isinstance(i, int) and i == 0):
                sp.wait_ge(sem(f"att_ld{s}"), 48 * i)
            row = 0
            for n, _ in PARTS:
                sp.dma_start(q_all[s][row:row + 16 * n, ds(i, 1)].rearrange("p o h t -> p (o h) t"),
                             at.q_scr[s].rearrange("j b (k d h) t -> (j b) (k d) h t", k=3, h=HG)[ds(i, 1), 0:16 * n]
                             .rearrange("o d h t -> (o d) h t")).then_inc(sem(f"att_ld{s}"), 16)
                row += 16 * n

        def load_group(sp, at, s, i):
            q, k = stk[s]
            row = 0
            for n, part in PARTS:
                sp.dma_start(q[row:row + 16 * n, :, :],
                             at.q_scr[s].rearrange("j b (k d h) t -> (j b) (k d) h t", k=3, h=HG)[ds(i, 1), 0:16 * n]
                             .rearrange("o d h t -> (o d) h t")).then_inc(sem(f"att_ld{s}"), 16)
                for m in range(n):
                    sp.dma_start(k[row + 16 * m:row + 16 * m + 16, :, :],
                                 at.k_scr[s].rearrange("j b (k d h) t -> (j b) (k d) h t", k=3, h=HG)
                                 [ds(i, 1), 16 * part:16 * part + 16].rearrange("o d h t -> (o d) h t"))\
                        .then_inc(sem(f"att_ld{s}"), 16)
                row += 16 * n
            if at.alibi:
                for side in range(2):
                    sp.dma_start(stk[s][side][STK:STK + 6, :, :],
                                 a["alibi"][side, s, ds(i, 1), :, :, :].rearrange("o r h t -> (o r) h t"))\
                        .then_inc(sem(f"att_ld{s}"), 16)

        def load_ones(sp, at):
            for s in range(2):
                sp.dma_start(stk[s][1][at.mrow:at.mrow + 6, :, :], a["ones"]).then_inc(sem("att_ones"), 16)

        def load_first(sp, at):
            if at.keys < S:
                load_queries(sp, at, 0, 0)
            else:
                load_group(sp, at, 0, 0)

        def token_stage(name, wn, source, norm, rms, outs, w, x_out=True, rows_out=False, final=False,
                        early_sp=None, late_sp=None, following=None):
            def t(n):
                return sem(f"tok_{n}")

            wo = w.get("wo")
            work = []
            for half in range(2):
                for o in outs:
                    if o[0] in ("latent", "logits"):
                        work.append((o[0], o, None, half))
                    elif o[0] in ("qk", "klat"):
                        work += [(o[0], o, f, half) for f in range(2)]
                    elif o[0] in ("v", "vlat"):
                        work += [(o[0], o, None, p) for p in (2 * half, 2 * half + 1)]
            nw = len(work)
            assert nw % 2 == 0
            nqk = sum(k in ("qk", "klat") for k, *_ in work)
            qk_no = {}
            for k, (kind, *_) in enumerate(work):
                if kind in ("qk", "klat"):
                    qk_no[k] = len(qk_no)
            assert nqk % NPLACE == 0
            scratch_use = nqk // NPLACE
            lats = [k for k, x in enumerate(work) if x[0] == "latent"]
            half_work = [list(enumerate(work))[:nw // 2], list(enumerate(work))[nw // 2:]]
            tr_src = h_tok if rms is not None else r_tok
            n_pairs = TPB // 2
            has_in = source != "x"

            def load_xt(sp, b):
                sp.dma_start(xts, a["xT"][:, b * S:(b + 1) * S].rearrange("(c p) t -> p c t", p=P))\
                    .then_inc(t("xt_in"), 16)

            def sp_batch(sp, b):
                for p in range(n_pairs):
                    if has_in and norm and x_out:
                        sp.wait_ge(t("xs"), b * TPB + 2 * p + 2)
                        sp.dma_start(x_tok[:, ds(b * TPB + 2 * p, 2), :], r_tok[:, 2 * p:2 * p + 2, :])\
                            .then_inc(t("x_out"), 16)
                for p in range(n_pairs):
                    if rows_out:
                        sp.wait_ge(t("h"), b * TPB + 2 * p + 2)
                        sp.dma_start(v_tok.rearrange("p (t d) -> p t d", t=NT)[:, ds(b * TPB + 2 * p, 2), :],
                                     h_tok[:, 2 * p:2 * p + 2, :]).then_inc(t("rows_out"), 16)
                for k, n in qk_no.items():
                    kind, o, f, half = work[k]
                    sp.wait_ge(t("third"), NPLACE + b * nqk + n + 1)
                    dst = o[-1]
                    for j in range(2):
                        sp.dma_start(
                            dst[f, j, ds(b, 1), :, half * 512:half * 512 + 512]
                            .rearrange("o (k r) t -> r (o k) t", k=3),
                            places[j * 64:j * 64 + 64, n % NPLACE, :, :]).then_inc(t(f"scr{n % NPLACE}"), 16)
                if final:
                    for p in range(n_pairs):
                        sp.wait_ge(t("xs"), b * TPB + 2 * p + 2)
                        sp.dma_start(out[ds(b, 1), p * 256:p * 256 + 256, :]
                                     .rearrange("o (t p) d -> p (o t) d", p=P),
                                     r_tok[:, 2 * p:2 * p + 2, :]).then_inc(t("out"), 16)

            def sp_prog(sp):
                for n in [f"scr{s}" for s in range(NPLACE)] + ["out", "x_out", "rows_out"]:
                    sp.sem_inc(t(n), 1)
                if source == "x":
                    load_xt(sp, 0)
                if wn is not None:
                    load_weights(sp, wn + 1)
                if early_sp:
                    early_sp(sp)
                if source == "x":
                    sp_batch(sp, 0)
                    sp.wait_ge(t("work_ps"), 1 + nw)
                    load_xt(sp, 1)
                    sp_batch(sp, 1)
                elif following and source == "proj":
                    sp_batch(sp, 0)
                    for s in range(NPLACE):
                        sp.wait_ge(t(f"scr{s}"), 1 + 32 * scratch_use)
                    load_first(sp, following)
                    sp_batch(sp, 1)
                else:
                    with sp.Fori(0, NB) as b:
                        sp_batch(sp, b)
                    if following:
                        load_first(sp, following)
                if late_sp:
                    late_sp(sp)
                if has_in and norm and x_out:
                    sp.wait_ge(t("x_out"), 1 + 16 * NB * n_pairs)
                if rows_out:
                    sp.wait_ge(t("rows_out"), 1 + 16 * NB * n_pairs)
                for s in range(NPLACE if nqk else 0):
                    wait(sp, t(f"scr{s}"), 32 * NB * scratch_use, 1)
                if final:
                    sp.wait_ge(t("out"), 1 + 16 * NB * n_pairs)

            def pool_prog(pool):
                if source == "comb":
                    for n in range(TPB):
                        gather_rows(pool, 0, n)
                    later = list(range(TPB))
                    for k, n in qk_no.items():
                        pool_third(pool, 0, n)
                        for _ in range(-(-TPB // nqk)):
                            if later:
                                gather_rows(pool, 1, later.pop(0))
                    for n in later:
                        gather_rows(pool, 1, n)
                    for k, n in qk_no.items():
                        pool_third(pool, 1, n)
                    return
                with pool.Fori(0, NB) as b:
                    if has_in:
                        behind = 1 if norm else 0
                        for p in range(n_pairs + behind):
                            if p < n_pairs:
                                pool_norm(pool, b, p)
                            if rms is not None and p >= behind:
                                pool_rms(pool, b, p - behind)
                        if x_out == "add":
                            for p in range(n_pairs):
                                hold(pool, t("r"), 2 + b * n_pairs + p + 1, t("held_pool"))
                                xp = x_tok[:, ds(b * TPB + 2 * p, 2), :]
                                nc.gpsimd.tensor_tensor(xp, xp, r_tok[:, 2 * p:2 * p + 2, :], ALU.add)\
                                    .then_inc(t("pool_x"), 1)
                    for k, n in qk_no.items():
                        pool_third(pool, b, n)

            def gather_rows(pool, b, u):
                rows_in = sem(f"{name}_rows{u // 2}")
                if b and u % 2 == 0:
                    pool.wait_ge(rows_in, 64 * b)
                n = b * TPB + u
                for k in range(2):
                    nc.gpsimd.indirect_dma_start(
                        out=gathered[:, k, n, :], out_offset=None, in_=ys_scr,
                        in_offset=bass.IndirectOffsetOnAxis(ap=slot_i[:, k, n:n + 1].bitcast(U32), axis=0))\
                        .then_inc(rows_in, 16)

            def pool_third(pool, b, n):
                s = n % NPLACE
                pool.wait_ge(t("second"), b * nqk + n + 1)
                nc.gpsimd.tensor_tensor(places[:, s, 2, :], rest[:, s, :], places[:, s, 1, :],
                                        ALU.subtract).then_inc(t("third"), 1)

            def pool_norm(pool, b, p):
                if not norm:
                    return
                hold(pool, t("mv"), b * TPB + 2 * p + 2, t("held_pool"))
                nc.gpsimd.tensor_scalar(rstd[:, 0, 2 * p:2 * p + 2], mv[:, 0, 2 * p:2 * p + 2, 1], 1e-5, None,
                                        ALU.add).then_inc(t("pool_n"), 1)
                pool.wait_ge(t("pool_n"), b * 2 * n_pairs + 2 * p + 1)
                nc.gpsimd.tensor_tensor(rstd[:, 0, 2 * p:2 * p + 2], rstd[:, 0, 2 * p:2 * p + 2],
                                        halves[:, 0:2], ALU.pow).then_inc(t("pool_n"), 1)

            def pool_rms(pool, b, p):
                sl = slice(2 * p, 2 * p + 2)
                base = b * 4 * n_pairs + 4 * p
                pool.wait_ge(t("mv2"), b * TPB + 2 * p + 2)
                nc.gpsimd.tensor_tensor(rstd[:, 1, sl], mv[:, 1, sl, 0], mv[:, 1, sl, 0], ALU.mult)\
                    .then_inc(t("pool_r"), 1)
                pool.wait_ge(t("pool_r"), base + 1)
                nc.gpsimd.tensor_tensor(rstd[:, 1, sl], rstd[:, 1, sl], mv[:, 1, sl, 1], ALU.add)\
                    .then_inc(t("pool_r"), 1)
                hold(pool, t("pool_r"), base + 2, t("held_pool"))
                nc.gpsimd.tensor_scalar(rstd[:, 1, sl], rstd[:, 1, sl], 1e-6, None, ALU.add)\
                    .then_inc(t("pool_r"), 1)
                pool.wait_ge(t("pool_r"), base + 3)
                nc.gpsimd.tensor_tensor(rstd[:, 1, sl], rstd[:, 1, sl], halves[:, 0:2], ALU.pow)\
                    .then_inc(t("pool_r"), 1)

            def act_second(act, b, n):
                s = n % NPLACE
                act.wait_ge(t("rest_u"), b * nqk + n + 1)
                nc.scalar.activation(places[:, s, 1, :], rest[:, s, :], ACT.Copy).then_inc(t("second"), 1)

            def act_prog(act):
                act.sem_inc(t("att"), 2)
                act.sem_inc(t("xts"), 2)
                if wn is not None:
                    weights_ready(act, wn)
                with act.Fori(0, NB) as b:
                    def stage_rows(p):
                        nc.scalar.activation(
                            ats[:, 2 * p:2 * p + 2, :].rearrange("p u (g w) -> p u g w", g=4),
                            o_tok.rearrange("p (g n) -> p g n", g=4)[:, :, ds(b * (TPB * 64) + p * 128, 128)]
                            .rearrange("p g (u w) -> p u g w", u=2), ACT.Copy).then_inc(t("ats"), 1)

                    if source == "proj":
                        wait(act, t("prj_ps"), b * n_pairs, 1)
                        if lats:
                            wait(act, t("work_ps"), b * nw, 1)
                        if rms is not None:
                            wait(act, t("trx_ps"), b * n_pairs, 1)
                        if rows_out:
                            wait(act, t("rows_out"), 16 * b * n_pairs, 1)
                        stage_rows(0)
                        stage_rows(1)
                        for p in range(n_pairs):
                            act.wait_ge(t("tra_ps"), 1 + b * n_pairs + p + 1)
                            nc.scalar.activation(att[:, 2 * p:2 * p + 2, :, :].rearrange("p t c q -> p (t c q)"),
                                                 bank[p % 2][:, :], ACT.Copy).then_inc(t("att"), 1)
                            if p + 2 < n_pairs:
                                stage_rows(p + 2)
                    if source == "comb":
                        for p in range(n_pairs):
                            act.wait_ge(t("mv"), b * TPB + 2 * p + 2)
                            nc.scalar.activation(rstd[:, 0, 2 * p:2 * p + 2], mv[:, 0, 2 * p:2 * p + 2, 1], ACT.Sqrt,
                                                 bias=eps_col[:, 0:1]).then_inc(t("root"), 1)
                    if has_in and nw:
                        wait(act, t("work_ps"), b * nw, 1)
                    for half in range(2):
                        if has_in and nw:
                            for p in (2 * half, 2 * half + 1):
                                act.wait_ge(t("trx_ps"), 1 + b * n_pairs + p + 1)
                                nc.scalar.activation(
                                    xts[:, :, 256 * p:256 * p + 256].rearrange("p c (t q) -> p t c q", t=2),
                                    bank[4 + p % 2][:, :].rearrange("p (t c q) -> p t c q", t=2, c=DC),
                                    ACT.Copy).then_inc(t("xts"), 1)
                        waiting = None
                        for k, _ in half_work[half] if nw else ():
                            if k in lats:
                                act.wait_ge(t("work_ps"), 1 + b * nw + k + 1)
                                act.wait_ge(t("prj_ps"), 1 + (b + 1) * n_pairs)
                                nc.scalar.activation(lat[:, half * 512:half * 512 + 512], bank[6 + k % 2][:, :],
                                                     ACT.Copy).then_inc(t("lat"), 1)
                            elif k in qk_no:
                                n = qk_no[k]
                                s = n % NPLACE
                                uses = (n - s) // NPLACE
                                act.wait_ge(t("work_ps"), 1 + b * nw + k + 1)
                                wait(act, t(f"scr{s}"), (b * scratch_use + uses) * 32, 1)
                                kind, o, f, _ = work[k]
                                if kind == "qk" and o[2] is not None:
                                    nc.scalar.activation(places[:, s, 0, :], bank[6 + k % 2][:, :], ACT.Identity,
                                                         bias=o[2][:, f:f + 1]).then_inc(t("first"), 1)
                                else:
                                    nc.scalar.activation(places[:, s, 0, :], bank[6 + k % 2][:, :], ACT.Copy)\
                                        .then_inc(t("first"), 1)
                            if waiting is not None:
                                act_second(act, b, waiting)
                            waiting = qk_no.get(k)
                        if waiting is not None:
                            act_second(act, b, waiting)

            def pe_prog(pe):
                for n in ("tra_ps", "prj_ps", "trx_ps", "work_ps"):
                    pe.sem_inc(t(n), 1)
                weights_ready(pe, wn)
                with pe.Fori(0, NB) as b:
                    def tra(p):
                        for u in (2 * p, 2 * p + 1):
                            if u == 2 * p:
                                pe.wait_ge(t("ats"), b * n_pairs + p + 1)
                                pe.wait_ge(t("att"), 2 + b * n_pairs + p - 1)
                            for c in range(DC):
                                at = (u % 2) * D + c * P
                                last = nc.tensor.transpose(bank[p % 2][:, at:at + P], ats[:, u, c * P:c * P + P],
                                                           ident)
                        last.then_inc(t("tra_ps"), 1)

                    def prj(p):
                        pe.wait_ge(t("att"), 2 + b * n_pairs + p + 1)
                        pe.wait_ge(t("r"), 2 + b * n_pairs + p - 1)
                        for u in (2 * p, 2 * p + 1):
                            for c in range(DC):
                                last = nc.tensor.matmul(bank[2 + p % 2][:, (u % 2) * D:(u % 2) * D + D],
                                                        att[:, u, c, :], wo[:, c, :],
                                                        start=(c == 0), stop=(c == DC - 1))
                        last.then_inc(t("prj_ps"), 1)

                    if source == "proj":
                        tra(0)
                        tra(1)
                        for p in range(n_pairs):
                            prj(p)
                            if p + 2 < n_pairs:
                                tra(p + 2)
                    for half in range(2 if nw else 0):
                        for p in (2 * half, 2 * half + 1):
                            if not has_in:
                                continue
                            if rms is not None:
                                pe.wait_ge(t("h"), b * TPB + 2 * p + 2)
                            else:
                                pe.wait_ge(t("xs"), b * TPB + 2 * p + 2)
                            pe.wait_ge(t("xts"), 2 + b * n_pairs + p - 1)
                            for u in (2 * p, 2 * p + 1):
                                for c in range(DC):
                                    at = (u % 2) * D + c * P
                                    last = nc.tensor.transpose(bank[4 + p % 2][:, at:at + P],
                                                               tr_src[:, u, c * P:c * P + P], ident)
                            last.then_inc(t("trx_ps"), 1)
                        if has_in:
                            pe.wait_ge(t("xts"), 2 + b * n_pairs + 2 * half + 2)
                        elif half == 0:
                            pe.wait_ge(t("xt_in"), 16 * (b + 1))
                        for k, (kind, o, f, part) in half_work[half]:
                            pe.wait_ge(t("work_free"), 2 + b * nw + k - 1)
                            ps = bank[6 + k % 2]
                            mat = o[1]
                            if kind == "qk":
                                for c in range(DC):
                                    last = nc.tensor.matmul(ps[:, :], mat[:, c, f * P:f * P + P],
                                                            xts[:, c, part * 512:part * 512 + 512],
                                                            start=(c == 0), stop=(c == DC - 1))
                            elif kind == "latent":
                                for c in range(DC):
                                    last = nc.tensor.matmul(ps[:, :], mat[:, c, :],
                                                            xts[:, c, part * 512:part * 512 + 512],
                                                            start=(c == 0), stop=(c == DC - 1))
                            elif kind == "klat":
                                pe.wait_ge(t("lat"), b * 2 + part + 1)
                                last = nc.tensor.matmul(ps[:, :], mat[:, 0, f * P:f * P + P],
                                                        lat[:, part * 512:part * 512 + 512], start=True, stop=True)
                            elif kind == "vlat":
                                for u in (2 * part, 2 * part + 1):
                                    last = nc.tensor.matmul(ps[:, (u % 2) * D:(u % 2) * D + D],
                                                            lat[:, u * P:u * P + P], mat[:, 0, :],
                                                            start=True, stop=True)
                            elif kind == "v":
                                for u in (2 * part, 2 * part + 1):
                                    for c in range(DC):
                                        last = nc.tensor.matmul(ps[:, (u % 2) * D:(u % 2) * D + D],
                                                                xts[:, c, u * P:u * P + P], mat[:, c, :],
                                                                start=(c == 0), stop=(c == DC - 1))
                            elif kind == "logits":
                                for u in range(4 * part, 4 * part + 4):
                                    for c in range(DC):
                                        last = nc.tensor.matmul(ps[:, (u % 4) * NX:(u % 4) * NX + NX],
                                                                xts[:, c, u * P:u * P + P], mat[:, c, :],
                                                                start=(c == 0), stop=(c == DC - 1))
                            last.then_inc(t("work_ps"), 1)

            def dve_prog(dve):
                if wn is not None:
                    weights_ready(dve, wn)
                if has_in:
                    dve.sem_inc(t("r"), 2)
                if nw:
                    dve.sem_inc(t("work_free"), 2)
                with dve.Fori(0, NB) as b:
                    def add(p):
                        rp = r_tok[:, 2 * p:2 * p + 2, :]
                        rows = x_tok[:, ds(b * TPB + 2 * p, 2), :]
                        if p == 0:
                            if nw and rms is None:
                                wait(dve, t("trx_ps"), b * n_pairs, 1)
                            if x_out == "add":
                                wait(dve, t("pool_x"), b * n_pairs, 1)
                            elif x_out:
                                wait(dve, t("x_out"), 16 * b * n_pairs, 1)
                            if final:
                                wait(dve, t("out"), 16 * b * n_pairs, 1)
                        if source == "proj":
                            dve.wait_ge(t("prj_ps"), 1 + b * n_pairs + p + 1)
                            nc.vector.tensor_tensor(rp, bank[2 + p % 2][:, :].rearrange("p (t d) -> p t d", t=2),
                                                    rows, ALU.add).then_inc(t("r"), 1)
                        else:
                            dve.wait_ge(sem(f"{name}_rows{p}"), 64 * (b + 1))
                            for n in range(2):
                                for u in range(2):
                                    last = nc.vector.scalar_tensor_tensor(
                                        out=r_tok[:, 2 * p + u, :],
                                        in0=gathered[:, n, ds(b * TPB + 2 * p + u, 1), :].rearrange("p o d -> p (o d)"),
                                        scalar=gate_w[:, n, ds(b * TPB + 2 * p + u, 1)],
                                        in1=(x_tok[:, ds(b * TPB + 2 * p + u, 1), :].rearrange("p o d -> p (o d)")
                                             if n == 0 else r_tok[:, 2 * p + u, :]),
                                        op0=ALU.mult, op1=ALU.add)
                                    if n == 0:
                                        last.then_inc(t("first_row"), 1)
                                if n == 0:
                                    dve.wait_ge(t("first_row"), b * TPB + 2 * p + 2)
                            last.then_inc(t("r"), 1)

                    def moments(p, n, src, ready, value, done):
                        dve.wait_ge(ready, value)
                        for u in (2 * p, 2 * p + 1):
                            nc.vector.bn_stats(bst[:, n, u, :], src[:, u, :]).then_inc(t(f"st{n}"), 1)
                        for u in (2 * p, 2 * p + 1):
                            hold(dve, t(f"st{n}"), b * TPB + u + 1, t("held_dve"))
                            nc.vector.bn_aggr(mv[:, n, u, :], bst[:, n, u, :]).then_inc(t(done), 1)

                    def norm_rows(p):
                        if source == "comb":
                            dve.wait_ge(t("root"), b * n_pairs + p + 1)
                            nc.vector.reciprocal(rstd[:, 0, 2 * p:2 * p + 2], rstd[:, 0, 2 * p:2 * p + 2])\
                                .then_inc(t("inverse"), 1)
                            dve.wait_ge(t("inverse"), b * n_pairs + p + 1)
                        else:
                            dve.wait_ge(t("pool_n"), b * 2 * n_pairs + 2 * p + 2)
                        for u in (2 * p, 2 * p + 1):
                            nc.vector.tensor_scalar(r_tok[:, u, :], r_tok[:, u, :], mv[:, 0, u, 0:1],
                                                    rstd[:, 0, u:u + 1], ALU.subtract, ALU.mult)\
                                .then_inc(t("xs"), 1)

                    def rms_rows(p):
                        dve.wait_ge(t("pool_r"), b * 4 * n_pairs + 4 * p + 4)
                        if p == 0:
                            if source == "proj":
                                dve.wait_ge(t("tra_ps"), 1 + (b + 1) * n_pairs)
                        for u in (2 * p, 2 * p + 1):
                            nc.vector.scalar_tensor_tensor(out=h_tok[:, u, :], in0=r_tok[:, u, :],
                                                           scalar=rstd[:, 1, u:u + 1], in1=rms,
                                                           op0=ALU.mult, op1=ALU.mult).then_inc(t("h"), 1)

                    if has_in:
                        for p in range(n_pairs + 1):
                            if p < n_pairs:
                                add(p)
                                if norm:
                                    moments(p, 0, r_tok, t("r"), 2 + b * n_pairs + p + 1, "mv")
                                elif rms is not None:
                                    moments(p, 1, r_tok, t("r"), 2 + b * n_pairs + p + 1, "mv2")
                            if p >= 1 and norm:
                                norm_rows(p - 1)
                                if rms is not None:
                                    moments(p - 1, 1, r_tok, t("xs"), b * TPB + 2 * p, "mv2")
                            behind = 2 if norm else 1
                            if rms is not None and p >= behind:
                                rms_rows(p - behind)
                        if rms is not None and norm:
                            rms_rows(n_pairs - 1)
                    for k, (kind, o, f, half) in enumerate(work):
                        dve_unit(dve, b, k, kind, o, f, half)

            def dve_unit(dve, b, k, kind, o, f, half):
                if kind == "latent":
                    dve.wait_ge(t("lat"), b * 2 + lats.index(k) + 1)
                    dve.wait_ge(t("work_free"), 2 + b * nw + k)
                    dve.sem_inc(t("work_free"), 1)
                    return
                ps = bank[6 + k % 2]
                if kind in ("qk", "klat"):
                    n = qk_no[k]
                    s = n % NPLACE
                    dve.wait_ge(t("work_ps"), 1 + b * nw + k + 1)
                    dve.wait_ge(t("first"), b * nqk + n + 1)
                    dve.wait_ge(t("third"), b * nqk + n + 1)
                    bias = o[2] if kind == "qk" else None
                    if bias is None:
                        nc.vector.tensor_tensor(rest[:, s, :], ps[:, :], places[:, s, 0, :], ALU.subtract)\
                            .then_inc(t("rest_u"), 1)
                    else:
                        nc.vector.scalar_tensor_tensor(out=rest[:, s, :], in0=ps[:, :], scalar=bias[:, f:f + 1],
                                                       in1=places[:, s, 0, :], op0=ALU.add, op1=ALU.subtract)\
                            .then_inc(t("rest_u"), 1)
                    dve.wait_ge(t("rest_u"), b * nqk + n + 1)
                    dve.sem_inc(t("work_free"), 1)
                elif kind in ("v", "vlat"):
                    dve.wait_ge(t("work_ps"), 1 + b * nw + k + 1)
                    for u in range(2):
                        dst = v_tok.rearrange("p (g n) -> p g n", g=4)[:, :, ds(b * (TPB * 64) + (2 * half + u) * 64, 64)]
                        src = ps[:, u * D:u * D + D].rearrange("p (g w) -> p g w", g=4)
                        if kind == "v":
                            last = nc.vector.tensor_tensor(dst, src, o[2].rearrange("p (g w) -> p g w", g=4), ALU.add)
                        else:
                            last = nc.vector.tensor_copy(dst, src)
                    last.then_inc(t("work_free"), 1)
                elif kind == "logits":
                    dve.wait_ge(t("work_ps"), 1 + b * nw + k + 1)
                    nc.vector.tensor_copy(o[2][:, ds(b * TPB * NX + half * 4 * NX, 4 * NX)], ps[:, 0:4 * NX])\
                        .then_inc(t("work_free"), 1)

            def pool_wrapped(pool):
                pool.sem_inc(t("pool_x"), 1)
                if nqk:
                    pool.sem_inc(t("third"), NPLACE)
                pool_prog(pool)

            progs = {"sp": sp_prog, "dve": dve_prog, "pool": pool_wrapped}
            progs["act"] = act_prog
            if nw or source == "proj":
                progs["pe"] = pe_prog
            stages.append((name, progs))

        def load_context_rows(sp):
            ct = o_tok[:, 2048:2048 + 2 * NB * SC].rearrange("p (c t) -> p c t", c=2)
            for c, n in enumerate((P, CW - P)):
                sp.dma_start(ct[0:n, c, :], a["ctxT"][c * P:c * P + n, :]).then_inc(sem("ctx_in"), 16)

        def context_stage(name, wn, following):
            ct = o_tok[:, 2048:2048 + 2 * NB * SC].rearrange("p (c t) -> p c t", c=2)
            vx_t = o_tok[:, 0:2 * 1024].rearrange("p (l g n w) -> p l g n w", l=2, g=4, n=4)
            rows = (P, CW - P)
            n_tok = NB * SC

            def t(n):
                return sem(f"ctx_{n}")

            kunits = [(l, f) for l in range(2) for f in range(2)]
            vunits = [(l, b, kb) for l in range(2) for b in range(NB) for kb in range(2)]

            def sp_prog(sp):
                load_first(sp, following)
                load_weights(sp, wn + 1)
                for n, (l, f) in enumerate(kunits):
                    sp.wait_ge(t("third"), n + 1)
                    for j in range(2):
                        for b in range(NB):
                            sp.dma_start(kx_scr[l][f, j, b, :, :].rearrange("(k r) t -> r k t", k=3),
                                         parts[j * 64:j * 64 + 64, n % 2, :, b * SC:b * SC + SC])\
                                .then_inc(t(f"scr{n % 2}"), 16)
                sp.wait_ge(t("v"), len(vunits))
                few = SC - P
                for l in range(2):
                    for b in range(NB):
                        for row, kb, r0, r1 in ((0, 0, 0, P), (P - few, 1, 0, few), (0, 1, few, P)):
                            sp.dma_start(vx_scr[l][row:row + r1 - r0, :, 2 * b + kb, :],
                                         vx_t[r0:r1, l, :, 2 * b + kb, :]).then_inc(t("vstored"), 16)
                sp.wait_ge(t("vstored"), 16 * 12)
                for s in range(2):
                    sp.wait_ge(t(f"scr{s}"), 16 * 4 * 2)

            def pe_prog(pe):
                weights_ready(pe, wn)
                pe.wait_ge(t("in"), 32)
                for n, (l, f) in enumerate(kunits):
                    wait(pe, t("u"), n - 1)
                    for c in range(2):
                        last = nc.tensor.matmul(bank[n % 2][:, 0:n_tok], w_ctx[l]["wk"][0:rows[c], c, f * P:f * P + P],
                                                ct[0:rows[c], c, :], start=(c == 0), stop=(c == 1))
                    last.then_inc(t("k_ps"), 1)
                for n, (l, b, kb) in enumerate(vunits):
                    wait(pe, t("v"), n - 1)
                    k0, kn = b * SC + kb * P, min(P, SC - kb * P)
                    for c in range(2):
                        last = nc.tensor.matmul(bank[2 + n % 2][0:kn, 0:D], ct[0:rows[c], c, k0:k0 + kn],
                                                w_ctx[l]["wv"][0:rows[c], c, :], start=(c == 0), stop=(c == 1))
                    last.then_inc(t("v_ps"), 1)

            def act_prog(act):
                for n in range(len(kunits)):
                    s = n % 2
                    act.wait_ge(t("u"), n + 1)
                    wait(act, t(f"scr{s}"), (n // 2) * 64)
                    nc.scalar.activation(parts[:, s, 0, 0:n_tok], u_f[:, s, 0:n_tok], ACT.Copy).then_inc(t("first"), 1)
                    act.wait_ge(t("rest"), n + 1)
                    nc.scalar.activation(parts[:, s, 1, 0:n_tok], u_f[:, s, 0:n_tok], ACT.Copy).then_inc(t("second"), 1)

            def pool_prog(pool):
                for n in range(len(kunits)):
                    s = n % 2
                    pool.wait_ge(t("second"), n + 1)
                    nc.gpsimd.tensor_tensor(parts[:, s, 2, 0:n_tok], u_f[:, s, 0:n_tok], parts[:, s, 1, 0:n_tok],
                                            ALU.subtract).then_inc(t("third"), 1)

            def dve_prog(dve):
                weights_ready(dve, wn)
                nc.vector.memset(vx_t, 0.0).then_inc(t("zero"), 1)
                for n, (l, f) in enumerate(kunits):
                    s = n % 2
                    wait(dve, t("third"), n - 1)
                    dve.wait_ge(t("k_ps"), n + 1)
                    nc.vector.tensor_scalar(u_f[:, s, 0:n_tok], bank[s][:, 0:n_tok], w_ctx[l]["bk"][:, f:f + 1], None,
                                            ALU.add).then_inc(t("u"), 1)
                    dve.wait_ge(t("first"), n + 1)
                    nc.vector.tensor_tensor(u_f[:, s, 0:n_tok], u_f[:, s, 0:n_tok], parts[:, s, 0, 0:n_tok],
                                            ALU.subtract).then_inc(t("rest"), 1)
                dve.wait_ge(t("zero"), 1)
                for n, (l, b, kb) in enumerate(vunits):
                    kn = min(P, SC - kb * P)
                    dve.wait_ge(t("v_ps"), n + 1)
                    nc.vector.tensor_tensor(vx_t[0:kn, l, :, 2 * b + kb, :],
                                            bank[2 + n % 2][0:kn, 0:D].rearrange("p (g w) -> p g w", g=4),
                                            w_ctx[l]["bv"][0:kn, :].rearrange("p (g w) -> p g w", g=4), ALU.add)\
                        .then_inc(t("v"), 1)

            stages.append((name, {"sp": sp_prog, "pe": pe_prog, "act": act_prog, "pool": pool_prog, "dve": dve_prog}))

        def add_bias(pool, n, row):
            weights_ready(pool, n)
            pool.wait_ge(sem("x_loaded"), 16)
            for p in range(0, NT, 4):
                nc.gpsimd.tensor_tensor(x_tok[:, p:p + 4, :], x_tok[:, p:p + 4, :],
                                        row.unsqueeze(1).to_broadcast([P, 4, D]), ALU.add)\
                    .then_inc(sem("bias_added"), 1)

        def load_context(sp, n):
            done = sem(f"context{n}")
            sp.dma_start(v_tok[:, 0:1024], vx_scr[n].rearrange("p g n w -> p (g n w)")).then_inc(done, 16)
            for s in range(2):
                row = 0
                for n_parts, part in PARTS:
                    for r in range(n_parts):
                        sp.dma_start(k_all[s][row:row + 16].rearrange("p i h t -> p i (h t)"),
                                     kx_scr[n][s].rearrange("j b (r h) t -> r (j b) (h t)", h=HG)
                                     [16 * part:16 * part + 16]).then_inc(done, 16)
                        row += 16
                sp.dma_start(k_all[s][STK:STK + 3].rearrange("p i h t -> p i (h t)"), a["ones_x"])\
                    .then_inc(done, 16)

        def context_loaded(eng, n):
            eng.wait_ge(sem(f"context{n}"), 16 * 15)

        def attention_stage(at, bias=None, extra_sp=None):
            def t(n):
                return sem(f"att_{n}")

            keys, nkb = at.keys, at.kblocks
            vtiles = TPB if keys == S else 2
            probs = [prob[:, 0], prob[:, 1]] + [w2_high[:, n * HG * 512:(n + 1) * HG * 512]
                                                .rearrange("p (h q) -> p h q", h=HG) for n in range(2)]
            floors = [floor_t, arena[:, floor_base:floor_base + HG * 512].rearrange("p (h q) -> p h q", h=HG)]
            a_bank = (0, 2)
            st_bank = (4, 5)

            resident = keys < S

            def q_rows(s, i, row0, row1, h, lo, hi):
                if resident:
                    return q_all[s][row0:row1, ds(i, 1), h, lo:hi].rearrange("p o t -> p (o t)")
                return stk[s][0][row0:row1, h, lo:hi]

            def k_rows(s, i, row0, row1, h, lo, hi):
                if resident:
                    return k_all[s][row0:row1, ds(i, 1), h, lo:hi].rearrange("p o t -> p (o t)")
                return stk[s][1][row0:row1, h, lo:hi]

            halved = at.halved

            def load_max(sp, s, i, row=at.mrow, later=halved):
                sp.wait_ge(t("m_parts"), 2 * i + s + 1 + later)
                for n in range(3):
                    q = q_all[s][:, ds(i, 1)].rearrange("p o h t -> p (o h) t") if resident else stk[s][0]
                    sp.dma_start(q[row + n:row + n + 1, :, :].rearrange("o h (b q) -> o (h b) q", q=P),
                                 m_parts[0:32, n, :]).then_inc(t(f"mld{s}"), 16)

            def sp_resident(sp):
                load_queries(sp, at, 1, 0)
                load_max(sp, 0, 0)
                load_queries(sp, at, 0, 1)
                with sp.Fori(0, 2) as i:
                    load_max(sp, 1, i)
                    load_queries(sp, at, 1, i + 1)
                    load_max(sp, 0, i + 1)
                    load_queries(sp, at, 0, i + 2)
                load_max(sp, 1, 2)
                load_queries(sp, at, 1, 3)
                load_max(sp, 0, 3)
                load_max(sp, 1, 3)

            def sp_prog(sp):
                if resident:
                    return sp_resident(sp)
                load_ones(sp, at)
                load_group(sp, at, 1, 0)
                load_max(sp, 0, 0, later=0)
                load_max(sp, 0, 0, at.mrow + 3, 1)
                if extra_sp:
                    extra_sp(sp)
                with sp.Fori(0, 3) as i:
                    load_max(sp, 1, i)
                    sp.wait_ge(t("st_ps"), HG * at.step(0, i, at.ns[0]))
                    load_group(sp, at, 0, i + 1)
                    load_max(sp, 0, i + 1)
                    sp.wait_ge(t("st_ps"), HG * at.step(1, i, at.ns[1]))
                    load_group(sp, at, 1, i + 1)
                load_max(sp, 1, 3)
                if extra_sp:
                    sp.wait_ge(sem("slots_zeroed"), 16 * NZERO)

            def stage_values(s, i):
                src = v_tok[:, ds(i * (vtiles * 64) + s * (2 * NB * vtiles * 64), vtiles * 64)]
                nc.gpsimd.tensor_copy(v_st[s][:, 0:vtiles, :, 0:HD],
                                      src.rearrange("p (k h w) -> p k h w", k=vtiles, h=HG)).then_inc(t("vs"), 1)

            def pool_prog(pool):
                for s in range(2):
                    nc.gpsimd.memset(v_st[s][:, :, :, HD:2 * HD], 1.0).then_inc(t("columns"), 1)
                if keys < S:
                    pool.wait_ge(t("columns"), 2)
                    for s in range(2):
                        nc.gpsimd.memset(v_st[s][0:96, 1, :, HD:2 * HD], 0.0).then_inc(t("columns"), 1)
                        nc.gpsimd.memset(v_st[s][96:2 * P - keys, 1, :, HD:2 * HD], 0.0).then_inc(t("columns"), 1)
                    pool.wait_ge(t("columns"), 6)
                    context_loaded(pool, at.vx)
                stage_values(0, 0)
                stage_values(1, 0)
                if bias:
                    add_bias(pool, *bias)
                with pool.Fori(0, 3) as i:
                    for s in range(2):
                        pool.wait_ge(t("pv"), at.n_prob + at.step(s, i, at.ns[s]))
                        stage_values(s, i + 1)

            def pe_max(pe, s, i, k):
                qb, heads, key0, width = at.units[s][k]
                u = at.unit(s, i, k)
                par = (k + (at.nu[0] if s else 0)) % 2
                if k == 0:
                    pe.wait_ge(t(f"ld{s}"), (48 if resident else 16 * at.loads) * (i + 1))
                pe.wait_ge(t("a_max"), 2 + u - 1)
                rows = STK + (6 if at.alibi else 0)
                mode = at.modes[s]
                for n, h in enumerate(heads):
                    if keys < S:
                        spans = [(bank[a_bank[par] + n // 2][:, (n % 2) * 256:(n % 2) * 256 + width], 0, width)]
                    elif len(heads) == 2:
                        spans = [(bank[a_bank[par] + n][:, 0:width], 0, width)]
                    else:
                        spans = [(bank[a_bank[par]][:, 0:512], 0, 512),
                                 (bank[a_bank[par] + 1][:, 0:width - 512], 512, width)]
                    dcol = {"fwd": width - P, "causal": width - P, "bwd": 0}.get(mode)
                    for dst, lo, hi in spans:
                        masked = dcol is not None and lo <= dcol < hi
                        last = nc.tensor.matmul(dst, q_rows(s, i, 0, rows, h, qb * P, qb * P + P),
                                                k_rows(s, i, 0, rows, h, key0 + lo, key0 + hi), start=True, stop=not masked)
                        if masked:
                            m = mask_left if mode == "bwd" else mask_right
                            last = nc.tensor.matmul(dst[:, dcol - lo:dcol - lo + P], identb, m,
                                                    start=False, stop=True)
                last.then_inc(t("a_ps"), 1)

            def pe_scores(pe, s, i, k, hh):
                qh, kb, key0, c0, c1, diag, first, last_ = at.steps[s][k]
                u = at.step(s, i, k) * HG + hh
                par = hh % 2
                own = halved and s == 0 and isinstance(i, int) and i == 0
                if k == 0 and hh == 0:
                    pe.wait_ge(t(f"mld{s}"), 48 * (i + 1 + (halved if s == 0 and not own else 0)))
                if own and qh == 1 and first and hh == 0:
                    pe.wait_ge(t("mld0"), 96)
                if at.clip and (kb == 0) and hh == 0:
                    for h in range(HG):
                        idx = ((2 * i + s) * 2 + qh) * HG + h
                        if h < 2:
                            pe.wait_ge(t("p"), 2 + at.step(s, i, k) * HG + h - 1)
                        pe.wait_ge(t("fl"), 2 + idx - 1)
                        nc.tensor.matmul(bank[st_bank[h % 2]][:, :], pick_max[0:at.mrow + 3, :],
                                         q_rows(s, i, 0, at.mrow + 3, h, qh * 512, qh * 512 + 512),
                                         start=True, stop=True).then_inc(t("fl_ps"), 1)
                if at.clip and kb == 0 and hh < 2:
                    pe.wait_ge(t("fl"), 2 + ((2 * i + s) * 2 + qh) * HG + HG + hh - 1)
                else:
                    pe.wait_ge(t("p"), 2 + u - 1)
                dst = bank[st_bank[par]][:, c0:c1]
                rows = at.mrow + (6 if own and qh == 1 else 3)
                last = nc.tensor.matmul(dst, k_rows(s, i, 0, rows, hh, key0, key0 + P),
                                        q_rows(s, i, 0, rows, hh, qh * 512 + c0, qh * 512 + c1),
                                        start=True, stop=diag is None)
                if diag is not None:
                    m = mask_right if at.modes[s] == "bwd" else mask_left
                    last = nc.tensor.matmul(bank[st_bank[par]][:, diag:diag + P], identb, m, start=False, stop=True)
                last.then_inc(t("st_ps"), 1)

            def pe_values(pe, s, i, k):
                qh, kb, key0, c0, c1, diag, first, last_ = at.steps[s][k]
                n = at.step(s, i, k)
                place = at.part(s, k)
                if k == 0:
                    pe.wait_ge(t("vs"), 2 * i + s + 1)
                if first:
                    wait(pe, t("o_sb"), (2 * i + s) * 2 + qh, 1)
                if at.clip:
                    pe.wait_ge(t("clip"), nkb + 1 + n + 1)
                else:
                    pe.wait_ge(t("p"), 2 + n * HG + HG)
                for hh in range(HG):
                    last = nc.tensor.matmul(bank[6][32 * hh:32 * hh + 32, c0:c1], v_st[s][:, kb, hh, :],
                                            probs[place][:, hh, c0:c1], start=first, stop=last_)
                last.then_inc(t("pv"), 1)

            def group_of(s, i, old):
                return (s, i) if not old else ((0, i) if s else (1, i - 1))

            def pe_events(pe, ev, s, i, s2, i2, t0):
                use = 0
                for e in ev:
                    if e[0] == "A":
                        pe_max(pe, s2, i2, e[1])
                    elif e[0] == "B":
                        pe_max(pe, 0, 0, e[1])
                    elif e[0] == "ST":
                        pe_scores(pe, s, i, e[1], e[2])
                    elif e[0] == "PV":
                        pe_values(pe, *group_of(s, i, e[2]), e[1])
                    elif e[0] in ("MT", "MT1", "MT2"):
                        sm, im, nm = (s2, i2, at.nu[s2]) if e[0] == "MT" else (0, 0, {"MT1": at.n_first,
                                                                                     "MT2": at.nu[0]}[e[0]])
                        pe.wait_ge(t("a_max"), 2 + at.unit(sm, im, nm))
                        wait(pe, t("t_read"), t0 + use)
                        nc.tensor.transpose(bank[7][0:32, 0:P], mstat[:, sm, :], ident).then_inc(t("t_ps"), 1)
                        use += 1
                    elif e[0] == "OT":
                        so, io = group_of(s, i, e[2])
                        pe.wait_ge(t("o_sb"), 1 + (2 * io + so) * 2 + e[1] + 1)
                        wait(pe, t("t_read"), t0 + use)
                        for b in range(4):
                            last = nc.tensor.transpose(bank[7][:, b * P:b * P + P], o_sb[:, b * P:b * P + P], ident)
                        last.then_inc(t("t_ps"), 1)
                        use += 1

            def each_block(run):
                eng, block, prologue = run
                prologue(eng)
                block(eng, at.events[0][2], 0, 0, 1, 0, 1)
                with eng.Fori(0, 3) as i:
                    block(eng, at.events[1][0], 1, i, 0, i + 1, 3 + halved + 6 * i)
                    block(eng, at.events[0][0], 0, i + 1, 1, i + 1, 6 + halved + 6 * i)
                block(eng, at.events[1][1], 1, 3, None, None, 21 + halved)
                block(eng, at.last, 0, 4, None, None, 23 + halved)

            def pe_prog(pe):
                def prologue(pe):
                    if resident:
                        context_loaded(pe, at.vx)
                    for k in range(at.n_first):
                        pe_max(pe, 0, 0, k)
                    if not resident:
                        pe.wait_ge(t("ones"), 32)
                    pe_events(pe, [("MT1",)], None, None, 0, 0, 0)
                each_block((pe, pe_events, prologue))

            def act_events(act, ev, s, i, s2, i2, t0):
                for e in ev:
                    if e[0] != "ST":
                        continue
                    k, hh = e[1], e[2]
                    qh, kb, key0, c0, c1, diag, first, last_ = at.steps[s][k]
                    n = at.step(s, i, k)
                    if at.clip and kb == 0 and hh == 0:
                        for h in range(HG):
                            idx = ((2 * i + s) * 2 + qh) * HG + h
                            act.wait_ge(t("fl_ps"), idx + 1)
                            if h == 0:
                                act.wait_ge(t("clip"), n + 1)
                            nc.scalar.activation(floors[qh][:, h, :], bank[st_bank[h % 2]][:, :], ACT.Exp,
                                                 bias=minus_clamp[:, 0:1], scale=QSCALE).then_inc(t("fl"), 1)
                    if hh == 0:
                        act.wait_ge(t("pv"), n + 1)
                    act.wait_ge(t("st_ps"), n * HG + hh + 1)
                    src = bank[st_bank[hh % 2]][:, c0:c1]
                    nc.scalar.activation(probs[at.part(s, k)][:, hh, c0:c1], src, ACT.Exp, scale=QSCALE)\
                        .then_inc(t("p"), 1)

            def act_prog(act):
                act.sem_inc(t("p"), 2)
                if at.clip:
                    act.sem_inc(t("fl"), 2)
                each_block((act, act_events, lambda act: None))

            def dve_max(dve, s, i, k):
                qb, heads, key0, width = at.units[s][k]
                u = at.unit(s, i, k)
                par = (k + (at.nu[0] if s else 0)) % 2
                dve.wait_ge(t("a_ps"), u + 1)
                both = psum[:, 1024 * par:1024 * par + 1024]
                if keys < S:
                    src = both.rearrange("p (h k) -> p h k", h=HG)[:, :, 0:width]
                elif len(heads) == 2:
                    src = both.rearrange("p (h k) -> p h k", h=2)[:, :, 0:width]
                else:
                    src = both[:, 0:width].unsqueeze(1)
                dst = mstat[:, s, :].rearrange("p (h b) -> p h b", h=HG)[:, heads[0]:heads[-1] + 1, qb]
                nc.vector.tensor_reduce(dst, src, AX.X, ALU.max).then_inc(t("a_max"), 1)

            def dve_events(dve, ev, s, i, s2, i2, t0):
                use = 0
                for e in ev:
                    if e[0] == "A":
                        dve_max(dve, s2, i2, e[1])
                    elif e[0] == "B":
                        dve_max(dve, 0, 0, e[1])
                    elif e[0] == "CL" and at.clip:
                        k = e[1]
                        qh, kb, key0, c0, c1, diag, first, last_ = at.steps[s][k]
                        n = at.step(s, i, k)
                        place = probs[at.part(s, k)]
                        if kb == 0:
                            dve.wait_ge(t("fl"), 2 + ((2 * i + s) * 2 + qh) * HG + HG)
                        dve.wait_ge(t("p"), 2 + n * HG + HG)
                        nc.vector.scalar_tensor_tensor(out=place, in0=place,
                                                       scalar=1.0, in1=floors[qh],
                                                       op0=ALU.min, op1=ALU.max).then_inc(t("clip"), 1)
                    elif e[0] == "OC":
                        so, io = group_of(s, i, e[2])
                        ends = [k for k, x in enumerate(at.steps[so]) if x[7]]
                        n = at.step(so, io, ends[e[1]])
                        dve.wait_ge(t("pv"), at.n_prob + n + 1)
                        nc.vector.tensor_copy(o_sb, bank[6][:, :]).then_inc(t("o_sb"), 1)
                    elif e[0] in ("MS", "MS1", "MS2"):
                        g = {"MS1": 0, "MS2": 1}.get(e[0])
                        if g is None:
                            g = 2 * i2 + s2 + halved
                        dve.wait_ge(t("t_ps"), t0 + use + 1)
                        if e[0] == "MS2":
                            dve.wait_ge(t("mld0"), 48)
                        elif e[0] == "MS":
                            before = 48 * (i2 + 1 + halved) if s2 else 48 * i2
                            dve.wait_ge(t(f"mld{1 - s2}"), before)
                        if at.clip:
                            nc.vector.tensor_scalar(m_f[0:32, :], bank[7][0:32, 0:P], -CLAMP / QSCALE,
                                                    CLAMP / QSCALE, ALU.max, ALU.min)\
                                .then_inc(t("m_step"), 1)
                            dve.wait_ge(t("m_step"), MS * g + 1)
                            nc.vector.tensor_scalar(m_f[0:32, :], m_f[0:32, :], -1.0, None, ALU.mult)\
                                .then_inc(t("m_step"), 1)
                            at0 = 2
                        else:
                            nc.vector.tensor_scalar(m_f[0:32, :], bank[7][0:32, 0:P], -1.0, None, ALU.mult)\
                                .then_inc(t("m_step"), 1)
                            at0 = 1
                        dve.wait_ge(t("m_step"), MS * g + at0)
                        dve.sem_inc(t("t_read"), 1)
                        nc.vector.tensor_copy(m_parts[0:32, 0, :], m_f[0:32, :]).then_inc(t("m_step"), 1)
                        dve.wait_ge(t("m_step"), MS * g + at0 + 1)
                        nc.vector.tensor_tensor(m_f[0:32, :], m_f[0:32, :], m_parts[0:32, 0, :], ALU.subtract)\
                            .then_inc(t("m_step"), 1)
                        dve.wait_ge(t("m_step"), MS * g + at0 + 2)
                        nc.vector.tensor_copy(m_parts[0:32, 1, :], m_f[0:32, :]).then_inc(t("m_step"), 1)
                        dve.wait_ge(t("m_step"), MS * g + at0 + 3)
                        nc.vector.tensor_tensor(m_parts[0:32, 2, :], m_f[0:32, :], m_parts[0:32, 1, :], ALU.subtract)\
                            .then_inc(t("m_parts"), 1)
                        use += 1
                    elif e[0] == "ON":
                        so, io = group_of(s, i, e[2])
                        g2 = (2 * io + so) * 2 + e[1]
                        dve.wait_ge(t("t_ps"), t0 + use + 1)
                        sums = bank[7][:, :].rearrange("p (n w) -> p n w", w=32)
                        nc.vector.reciprocal(orec, sums[:, :, HD]).then_inc(t("rec"), 1)
                        dve.wait_ge(t("rec"), g2 + 1)
                        dst = o_tok[:, ds(io * (TPB * 64) + so * (2 * NB * TPB * 64) + e[1] * 256, 256)]
                        nc.vector.tensor_tensor(dst.rearrange("p (n w) -> p n w", w=HD), sums[:, :, 0:HD],
                                                orec.unsqueeze(2).to_broadcast([P, 16, HD]), ALU.mult)\
                            .then_inc(t("t_read"), 1)
                        use += 1

            MS = 5 if at.clip else 4

            def dve_prog(dve):
                dve.sem_inc(t("a_max"), 2)
                dve.sem_inc(t("o_sb"), 1)
                dve.sem_inc(t("clip"), nkb + 1)

                def prologue(dve):
                    if halved:
                        nc.vector.memset(mstat[:, 0, :], 0.0).then_inc(t("cleared"), 1)
                        dve.wait_ge(t("cleared"), 1)
                    for k in range(at.n_first):
                        dve_max(dve, 0, 0, k)
                    dve_events(dve, [("MS1",)], None, None, 0, 0, 0)
                each_block((dve, dve_events, prologue))

            def pe_wrapped(pe):
                pe.sem_inc(t("pv"), at.n_prob)
                pe_prog(pe)

            stages.append((at.name, {"sp": sp_prog, "pool": pool_prog, "pe": pe_wrapped, "act": act_prog,
                                     "dve": dve_prog}))

        scratch = arena[:, route_base:route_base + 20 * NT * NX]

        def routing_stage(name, rows, soft_all, extra_sp=None):
            def t(n):
                return sem(f"route_{n}")

            def tile_of(n, k=NX):
                return scratch[:, n * NT * NX:n * NT * NX + NT * k].rearrange("p (t e) -> p t e", t=NT)

            lg, tmp, oh1, lg2, oh2, ex, pos = (tile_of(n) for n in range(7))
            acc = scratch[:, 8 * 128:8 * 128 + (NT + 1) * NX].rearrange("p (t e) -> p t e", t=NT + 1)
            acc2 = scratch[:, 17 * 128:17 * 128 + (NT + 1) * NX].rearrange("p (t e) -> p t e", t=NT + 1)
            small = scratch[:, 10 * 128:11 * 128]
            m1, m2, mr, e2, den, s1 = (small[:, n * NT:n * NT + NT] for n in range(6))
            few = scratch[:, 11 * 128:11 * 128 + 64]
            tiles_f, tiles_i, start, base = (few[:, n * 8:n * 8 + 8] for n in (0, 1, 2, 3))
            tiles_i = tiles_i.bitcast(I32)
            ohb = scratch[:, 12 * 128:12 * 128 + 64].bitcast(BF16)
            cmp = scratch[:, 13 * 128:13 * 128 + NTILE * (NX - 1)].rearrange("p (n e) -> p n e", n=NTILE)
            te_f = scratch[:, 16 * 128:16 * 128 + NTILE]

            def over_e(v):
                return v.unsqueeze(2).to_broadcast([P, NT, NX])

            def dve_prog(dve):
                done = [0]

                def then(ins):
                    done[0] += 1
                    ins.then_inc(t("step"), 1)
                    dve.wait_ge(t("step"), done[0])

                V = nc.vector
                for src, m, oh in ((lg, m1, oh1), (lg2, m2, oh2)):
                    then(V.tensor_reduce(m, src, AX.X, ALU.max))
                    then(V.tensor_tensor(tmp, src, over_e(m), ALU.is_equal))
                    then(V.tensor_tensor(tmp, tmp, expert_rank, ALU.mult))
                    then(V.tensor_reduce(mr, tmp, AX.X, ALU.max))
                    then(V.tensor_tensor(oh, expert_rank, over_e(mr), ALU.is_equal))
                    if oh is oh1:
                        then(V.scalar_tensor_tensor(out=lg2, in0=oh1, scalar=-3e38, in1=lg,
                                                    op0=ALU.mult, op1=ALU.add))
                V.tensor_tensor(ohb.rearrange("p (t e) -> p t e", t=NT), oh1, oh2, ALU.add).then_inc(t("oh"), 1)
                if soft_all:
                    V.tensor_tensor(ex, lg, over_e(m1), ALU.subtract).then_inc(t("ex_in"), 1)
                V.tensor_tensor(e2, m2, m1, ALU.subtract).then_inc(t("ex_in"), 1)
                dve.wait_ge(t("rank_ps"), 1)
                V.memset(acc[:, 0, :], 0.0).then_inc(t("zero"), 1)
                then(V.tensor_copy(acc[:, 1:NT + 1, :].rearrange("p t e -> p (t e)"), bank[0][:, 0:P]))
                src, dst = acc, acc2
                d = 1
                while d < NT:
                    V.tensor_copy(dst[:, 0:d + 1, :], src[:, 0:d + 1, :]).then_inc(t("zero"), 1)
                    then(V.tensor_tensor(dst[:, d + 1:NT + 1, :], src[:, d + 1:NT + 1, :], src[:, 1:NT + 1 - d, :],
                                         ALU.add))
                    dve.wait_ge(t("zero"), 1 + d.bit_length())
                    src, dst, d = dst, src, 2 * d
                sums = src
                then(V.tensor_scalar(tiles_i, sums[:, NT, :], float(P - 1), None, ALU.add))
                then(V.tensor_scalar(tiles_i, tiles_i, 7, None, ALU.arith_shift_right))
                then(V.tensor_copy(tiles_f, tiles_i))
                then(V.memset(start[:, 0:1], 0.0))
                for e in range(NX - 1):
                    then(V.tensor_tensor(start[:, e + 1:e + 2], start[:, e:e + 1], tiles_f[:, e:e + 1], ALU.add))
                then(V.tensor_scalar(base, start, float(P), None, ALU.mult))
                then(V.tensor_tensor(pos.rearrange("p t e -> p (t e)"), bank[0][:, P:2 * P],
                                     sums[:, 0:NT, :].rearrange("p t e -> p (t e)"), ALU.add))
                then(V.tensor_tensor(pos, pos, base.unsqueeze(1).to_broadcast([P, NT, NX]), ALU.add))
                for k, oh in enumerate((oh1, oh2)):
                    then(V.tensor_tensor(tmp, pos, oh, ALU.mult))
                    then(V.tensor_reduce(s1, tmp, AX.X, ALU.add))
                    then(V.tensor_copy(slot_i[:, k, :], s1))
                    dve.sem_inc(t("slots"), 1)
                then(V.tensor_tensor(cmp, tile_no.unsqueeze(2).to_broadcast([P, NTILE, NX - 1]),
                                     start[:, 1:NX].unsqueeze(1).to_broadcast([P, NTILE, NX - 1]), ALU.is_ge))
                then(V.tensor_reduce(te_f, cmp, AX.X, ALU.add))
                then(V.tensor_copy(tile_expert, te_f))
                dve.wait_ge(t("ex_out"), 2 if soft_all else 1)
                if soft_all:
                    then(V.tensor_reduce(den, ex, AX.X, ALU.add))
                else:
                    then(V.tensor_scalar(den, e2, 1.0, None, ALU.add))
                then(V.reciprocal(gate_w[:, 0, :], den))
                then(V.tensor_tensor(gate_w[:, 1, :], gate_w[:, 0, :], e2, ALU.mult))

            def pe_prog(pe):
                pe.wait_ge(t("oh"), 1)
                nc.tensor.matmul(bank[0][:, 0:P], onesb, ohb, start=True, stop=True)
                nc.tensor.matmul(bank[0][:, P:2 * P], lower, ohb, start=True, stop=True).then_inc(t("rank_ps"), 1)

            def act_prog(act):
                for n, v in enumerate(([ex] if soft_all else []) + [e2]):
                    act.wait_ge(t("ex_in"), n + 1)
                    nc.scalar.activation(v, v, ACT.Exp).then_inc(t("ex_out"), 1)

            def pool_prog(pool):
                for k in range(2):
                    pool.wait_ge(t("slots"), k + 1)
                    for n in range(NT):
                        nc.gpsimd.indirect_dma_start(
                            out=xs_scr, out_offset=bass.IndirectOffsetOnAxis(ap=slot_i[:, k, n:n + 1].bitcast(U32), axis=0),
                            in_=rows[:, n, :], in_offset=None).then_inc(sem(f"{name}_scattered"), 16)
                pool.wait_ge(sem(f"{name}_scattered"), 16 * 2 * NT)

            progs = {"dve": dve_prog, "pe": pe_prog, "act": act_prog, "pool": pool_prog}
            if extra_sp:
                progs["sp"] = extra_sp
            stages.append((name, progs))

        def expert_stage(name, gated, F, wu, w2, weights_wait, bias=None):
            def t(n):
                return sem(f"experts_{n}")

            nf = (F + P - 1) // P
            fw = [min(P, F - n * P) for n in range(nf)]
            half = F // 2 if F > 512 else F
            nh = F // half
            at = [exp_base]

            def buf(n):
                at[0] += n
                return arena[:, at[0] - n:at[0]]

            xin = buf(2 * D).rearrange("p (s d) -> p s d", s=2)
            xT = buf(2 * D).rearrange("p (s c q) -> p s c q", s=2, c=DC)
            yo = buf(2 * D).rearrange("p (s d) -> p s d", s=2)
            gl, hs = buf(F), buf(F)
            hT = buf(2 * nf * P).rearrange("p (s n q) -> p s n q", s=2, n=nf)
            assert at[0] <= route_base

            def sp_load(sp, n, s):
                sp.dma_start(xin[:, s, :], xs_scr[ds(n * P, P), :]).then_inc(t(f"in{s}"), 16)

            def sp_store(sp, n, s):
                sp.wait_ge(t("y"), 1 + n + 1)
                sp.dma_start(ys_scr[ds(n * P, P), :], yo[:, s, :]).then_inc(t(f"st{s}"), 16)

            def sp_prog(sp):
                for s in range(2):
                    sp.sem_inc(t(f"st{s}"), 1)
                def next_load(n, s):
                    sp.wait_ge(t("xT_ps"), n + 1)
                    sp_load(sp, n + 2, s)

                sp_load(sp, 0, 0)
                sp_load(sp, 1, 1)
                next_load(0, 0)
                with sp.Fori(0, (NTILE - 3) // 2) as i:
                    for s in range(2):
                        next_load(2 * i + 1 + s, 1 - s)
                        sp_store(sp, 2 * i + s, s)
                for n in range(NTILE - 3, NTILE):
                    sp_store(sp, n, n % 2)
                for s in range(2):
                    sp.wait_ge(t(f"st{s}"), 1 + 16 * ((NTILE + 1 - s) // 2))

            def pe_xt(pe, n, s, n2):
                pe.wait_ge(t(f"in{s}"), 16 * (n2 + 1))
                wait(pe, t("xT"), n)
                for c in range(DC):
                    last = nc.tensor.transpose(bank[6][:, c * P:c * P + P], xin[:, s, c * P:c * P + P], ident)
                last.then_inc(t("xT_ps"), 1)

            def pe_up(pe, n, s):
                e = pe.value_load(tile_expert[0:1, ds(n, 1)], min_val=0, max_val=NX - 1)
                pe.wait_ge(t("xT"), n + 1)
                wait(pe, t("g" if gated else "h"), n)
                for w in range(2 if gated else 1):
                    if w == 1:
                        wait(pe, t("h"), n)
                    for hf in range(nh):
                        for c in range(DC):
                            last = nc.tensor.matmul(
                                bank[2 * w + hf][:, 0:half], xT[:, s, c, :],
                                wu[:, ds(e, 1), c, w, hf * half:hf * half + half].rearrange("p o f -> p (o f)"),
                                start=(c == 0), stop=(c == DC - 1))
                    last.then_inc(t("up"), 1)

            def pe_ht(pe, n):
                pe.wait_ge(t("h"), n + 1)
                wait(pe, t("hT"), n)
                for f in range(nf):
                    last = nc.tensor.transpose(bank[4 + f // 4][0:fw[f], (f % 4) * P:(f % 4) * P + P],
                                               hs[:, f * P:f * P + fw[f]], ident)
                last.then_inc(t("hT_ps"), 1)

            def pe_down(pe, n, s):
                e = pe.value_load(tile_expert[0:1, ds(n, 1)], min_val=0, max_val=NX - 1)
                pe.wait_ge(t("hT"), n + 1)
                wait(pe, t("y"), n, 1)
                for f in range(nf):
                    last = nc.tensor.matmul(bank[7][:, 0:D], hT[0:fw[f], s, f, :],
                                            w2[f][0:fw[f], ds(e, 1), :].rearrange("p o d -> p (o d)"),
                                            start=(f == 0), stop=(f == nf - 1))
                last.then_inc(t("y_ps"), 1)

            def pe_prog(pe):
                weights_wait(pe)
                pe.sem_inc(t("y_ps"), 1)
                pe_xt(pe, 0, 0, 0)
                pe_up(pe, 0, 0)
                pe_xt(pe, 1, 1, 0)
                pe_ht(pe, 0)
                with pe.Fori(0, (NTILE - 3) // 2) as i:
                    pe_up(pe, 2 * i + 1, 1)
                    pe_xt(pe, 2 * i + 2, 0, i + 1)
                    pe_down(pe, 2 * i, 0)
                    pe_ht(pe, 2 * i + 1)
                    pe_up(pe, 2 * i + 2, 0)
                    pe_xt(pe, 2 * i + 3, 1, i + 1)
                    pe_down(pe, 2 * i + 1, 1)
                    pe_ht(pe, 2 * i + 2)
                pe_up(pe, NTILE - 2, 1)
                pe_xt(pe, NTILE - 1, 0, (NTILE - 1) // 2)
                pe_down(pe, NTILE - 3, 0)
                pe_ht(pe, NTILE - 2)
                pe_up(pe, NTILE - 1, 0)
                pe_down(pe, NTILE - 2, 1)
                pe_ht(pe, NTILE - 1)
                pe_down(pe, NTILE - 1, 0)

            up = 2 if gated else 1

            def act_xt(act, n, s):
                act.wait_ge(t("xT_ps"), n + 1)
                wait(act, t("up"), (n - 1) * up)
                nc.scalar.activation(xT[:, s, :, :].rearrange("p c q -> p (c q)"), bank[6][:, 0:D], ACT.Copy)\
                    .then_inc(t("xT"), 1)

            def act_hidden(act, n):
                act.wait_ge(t("up"), n * up + 1)
                if gated:
                    wait(act, t("h"), n)
                    nc.scalar.activation(gl.rearrange("p (h f) -> p h f", h=nh),
                                         psum[:, 0:1024].rearrange("p (h f) -> p h f", h=2)[:, :, 0:half],
                                         ACT.Gelu).then_inc(t("g"), 1)
                else:
                    wait(act, t("hT_ps"), n)
                    nc.scalar.activation(hs, bank[0][:, 0:F], ACT.Silu).then_inc(t("h"), 1)

            def act_out(act, n, s, n2):
                act.wait_ge(t("y_ps"), 1 + n + 1)
                wait(act, t(f"st{s}"), 16 * n2, 1)
                nc.scalar.activation(yo[:, s, :], bank[7][:, 0:D], ACT.Copy).then_inc(t("y"), 1)

            def act_prog(act):
                act.sem_inc(t("y"), 1)
                act_xt(act, 0, 0)
                act_hidden(act, 0)
                act_xt(act, 1, 1)
                with act.Fori(0, (NTILE - 3) // 2) as i:
                    act_hidden(act, 2 * i + 1)
                    act_xt(act, 2 * i + 2, 0)
                    act_out(act, 2 * i, 0, i)
                    act_hidden(act, 2 * i + 2)
                    act_xt(act, 2 * i + 3, 1)
                    act_out(act, 2 * i + 1, 1, i)
                act_hidden(act, NTILE - 2)
                act_xt(act, NTILE - 1, 0)
                act_out(act, NTILE - 3, 0, (NTILE - 3) // 2)
                act_hidden(act, NTILE - 1)
                act_out(act, NTILE - 2, 1, (NTILE - 3) // 2)
                act_out(act, NTILE - 1, 0, (NTILE - 1) // 2)

            def dve_tile(dve, n, s):
                if gated:
                    dve.wait_ge(t("g"), n + 1)
                    dve.wait_ge(t("up"), n * up + 2)
                    wait(dve, t("hT_ps"), n)
                    nc.vector.tensor_tensor(hs.rearrange("p (h f) -> p h f", h=nh),
                                            gl.rearrange("p (h f) -> p h f", h=nh),
                                            psum[:, 1024:2048].rearrange("p (h f) -> p h f", h=2)[:, :, 0:half],
                                            ALU.mult).then_inc(t("h"), 1)
                dve.wait_ge(t("hT_ps"), n + 1)
                wait(dve, t("y_ps"), n - 1, 1)
                whole = F // P
                last = nc.vector.tensor_copy(hT[:, s, 0:whole, :].rearrange("p n q -> p (n q)"),
                                             psum[:, 2048:2048 + whole * P])
                if whole < nf:
                    last = nc.vector.tensor_copy(hT[0:fw[whole], s, whole, :],
                                                 psum[0:fw[whole], 2048 + whole * P:2048 + whole * P + P])
                last.then_inc(t("hT"), 1)

            def dve_prog(dve):
                dve_tile(dve, 0, 0)
                with dve.Fori(0, (NTILE - 1) // 2) as i:
                    dve_tile(dve, 2 * i + 1, 1)
                    dve_tile(dve, 2 * i + 2, 0)

            progs = {"sp": sp_prog, "pe": pe_prog, "act": act_prog, "dve": dve_prog}
            if bias:
                progs["pool"] = lambda pool: add_bias(pool, *bias)
            stages.append((name, progs))

        g = a.get
        W = {}
        v = weights(("mat", g("L0_attn_Wq")), ("mat", g("L0_attn_Wk")), ("mat", g("L0_attn_Wv")),
                    ("row", g("L0_attn_bv")), ("col", g("L0_attn_bq")), ("col", g("L0_attn_bk")))
        W["t0"] = dict(zip(("wq", "wk", "wv", "bv", "bq", "bk"), v))
        v = weights(("mat", g("L0_xattn_Wk")), ("mat", g("L0_xattn_Wv")), ("row", g("L0_xattn_bv")),
                    ("col", g("L0_xattn_bk")),
                    ("mat", g("L1_xattn_wk")), ("mat", g("L1_xattn_wv")), ("col", g("L1_xattn_bk")))
        w_ctx = [dict(zip(("wk", "wv", "bv", "bk"), v[0:4])), dict(zip(("wk", "wv", "bk"), v[4:7]))]
        bvx1 = floor_t.rearrange("p h q -> p (h q)")[:, 0:D]
        wdefs[-1].append((bvx1, g("L1_xattn_bv").partition_broadcast(P)))
        w_ctx[1]["bv"] = bvx1
        v = weights(("mat", g("L0_attn_Wf")), ("row", g("L0_attn_bf")), ("mat", g("L0_xattn_Wq")), ("col", g("L0_xattn_bq")))
        W["t1"] = dict(zip(("wo", "brow", "wq", "bq"), v))
        v = weights(("mat", g("L0_xattn_Wo")), ("row", g("L0_xattn_bo")), ("mat", g("L0_ffn_router_w")))
        W["t2"] = dict(zip(("wo", "brow", "router"), v))
        qkv = g("L1_attn_W_qkv")
        bqkv = g("L1_attn_b_qkv")
        v = weights(("mat", qkv[:, 0:D]), ("mat", qkv[:, D:2 * D]), ("mat", qkv[:, 2 * D:3 * D]),
                    ("row", bqkv[2 * D:3 * D]), ("col", bqkv[0:D]), ("col", bqkv[D:2 * D]), ("row", g("L0_ffn_bias")))
        W["t3"] = dict(zip(("wq", "wk", "wv", "bv", "bq", "bk", "brow"), v))
        v = weights(("mat", g("L1_attn_W_out")), ("row", g("L1_attn_b_out")), ("mat", g("L1_xattn_wq")), ("col", g("L1_xattn_bq")))
        W["t4"] = dict(zip(("wo", "brow", "wq", "bq"), v))
        v = weights(("mat", g("L1_xattn_wo")), ("row", g("L1_xattn_bo")), ("row", g("L1_ffn_g1")), ("mat", g("L1_ffn_Wq")),
                    ("mat", g("L1_ffn_Wdkv")), ("mat", g("L1_ffn_Wuk")), ("mat", g("L1_ffn_Wuv")))
        W["t5"] = dict(zip(("wo", "brow", "g1", "wq", "wdkv", "wuk", "wuv"), v))
        v = weights(("mat", g("L1_ffn_Wo")), ("row", g("L1_ffn_g2")), ("mat", g("L1_ffn_gate_w")))
        W["t6"] = dict(zip(("wo", "g2", "router"), v))

        logits = scratch[:, 0:NT * NX]
        wu0 = arena[:, att_base:att_base + NX * DC * 2 * F0].rearrange("p (e c w f) -> p e c w f", e=NX, c=DC, w=2)
        w2_0 = [w2_low[:, n * 2048:n * 2048 + 2048].rearrange("p (e d) -> p e d", e=NX) for n in range(4)] + \
               [w2_high[:, n * 2048:n * 2048 + 2048].rearrange("p (e d) -> p e d", e=NX) for n in range(2)]
        nw1 = NX * DC * F1
        wu1 = arena[:, att_base:att_base + nw1].rearrange("p (e c w f) -> p e c w f", e=NX, c=DC, w=1)
        w2_1 = [arena[:, att_base + nw1 + n * 2048:att_base + nw1 + n * 2048 + 2048]
                .rearrange("p (e d) -> p e d", e=NX) for n in range(4)]
        assert att_base + nw1 + 8192 <= v_base

        def up_weights0(sp, first, end):
            for e in range(first, end):
                for w, src in enumerate((g("L0_ffn_w1"), g("L0_ffn_v1"))):
                    sp.dma_start(wu0[:, e, :, w, :], src[e].rearrange("(c p) f -> p c f", p=P)).then_inc(sem("up0"), 16)
            if end == NX:
                down_weights0(sp, (4, 5))

        def down_weights0(sp, chunks):
            for n in chunks:
                r = min(P, F0 - n * P)
                sp.dma_start(w2_0[n][0:r, :, :], g("L0_ffn_w2")[:, n * P:n * P + r, :].rearrange("e p d -> p e d"))\
                    .then_inc(sem("down0"), 16)

        def weights1(sp):
            for e in range(NX):
                sp.dma_start(wu1[:, e, :, 0, :], g("L1_ffn_w1")[e].rearrange("(c p) f -> p c f", p=P))\
                    .then_inc(sem("up1"), 16)
            for n in range(4):
                sp.dma_start(w2_1[n], g("L1_ffn_w2")[:, n * P:n * P + P, :].rearrange("e p d -> p e d"))\
                    .then_inc(sem("down1"), 16)

        def weights0_wait(pe):
            pe.wait_ge(sem("up0"), 16 * 2 * NX)
            pe.wait_ge(sem("down0"), 16 * 6)

        def weights1_wait(pe):
            pe.wait_ge(sem("up1"), 16 * NX)
            pe.wait_ge(sem("down1"), 16 * 4)

        at0 = Attention("at0", ("fwd", "bwd"), S, True, False, q_scr, k_scr, None)
        xa0 = Attention("xa0", ("full", "full"), SC, False, True, q_scr, kx_scr[0], 0)
        at1 = Attention("at1", ("full", "full"), S, False, False, q_scr, k_scr, None)
        xa1 = Attention("xa1", ("full", "full"), SC, False, False, q_scr, kx_scr[1], 1)
        mla = Attention("mla", ("causal", "causal"), S, False, False, q_scr, k_scr, None)
        w = W["t0"]
        token_stage("t0", 0, "x", False, None,
                    [("qk", w["wq"], w["bq"], q_scr), ("qk", w["wk"], w["bk"], k_scr),
                     ("v", w["wv"], w["bv"])], w, late_sp=load_inputs)
        context_stage("ctx", 1, at0)
        attention_stage(at0, (2, W["t1"]["brow"]), zero_slots)
        w = W["t1"]
        token_stage("t1", 2, "proj", True, None, [("qk", w["wq"], w["bq"], q_scr)], w,
                    early_sp=lambda sp: load_context(sp, 0), following=xa0)
        attention_stage(xa0, (3, W["t2"]["brow"]))
        w = W["t2"]
        token_stage("t2", 3, "proj", True, None, [("logits", w["router"], logits)], w, 
                    early_sp=lambda sp: up_weights0(sp, 0, EARLY), late_sp=lambda sp: up_weights0(sp, EARLY, NX))
        routing_stage("rt0", x_tok, True, lambda sp: down_weights0(sp, (0, 1, 2, 3)))
        expert_stage("ex0", True, F0, wu0, w2_0, weights0_wait, (4, W["t3"]["brow"]))
        w = W["t3"]
        token_stage("t3", 4, "comb", True, None,
                    [("qk", w["wq"], w["bq"], q_scr), ("qk", w["wk"], w["bk"], k_scr),
                     ("v", w["wv"], w["bv"])], w, following=at1)
        attention_stage(at1, (5, W["t4"]["brow"]))
        w = W["t4"]
        token_stage("t4", 5, "proj", True, None, [("qk", w["wq"], w["bq"], q_scr)], w,
                    early_sp=lambda sp: load_context(sp, 1), following=xa1)
        attention_stage(xa1, (6, W["t5"]["brow"]))
        w = W["t5"]
        token_stage("t5", 6, "proj", True, w["g1"],
                    [("latent", w["wdkv"]), ("qk", w["wq"], None, q_scr), ("klat", w["wuk"], k_scr),
                     ("vlat", w["wuv"])], w, following=mla)
        attention_stage(mla)
        w = W["t6"]
        token_stage("t6", 7, "proj", False, w["g2"], [("logits", w["router"], logits)], w, x_out="add", rows_out=True,
                    late_sp=weights1)
        routing_stage("rt1", v_tok.rearrange("p (t d) -> p t d", t=NT), False)
        expert_stage("ex1", False, F1, wu1, w2_1, weights1_wait)
        token_stage("t7", None, "comb", True, None, [], {}, x_out=False, final=True)

        family = {"t": "tok_", "c": "ctx_", "a": "att_", "x": "att_", "m": "att_", "r": "route_", "e": "experts_"}

        def run(eng, key):
            for n, (name, progs) in enumerate(stages):
                if n:
                    eng.wait_ge(stage_done, 5 * n)
                    if key == "pool":
                        kind = family.get(stages[n - 1][0][0])
                        for other, handle in sems.items():
                            if kind and other.startswith(kind):
                                eng.sem_clear(handle)
                if key in progs:
                    progs[key](eng)
                if n + 1 < len(stages):
                    eng.drain().then_inc(stage_done, 1)

        block = stack.enter_context(nc.Block())

        @block.sync
        def _(sp):
            run(sp, "sp")

        @block.tensor
        def _(pe):
            run(pe, "pe")

        @block.scalar
        def _(act):
            run(act, "act")

        @block.vector
        def _(dve):
            run(dve, "dve")

        @block.gpsimd
        def _(pool):
            run(pool, "pool")


NAMES = ['L0_attn_Wq', 'L0_attn_bq', 'L0_attn_Wk', 'L0_attn_bk', 'L0_attn_Wv', 'L0_attn_bv', 'L0_attn_Wf', 'L0_attn_bf',
         'L0_xattn_Wq', 'L0_xattn_bq', 'L0_xattn_Wk', 'L0_xattn_bk', 'L0_xattn_Wv', 'L0_xattn_bv', 'L0_xattn_Wo',
         'L0_xattn_bo', 'L0_ffn_router_w', 'L0_ffn_w1', 'L0_ffn_v1', 'L0_ffn_w2', 'L0_ffn_bias', 'L1_attn_W_qkv',
         'L1_attn_b_qkv', 'L1_attn_W_out', 'L1_attn_b_out', 'L1_xattn_wq', 'L1_xattn_bq', 'L1_xattn_wk', 'L1_xattn_bk',
         'L1_xattn_wv', 'L1_xattn_bv', 'L1_xattn_wo', 'L1_xattn_bo', 'L1_ffn_g1', 'L1_ffn_Wq', 'L1_ffn_Wdkv',
         'L1_ffn_Wuk', 'L1_ffn_Wuv', 'L1_ffn_Wo', 'L1_ffn_g2', 'L1_ffn_gate_w', 'L1_ffn_w1', 'L1_ffn_w2']


QK_NAMES = ('L0_attn_Wq', 'L0_attn_bq', 'L0_attn_Wk', 'L0_attn_bk', 'L0_xattn_Wq', 'L0_xattn_bq', 'L0_xattn_Wk',
            'L0_xattn_bk', 'L1_xattn_wq', 'L1_xattn_bq', 'L1_xattn_wk', 'L1_xattn_bk', 'L1_ffn_Wq', 'L1_ffn_Wuk')


def heads_inside(w):
    return np.ascontiguousarray(w.reshape(w.shape[:-1] + (-1, HG, HD)).swapaxes(-1, -2).reshape(w.shape))


def alibi_rows():
    bf = mybir.dt.np(BF16)
    half = H // 2
    slopes = 1.0 / (24.0 ** (1.0 / half)) ** np.arange(1, half + 1)
    rows = np.ones((2, 2, 2 * NB, 6, HG, S), bf)
    for slot in range(2):
        for i in range(2 * NB):
            for h in range(HG):
                value = slopes[HG * (i // NB) + h] * np.arange(S) * (-1.0 if slot else 1.0)
                for side, sign, at in ((0, -1.0, 0), (1, 1.0, 3)):
                    rest = sign * value / QSCALE
                    for n in range(3):
                        rows[side, slot, i, at + n, h] = rest.astype(bf)
                        rest = rest - rows[side, slot, i, at + n, h].astype(np.float64)
    return rows


def kernel(**inputs):
    import concourse.bacc as bacc
    from concourse.bass_utils import run_bass_kernel_spmd

    nc = bacc.Bacc("TRN2", target_bir_lowering=False, num_devices=1)
    x = np.asarray(inputs["x"])
    ctx = np.asarray(inputs["ctx_768"])
    arrays = {"x": x, "xT": np.ascontiguousarray(x.reshape(T, D).T),
              "ctxT": np.ascontiguousarray(ctx.reshape(NB * SC, CW).T),
              "alibi": alibi_rows(), "ones": np.ones((6, HG, S), mybir.dt.np(BF16)),
              "ones_x": np.ones((3, 2 * NB, HG * SC), mybir.dt.np(BF16))}
    for name in NAMES:
        arrays[name] = np.ascontiguousarray(inputs[name])
        if name in QK_NAMES:
            arrays[name] = heads_inside(arrays[name])
        elif name in ("L1_attn_W_qkv", "L1_attn_b_qkv"):
            arrays[name] = np.concatenate([heads_inside(arrays[name][..., 0:2 * D]), arrays[name][..., 2 * D:]], -1)
    aps = {name: nc.dram_tensor(f"in_{name}", v.shape, mybir.dt.from_np(v.dtype), kind="ExternalInput").ap()
           for name, v in arrays.items()}
    out = nc.dram_tensor("out", (NB, S, D), F32, kind="ExternalOutput").ap()
    build_decoder(nc, aps, out)
    r = run_bass_kernel_spmd(nc, [{f"in_{name}": v for name, v in arrays.items()}], core_ids=[0])
    return r.results[0]["out"]
```
